# Optimizing a Trainium2 kernel written in Bass

```python
import numpy as np
import jax
import jax.numpy as jnp

def _softmax(x, axis=-1):
    return jax.nn.softmax(x, axis=axis)

def _gelu(x):
    return jax.nn.gelu(x, approximate=True)

def _silu(x):
    return jax.nn.silu(x)

def _sigmoid(x):
    return jax.nn.sigmoid(x)

def _layernorm(x, axis=-1, eps=1e-05):
    m = jnp.mean(x, axis=axis, keepdims=True)
    v = jnp.var(x, axis=axis, keepdims=True)
    return (x - m) / jnp.sqrt(v + eps)

def _scatter_add(tgt, idx, src, axis=0):
    return tgt.at[idx].add(src)

def _segment_sum(src, seg, n):
    return jax.ops.segment_sum(src, seg, n)
kernel_name = 'mk_recurrent_d1_jaxref_r4_25e84b'

def setup_inputs(seed: int=0):
    np.random.seed(seed)
    _w = jnp.asarray

    def _L0_attn_setup():
        import jax, jax.numpy as jnp
        import numpy as np
        from jax import lax
        H = 64
        P = 64
        N = 128
        G = 8
        K = 4
        D_MODEL = 1024
        I = H * P
        GN = G * N
        CONV_DIM = I + 2 * GN
        PROJ = I + CONV_DIM + H
        EPS = 1e-05
        GROUP_SIZE = I // G

        def _reference_tuple_inner(hidden_states, in_proj_w, conv_weight, conv_bias, dt_bias, A_log, D, norm_weight, out_proj_w):
            B, L, _ = hidden_states.shape
            proj = jnp.einsum('bld,pd->blp', hidden_states, in_proj_w)
            gate = proj[..., :I]
            hbc = proj[..., I:I + CONV_DIM]
            dt = proj[..., -H:]
            pad = jnp.pad(hbc, ((0, 0), (K - 1, 0), (0, 0)))
            conv = conv_bias
            for k in range(K):
                conv = conv + pad[:, k:k + L, :] * conv_weight[:, k]
            xBC = jax.nn.silu(conv)
            x = xBC[..., :I].reshape(B, L, H, P)
            Bm = xBC[..., I:I + GN].reshape(B, L, G, N)
            Cm = xBC[..., I + GN:].reshape(B, L, G, N)
            hpg = H // G
            B_h = jnp.repeat(Bm, hpg, axis=2)
            C_h = jnp.repeat(Cm, hpg, axis=2)
            dt_p = jax.nn.softplus(dt + dt_bias)
            A = -jnp.exp(A_log)
            dA = jnp.exp(dt_p * A)
            dtx = dt_p[..., None] * x

            def step(state, inp):
                dA_t, dtx_t, B_t, C_t = inp
                state = state * dA_t[..., None, None] + dtx_t[..., None] * B_t[:, :, None, :]
                y_t = jnp.einsum('bhpn,bhn->bhp', state, C_t)
                return (state, y_t)
            xs = (jnp.moveaxis(dA, 1, 0), jnp.moveaxis(dtx, 1, 0), jnp.moveaxis(B_h, 1, 0), jnp.moveaxis(C_h, 1, 0))
            state0 = jnp.zeros((B, H, P, N), jnp.float32)
            final_state, ys = lax.scan(step, state0, xs)
            y = jnp.moveaxis(ys, 0, 1) + x * D[None, None, :, None]
            y = y.reshape(B, L, I)
            yg = y.reshape(B, L, G, GROUP_SIZE)
            var = jnp.mean(yg * yg, axis=-1, keepdims=True)
            yn = (yg * lax.rsqrt(var + EPS)).reshape(B, L, I) * norm_weight
            yn = yn * jax.nn.silu(gate)
            out = jnp.einsum('bli,di->bld', yn, out_proj_w)
            conv_state_new = jnp.moveaxis(hbc[:, L - (K - 1):, :], 1, 2)
            return (out, conv_state_new, final_state)
        key = jax.random.key(seed)
        ks = jax.random.split(key, 6)
        B, L = (2, 512)
        s = 0.02
        return {'hidden_states': jax.random.normal(ks[0], (B, L, D_MODEL), jnp.float32), 'in_proj_w': jax.random.normal(ks[1], (PROJ, D_MODEL), jnp.float32) * s, 'conv_weight': jax.random.normal(ks[2], (CONV_DIM, K), jnp.float32) * s, 'conv_bias': jnp.zeros((CONV_DIM,), jnp.float32), 'dt_bias': jnp.ones((H,), jnp.float32), 'A_log': jnp.log(jnp.arange(1, H + 1, dtype=jnp.float32)), 'D': jnp.ones((H,), jnp.float32), 'norm_weight': jnp.ones((I,), jnp.float32), 'out_proj_w': jax.random.normal(ks[3], (D_MODEL, I), jnp.float32) * s}
    _L0_attn_in = _L0_attn_setup()

    def _L0_ffn_setup():
        import jax, jax.numpy as jnp
        import numpy as np
        N_STREAMS = 4
        DIM = 256
        SINKHORN_ITERS = 50
        SINKHORN_TAU = 0.1
        RMS_EPS = 1.1920929e-07

        def sinkhorn_log(logits, num_iters=SINKHORN_ITERS, tau=SINKHORN_TAU):
            Z = logits / tau
            u0 = jnp.zeros(Z.shape[:-1], Z.dtype)
            v0 = jnp.zeros_like(u0)

            def step(carry, _):
                u, v = carry
                u = -jax.nn.logsumexp(Z + v[..., None, :], axis=-1)
                v = -jax.nn.logsumexp(Z + u[..., :, None], axis=-2)
                return ((u, v), None)
            (u, v), _ = jax.lax.scan(step, (u0, v0), None, length=num_iters)
            return jnp.exp(Z + u[..., :, None] + v[..., None, :])
        key = jax.random.key(seed)
        ks = jax.random.split(key, 6)
        B, T = (4, 512)
        n, C = (N_STREAMS, DIM)
        wd = n * C
        x = jax.random.normal(ks[0], (B, T, wd), dtype=jnp.float32)
        W_res = 0.01 * jax.random.normal(ks[1], (n * n, wd), dtype=jnp.float32)
        W_pre = 0.01 * jax.random.normal(ks[2], (n, wd), dtype=jnp.float32)
        W_post = 0.01 * jax.random.normal(ks[3], (n, wd), dtype=jnp.float32)
        H_res_base = jnp.full((n, n), -0.5, dtype=jnp.float32)
        H_res_base = H_res_base.at[jnp.arange(n), jnp.arange(n)].set(0.0)
        H_pre_base = jnp.zeros((n,), dtype=jnp.float32).at[0].set(1.0)
        H_post_base = jnp.zeros((n,), dtype=jnp.float32)
        gate = jnp.array([5.0], dtype=jnp.float32)
        W_branch = 1.0 / np.sqrt(C) * jax.random.normal(ks[4], (C, C), dtype=jnp.float32)
        return {'x': x, 'W_res': W_res, 'W_pre': W_pre, 'W_post': W_post, 'H_res_base': H_res_base, 'H_pre_base': H_pre_base, 'H_post_base': H_post_base, 'gate': gate, 'W_branch': W_branch}
    _L0_ffn_in = _L0_ffn_setup()
    _d = {'L0_attn_hidden_states': _L0_attn_in['hidden_states'], 'L0_attn_in_proj_w': _L0_attn_in['in_proj_w'], 'L0_attn_conv_weight': _L0_attn_in['conv_weight'], 'L0_attn_conv_bias': _L0_attn_in['conv_bias'], 'L0_attn_dt_bias': _L0_attn_in['dt_bias'], 'L0_attn_A_log': _L0_attn_in['A_log'], 'L0_attn_D': _L0_attn_in['D'], 'L0_attn_norm_weight': _L0_attn_in['norm_weight'], 'L0_attn_out_proj_w': _L0_attn_in['out_proj_w'], 'L0_ffn_W_res': _L0_ffn_in['W_res'], 'L0_ffn_W_pre': _L0_ffn_in['W_pre'], 'L0_ffn_W_post': _L0_ffn_in['W_post'], 'L0_ffn_H_res_base': _L0_ffn_in['H_res_base'], 'L0_ffn_H_pre_base': _L0_ffn_in['H_pre_base'], 'L0_ffn_H_post_base': _L0_ffn_in['H_post_base'], 'L0_ffn_gate': _L0_ffn_in['gate'], 'L0_ffn_W_branch': _L0_ffn_in['W_branch']}
    _x0 = _d['L0_attn_hidden_states']
    _d['L0_attn_hidden_states'] = jax.random.normal(jax.random.fold_in(jax.random.key(seed), 1), (4, 512, 1024), dtype=_x0.dtype)
    del _x0
    return _d

def reference(L0_attn_hidden_states, L0_attn_in_proj_w, L0_attn_conv_weight, L0_attn_conv_bias, L0_attn_dt_bias, L0_attn_A_log, L0_attn_D, L0_attn_norm_weight, L0_attn_out_proj_w, L0_ffn_W_res, L0_ffn_W_pre, L0_ffn_W_post, L0_ffn_H_res_base, L0_ffn_H_pre_base, L0_ffn_H_post_base, L0_ffn_gate, L0_ffn_W_branch):

    def _L0_attn_ref(hidden_states, in_proj_w, conv_weight, conv_bias, dt_bias, A_log, D, norm_weight, out_proj_w):
        import jax, jax.numpy as jnp
        import numpy as np
        from jax import lax
        H = 64
        P = 64
        N = 128
        G = 8
        K = 4
        D_MODEL = 1024
        I = H * P
        GN = G * N
        CONV_DIM = I + 2 * GN
        PROJ = I + CONV_DIM + H
        EPS = 1e-05
        GROUP_SIZE = I // G

        def _reference_tuple_inner(hidden_states, in_proj_w, conv_weight, conv_bias, dt_bias, A_log, D, norm_weight, out_proj_w):
            B, L, _ = hidden_states.shape
            proj = jnp.einsum('bld,pd->blp', hidden_states, in_proj_w)
            gate = proj[..., :I]
            hbc = proj[..., I:I + CONV_DIM]
            dt = proj[..., -H:]
            pad = jnp.pad(hbc, ((0, 0), (K - 1, 0), (0, 0)))
            conv = conv_bias
            for k in range(K):
                conv = conv + pad[:, k:k + L, :] * conv_weight[:, k]
            xBC = jax.nn.silu(conv)
            x = xBC[..., :I].reshape(B, L, H, P)
            Bm = xBC[..., I:I + GN].reshape(B, L, G, N)
            Cm = xBC[..., I + GN:].reshape(B, L, G, N)
            hpg = H // G
            B_h = jnp.repeat(Bm, hpg, axis=2)
            C_h = jnp.repeat(Cm, hpg, axis=2)
            dt_p = jax.nn.softplus(dt + dt_bias)
            A = -jnp.exp(A_log)
            dA = jnp.exp(dt_p * A)
            dtx = dt_p[..., None] * x

            def step(state, inp):
                dA_t, dtx_t, B_t, C_t = inp
                state = state * dA_t[..., None, None] + dtx_t[..., None] * B_t[:, :, None, :]
                y_t = jnp.einsum('bhpn,bhn->bhp', state, C_t)
                return (state, y_t)
            xs = (jnp.moveaxis(dA, 1, 0), jnp.moveaxis(dtx, 1, 0), jnp.moveaxis(B_h, 1, 0), jnp.moveaxis(C_h, 1, 0))
            state0 = jnp.zeros((B, H, P, N), jnp.float32)
            final_state, ys = lax.scan(step, state0, xs)
            y = jnp.moveaxis(ys, 0, 1) + x * D[None, None, :, None]
            y = y.reshape(B, L, I)
            yg = y.reshape(B, L, G, GROUP_SIZE)
            var = jnp.mean(yg * yg, axis=-1, keepdims=True)
            yn = (yg * lax.rsqrt(var + EPS)).reshape(B, L, I) * norm_weight
            yn = yn * jax.nn.silu(gate)
            out = jnp.einsum('bli,di->bld', yn, out_proj_w)
            conv_state_new = jnp.moveaxis(hbc[:, L - (K - 1):, :], 1, 2)
            return (out, conv_state_new, final_state)
        return _reference_tuple_inner(hidden_states, in_proj_w, conv_weight, conv_bias, dt_bias, A_log, D, norm_weight, out_proj_w)[0]

    def _L0_ffn_ref(x, W_res, W_pre, W_post, H_res_base, H_pre_base, H_post_base, gate, W_branch):
        import jax, jax.numpy as jnp
        import numpy as np
        N_STREAMS = 4
        DIM = 256
        SINKHORN_ITERS = 50
        SINKHORN_TAU = 0.1
        RMS_EPS = 1.1920929e-07

        def sinkhorn_log(logits, num_iters=SINKHORN_ITERS, tau=SINKHORN_TAU):
            Z = logits / tau
            u0 = jnp.zeros(Z.shape[:-1], Z.dtype)
            v0 = jnp.zeros_like(u0)

            def step(carry, _):
                u, v = carry
                u = -jax.nn.logsumexp(Z + v[..., None, :], axis=-1)
                v = -jax.nn.logsumexp(Z + u[..., :, None], axis=-2)
                return ((u, v), None)
            (u, v), _ = jax.lax.scan(step, (u0, v0), None, length=num_iters)
            return jnp.exp(Z + u[..., :, None] + v[..., None, :])
        B, T, nC = x.shape
        n = N_STREAMS
        C = nC // n
        x_norm = x * jax.lax.rsqrt(jnp.mean(x * x, axis=-1, keepdims=True) + RMS_EPS)
        H_res_logits = (x_norm @ W_res.T).reshape(B, T, n, n) + H_res_base
        H_pre_logits = x_norm @ W_pre.T + H_pre_base
        H_post_logits = x_norm @ W_post.T + H_post_base
        H_res = sinkhorn_log(H_res_logits)
        H_pre = jax.nn.softmax(H_pre_logits, axis=-1)
        H_post = jax.nn.softmax(H_post_logits, axis=-1)
        g = jax.nn.sigmoid(gate)[0]
        I = jnp.eye(n, dtype=H_res.dtype)
        H_res = (1.0 - g) * I + g * H_res
        x_streams = x.reshape(B, T, n, C)
        x_pre = jnp.einsum('btnc,btn->btc', x_streams, H_pre)
        y = x_pre @ W_branch
        x_mixed = jnp.einsum('btij,btjc->btic', H_res, x_streams)
        y_distributed = jnp.einsum('btc,btn->btnc', y, H_post)
        return (x_mixed + y_distributed).reshape(B, T, nC)
    x = L0_attn_hidden_states
    xn = _layernorm(x, axis=-1)
    s = _L0_attn_ref(xn, L0_attn_in_proj_w, L0_attn_conv_weight, L0_attn_conv_bias, L0_attn_dt_bias, L0_attn_A_log, L0_attn_D, L0_attn_norm_weight, L0_attn_out_proj_w)
    g = _silu(_L0_ffn_ref(xn, L0_ffn_W_res, L0_ffn_W_pre, L0_ffn_W_post, L0_ffn_H_res_base, L0_ffn_H_pre_base, L0_ffn_H_post_base, L0_ffn_gate, L0_ffn_W_branch))
    x = x + s * g
    return x

_drawn_inputs = setup_inputs


def setup_inputs(seed=0):
    import zlib

    import numpy as np

    out = dict(_drawn_inputs(seed))
    spreads = {'L0_attn_conv_bias': (0.0, 0.1),
     'L0_attn_dt_bias': (1.0, 0.6),
     'L0_attn_D': (1.0, 0.2),
     'L0_attn_norm_weight': (1.0, 0.2),
     'L0_ffn_H_post_base': (0.0, 0.8)}
    factors = {'L0_attn_A_log': 8.0, 'L0_ffn_W_pre': 4.643, 'L0_ffn_W_post': 3.897}
    for name, (base, spread) in spreads.items():
        noise = np.random.default_rng([zlib.crc32(name.encode()), seed]).standard_normal(out[name].shape)
        drawn = base * np.exp(spread * noise) if base else spread * noise
        out[name] = jnp.asarray(drawn.astype(out[name].dtype))
    for name, factor in factors.items():
        out[name] = (out[name] * factor).astype(out[name].dtype)
    return out
```

```python
from contextlib import ExitStack

import concourse.bass as bass
from concourse import mybir

F32 = mybir.dt.float32
F32R = mybir.dt.float32r
ALU = mybir.AluOpType
ACT = mybir.ActivationFunctionType
AX = mybir.AxisListType

P = 128
TOKENS, DM = 2048, 1024
SEQ = 512
HALF = 1024
HALVES = TOKENS // HALF
SEQS = HALF // SEQ
NT = HALF // P
CHUNKS = SEQ // P
KT = DM // P
HEADS, HD, GROUPS = 64, 64, 8
HPG = HEADS // GROUPS
GC = HPG * HD
XT = GC // P
INNER = HEADS * HD
CONV_TILES = XT + 2
TILES = CONV_TILES + XT
SLOTS = TILES * SEQS
CONV_SLOTS = CONV_TILES * SEQS
GATE_SLOTS = XT * SEQS
OT = INNER // P
STREAMS, CW = 4, 256
SMALL = HEADS + STREAMS * STREAMS + 2 * STREAMS
LN_EPS, NORM_EPS, RMS_EPS = 1e-5, 1e-5, 1.1920929e-07
TAU = 0.1
SINKHORN = 50
LOG_ZERO = -110.0


def need(eng, sem, value):
    if isinstance(value, int) and value <= 0:
        return
    eng.wait_ge(sem, value)


def chunk_tile(k):
    return CHUNKS * (k % SEQS) + k // SEQS


class Core:

    def __init__(self, nc, ctx, dram):
        self.nc, self.dram = nc, dram
        self.phase_sems = []

        def sb(name, shape, dt=F32):
            return ctx.enter_context(nc.sbuf_tensor(name, shape, dt))

        self.bank = [ctx.enter_context(nc.psum_tensor(f"bank{i}", [P, 512], F32)) for i in range(8)]
        self.ident = sb("ident", [P, P])
        self.causal = sb("causal", [P, P])
        self.neg_half = sb("neg_half", [P, NT])
        self.mean = sb("mean", [P, 2 * NT])
        self.rstd = sb("rstd", [P, 2 * NT])
        self.res_logits = sb("res_logits", [P, 2 * NT, STREAMS * STREAMS])
        self.h_post = sb("h_post", [P, 2 * NT, STREAMS])
        self.gate_value = sb("gate_value", [P, 1])

    def semaphore(self, name):
        self.phase_sems.append(self.nc.alloc_semaphore(name=name))
        return self.phase_sems[-1]

    def end_phase(self):
        self.nc.all_engine_barrier()
        self.nc.clear_and_free_semaphores(self.phase_sems)
        self.phase_sems = []
        self.nc.all_engine_barrier()


def setup_block(nc, core, mix):
    d = core.dram
    with ExitStack() as ctx:
        loaded = core.semaphore("loaded")
        pool_step = core.semaphore("pool_step")
        halved = core.semaphore("halved")
        scaled = core.semaphore("scaled")
        block = ctx.enter_context(nc.Block())

        @block.sync
        def _(sp):
            sp.dma_start(mix.conv_w[:, :, :, :], d["conv_w"]).then_inc(loaded, 16)
            sp.dma_start(mix.norm_w[:, :, :], d["norm_w"]).then_inc(loaded, 16)
            sp.dma_start(mix.d_all[:, :], d["D"].partition_broadcast(P)).then_inc(loaded, 16)
            sp.dma_start(mix.dt_bias[:, :], d["dt_bias"]).then_inc(loaded, 16)
            sp.dma_start(mix.a_neg[:, :], d["A_log"]).then_inc(loaded, 16)
            sp.dma_start(core.gate_value[:, :], d["gate"].partition_broadcast(P)).then_inc(loaded, 16)

        @block.gpsimd
        def _(pool):
            pool.memset(core.ident[:, :], 0.0).then_inc(pool_step, 1)
            pool.memset(core.causal[:, :], 1.0).then_inc(pool_step, 1)
            pool.memset(core.neg_half[:, :], -0.5).then_inc(pool_step, 1)
            pool.wait_ge(pool_step, 3)
            pool.affine_select(out=core.ident[:, :], in_=core.ident[:, :], compare_op=ALU.not_equal,
                               fill=1.0, base=0, pattern=[[-1, P]], channel_multiplier=1).then_inc(pool_step, 1)
            pool.affine_select(out=core.causal[:, :], in_=core.causal[:, :], compare_op=ALU.is_ge,
                               fill=0.0, base=0, pattern=[[1, P]], channel_multiplier=-1).then_inc(pool_step, 1)
            pool.wait_ge(pool_step, 5)

        @block.scalar
        def _(act):
            act.wait_ge(loaded, 96)
            act.activation(mix.a_neg[:, :], mix.a_neg[:, :], ACT.Exp).then_inc(halved, 1)

        @block.vector
        def _(dve):
            dve.wait_ge(loaded, 96)
            dve.tensor_scalar(mix.conv_w[:, :, :, :], mix.conv_w[:, :, :, :], 0.5, None, ALU.mult)
            dve.tensor_scalar(mix.norm_w[:, :, :], mix.norm_w[:, :, :], 0.5, None, ALU.mult).then_inc(scaled, 1)
            dve.wait_ge(halved, 1)
            dve.tensor_scalar(mix.a_neg[:, :], mix.a_neg[:, :], -1.0, None, ALU.mult).then_inc(scaled, 1)
            dve.wait_ge(scaled, 2)


class Mixer:

    def __init__(self, nc, ctx):
        def sb(name, shape, dt=F32):
            return ctx.enter_context(nc.sbuf_tensor(name, shape, dt))

        self.conv_w = sb("conv_w", [P, GROUPS, CONV_TILES, 5])
        self.norm_w = sb("norm_w", [P, GROUPS, XT])
        self.d_all = sb("d_all", [P, HEADS])
        self.dt_bias = sb("dt_bias", [HEADS, 1])
        self.a_neg = sb("a_neg", [HEADS, 1])
        self.x_hi = sb("x_hi", [P, KT, HALF], F32R)
        self.x_lo = sb("x_lo", [P, KT, HALF], F32R)
        self.dt = sb("dt", [P, NT, HEADS])
        self.cum = sb("cum", [P, NT, HEADS])
        self.exp_cum = sb("exp_cum", [P, NT, HEADS])
        self.decay = sb("decay", [P, NT, HEADS])
        self.exp_last = sb("exp_last", [P, NT, HEADS])


def prepare_block(nc, core, mix, half):
    d = core.dram
    bank = core.bank
    with ExitStack() as ctx:
        def sb(name, shape, dt=F32):
            return ctx.enter_context(nc.sbuf_tensor(f"{name}_{half}", shape, dt))

        def sem(name):
            return core.semaphore(f"{name}_{half}")

        base = sb("base", [P, SMALL - HEADS])
        w_branch = sb("w_branch", [P, 2, CW])
        ones = sb("ones", [HEADS, P])
        small_raw = sb("small_raw", [P, KT, SMALL])
        small_hi = sb("small_hi", [P, KT, SMALL], F32R)
        small_lo = sb("small_lo", [P, KT, SMALL], F32R)
        xt = sb("xt", [P, NT, DM])
        junk = sb("junk", [P, DM])
        stats = sb("stats", [P, 2, 2, 6])
        mv = sb("mv", [P, NT, 2])
        var_eps = sb("var_eps", [P, NT])
        xsq = sb("xsq", [P, NT])
        ms_eps = sb("ms_eps", [P, NT])
        rms = sb("rms", [P, NT])
        small = sb("small", [SMALL, HALF])
        pos = sb("pos", [HEADS, HALF])
        soft = sb("soft", [HEADS, HALF])
        dt_fm = sb("dt_fm", [HEADS, HALF])
        log_decay = sb("log_decay", [HEADS, HALF])
        cum_fm = sb("cum_fm", [HEADS, HALF])
        last_fm = sb("last_fm", [HEADS, NT])
        last = sb("last", [P, HEADS, NT])
        logits = sb("logits", [P, NT, SMALL - HEADS])
        sm_max = sb("sm_max", [P, NT, 2])
        sm_sum = sb("sm_sum", [P, NT, 2])
        sm = sb("sm", [P, NT, 2, STREAMS])
        mixed = sb("mixed", [P, 2, CW])
        mixed_t = sb("mixed_t", [P, 2, CW])
        branch = sb("branch", [P, NT, CW])

        params_loaded, small_step = sem("params_loaded"), sem("small_step")
        x_loaded = [sem(f"x_loaded{t}") for t in range(NT)]
        bn_step, aggr_done = sem("bn_step"), sem("aggr_done")
        eps_done, rstd_done = sem("eps_done"), sem("rstd_done")
        xn_done, sq_done = sem("xn_done"), sem("sq_done")
        turned, hi_done, lo_done = sem("turned"), sem("hi_done"), sem("lo_done")
        small_done, small_copied = sem("small_done"), sem("small_copied")
        soft_step, dt_step, scanned = sem("soft_step"), sem("dt_step"), sem("scanned")
        to_tokens, tokens_copied, tables = sem("to_tokens"), sem("tokens_copied"), sem("tables")
        cum_stored, last_stored, last_loaded = sem("cum_stored"), sem("last_stored"), sem("last_loaded")
        rms_done, lg_step, lg_exp = sem("rms_done"), sem("lg_step"), sem("lg_exp")
        mix_step, mix_turned, mix_copied = sem("mix_step"), sem("mix_turned"), sem("mix_copied")
        branch_done, branch_copied, branch_stored = sem("branch_done"), sem("branch_copied"), sem("branch_stored")
        block = ctx.enter_context(nc.Block())

        @block.sync
        def _(sp):
            for t in range(NT):
                sp.dma_start(xt[:, t, :], d["x"][half * NT + t]).then_inc(x_loaded[t], 16)
                if t == 1:
                    sp.dma_start(small_raw[:, :, :], d["w_small"]).then_inc(params_loaded, 16)
                    sp.dma_start(base[:, :], d["base"].partition_broadcast(P)).then_inc(params_loaded, 16)
                    sp.dma_start(w_branch[:, :, :], d["w_branch"]).then_inc(params_loaded, 16)
            sp.wait_ge(scanned, NT + 1)
            sp.dma_start(d["last"][half], last_fm[:, :]).then_inc(last_stored, 16)
            sp.dma_start(d["cum"][half].rearrange("t h i -> h t i"),
                         cum_fm[:, :].rearrange("h (t i) -> h t i", i=P)).then_inc(cum_stored, 16)
            sp.wait_ge(last_stored, 16)
            sp.dma_start(last[:, :, :], d["last"][half].partition_broadcast(P)).then_inc(last_loaded, 16)
            sp.wait_ge(branch_copied, NT)
            sp.dma_start(d["branch"][half], branch[:, :, :]).then_inc(branch_stored, 16)
            sp.wait_ge(cum_stored, 16)
            sp.wait_ge(branch_stored, 16)

        @block.gpsimd
        def _(pool):
            for t in range(NT):
                pool.wait_ge(aggr_done, t + 1)
                pool.tensor_scalar(var_eps[:, t:t + 1], mv[:, t, 1:2], LN_EPS, None, ALU.add).then_inc(eps_done, 1)
                pool.wait_ge(eps_done, t + 1)
                pool.tensor_tensor(core.rstd[:, half * NT + t:half * NT + t + 1], var_eps[:, t:t + 1],
                                   core.neg_half[:, 0:1], ALU.pow).then_inc(rstd_done, 1)
            pool.wait_ge(sq_done, NT)
            pool.tensor_scalar(ms_eps[:, :], xsq[:, :], 1.0 / DM, RMS_EPS, ALU.mult, ALU.add).then_inc(eps_done, 1)
            pool.wait_ge(eps_done, NT + 1)
            pool.tensor_tensor(rms[:, :], ms_eps[:, :], core.neg_half[:, :], ALU.pow).then_inc(rms_done, 1)

        @block.vector
        def _(dve):
            def split_low(n):
                t, h = divmod(n, 2)
                dve.wait_ge(hi_done, n + 1)
                dve.tensor_tensor(mix.x_lo[:, 4 * h:4 * h + 4, t * P:(t + 1) * P],
                                  bank[n % 4][:, :].rearrange("p (k c) -> p k c", c=P),
                                  mix.x_hi[:, 4 * h:4 * h + 4, t * P:(t + 1) * P].bitcast(F32),
                                  ALU.subtract).then_inc(lo_done, 1)

            for t in range(NT):
                dve.wait_ge(x_loaded[t], 16)
                for h in range(2):
                    dve.bn_stats(stats[:, t % 2, h, :], xt[:, t, h * 512:(h + 1) * 512]).then_inc(bn_step, 1)
                dve.wait_ge(bn_step, 2 * t + 2)
                dve.bn_aggr(mv[:, t, :], stats[:, t % 2, :, :]).then_inc(aggr_done, 1)
                if t:
                    split_low(2 * t - 2)
                    split_low(2 * t - 1)
                dve.wait_ge(rstd_done, t + 1)
                dve.wait_ge(aggr_done, t + 1)
                dve.tensor_scalar(xt[:, t, :], xt[:, t, :], mv[:, t, 0:1],
                                  core.rstd[:, half * NT + t:half * NT + t + 1],
                                  ALU.subtract, ALU.mult).then_inc(xn_done, 1)
            split_low(2 * NT - 2)
            split_low(2 * NT - 1)
            dve.memset(ones[:, :], 1.0).then_inc(dt_step, 1)
            dve.wait_ge(small_step, 1)
            dve.tensor_tensor(small_lo[:, :, :], small_raw[:, :, :], small_hi[:, :, :].bitcast(F32),
                              ALU.subtract).then_inc(small_step, 1)
            dve.tensor_copy(core.mean[:, half * NT:(half + 1) * NT], mv[:, :, 0])

            dve.wait_ge(small_copied, 2)
            dve.tensor_scalar(pos[:, :], small[0:HEADS, :], mix.dt_bias[:, 0:1], 0.0,
                              ALU.add, ALU.max).then_inc(dt_step, 1)
            dve.wait_ge(dt_step, 2)
            dve.wait_ge(soft_step, 3)
            dve.tensor_tensor(dt_fm[:, :], pos[:, :], soft[:, :], ALU.add).then_inc(dt_step, 1)
            dve.wait_ge(dt_step, 3)
            dve.tensor_scalar(log_decay[:, :], dt_fm[:, :], mix.a_neg[:, 0:1], LOG_ZERO,
                              ALU.mult, ALU.max).then_inc(dt_step, 1)
            dve.wait_ge(dt_step, 4)
            for t in range(NT):
                dve.tensor_tensor_scan(cum_fm[:, t * P:(t + 1) * P], ones[:, :],
                                       log_decay[:, t * P:(t + 1) * P], 0.0, ALU.mult, ALU.add).then_inc(scanned, 1)
            dve.wait_ge(scanned, NT)
            dve.tensor_copy(last_fm[:, :], cum_fm[:, P - 1::P]).then_inc(scanned, 1)

            for h in range(2):
                dve.wait_ge(to_tokens, h + 1)
                dve.tensor_copy(logits[:, 4 * h:4 * h + 4, :],
                                bank[2 + h][:, 0:4 * SMALL].rearrange("p (t c) -> p t c", c=SMALL)[:, :, HEADS:]
                                ).then_inc(lg_step, 1)
            dve.wait_ge(lg_step, 2)
            dve.wait_ge(rms_done, 1)
            dve.tensor_tensor(logits[:, :, :], logits[:, :, :],
                              rms[:, :].unsqueeze(2).to_broadcast([P, NT, SMALL - HEADS]), ALU.mult).then_inc(lg_step, 1)
            dve.wait_ge(lg_step, 3)
            dve.tensor_tensor(logits[:, :, :], logits[:, :, :],
                              base[:, :].unsqueeze(1).to_broadcast([P, NT, SMALL - HEADS]), ALU.add).then_inc(lg_step, 1)
            dve.wait_ge(lg_step, 4)
            nres = STREAMS * STREAMS
            dve.tensor_copy(core.res_logits[:, half * NT:(half + 1) * NT, :], logits[:, :, 0:nres])
            two = logits[:, :, nres:].rearrange("p t (w s) -> p t w s", s=STREAMS)
            dve.tensor_reduce(sm_max[:, :, :], two, AX.X, ALU.max).then_inc(lg_step, 1)
            dve.wait_ge(lg_step, 5)
            dve.tensor_tensor(sm[:, :, :, :], two, sm_max[:, :, :].unsqueeze(3).to_broadcast([P, NT, 2, STREAMS]),
                              ALU.subtract).then_inc(lg_step, 1)
            dve.wait_ge(lg_exp, 1)
            dve.tensor_reduce(sm_sum[:, :, :], sm[:, :, :, :], AX.X, ALU.add).then_inc(lg_step, 1)
            dve.wait_ge(lg_step, 7)
            dve.reciprocal(sm_sum[:, :, :], sm_sum[:, :, :]).then_inc(lg_step, 1)
            dve.wait_ge(lg_step, 8)
            dve.tensor_tensor(sm[:, :, :, :], sm[:, :, :, :],
                              sm_sum[:, :, :].unsqueeze(3).to_broadcast([P, NT, 2, STREAMS]), ALU.mult).then_inc(lg_step, 1)
            dve.wait_ge(lg_step, 9)
            dve.tensor_copy(core.h_post[:, half * NT:(half + 1) * NT, :], sm[:, :, 1, :])

            for t in range(NT):
                if t >= 2:
                    dve.wait_ge(mix_turned, t - 1)
                dve.tensor_scalar(mixed[:, t % 2, :], xt[:, t, 0:CW], sm[:, t, 0, 0:1], None, ALU.mult).then_inc(mix_step, 1)
                for s in range(1, STREAMS):
                    dve.wait_ge(mix_step, STREAMS * t + s)
                    dve.scalar_tensor_tensor(mixed[:, t % 2, :], xt[:, t, s * CW:(s + 1) * CW], sm[:, t, 0, s:s + 1],
                                             mixed[:, t % 2, :], ALU.mult, ALU.add).then_inc(mix_step, 1)

            dve.wait_ge(last_loaded, 16)
            dve.wait_ge(tokens_copied, 3)
            dve.tensor_tensor(mix.decay[:, :, :], last[:, :, :].rearrange("p h t -> p t h"), mix.cum[:, :, :],
                              ALU.subtract).then_inc(tables, 1)

        @block.scalar
        def _(act):
            def high(n):
                t, h = divmod(n, 2)
                act.wait_ge(turned, n + 1)
                act.activation(mix.x_hi[:, 4 * h:4 * h + 4, t * P:(t + 1) * P],
                               bank[n % 4][:, :].rearrange("p (k c) -> p k c", c=P), ACT.Copy).then_inc(hi_done, 1)

            for t in range(NT):
                act.wait_ge(xn_done, t + 1)
                act.activation(junk[:, :], xt[:, t, :], ACT.Square, accum_out=xsq[:, t:t + 1]).then_inc(sq_done, 1)
                high(2 * t)
                high(2 * t + 1)
            act.wait_ge(params_loaded, 48)
            act.activation(small_hi[:, :, :], small_raw[:, :, :], ACT.Copy).then_inc(small_step, 1)
            for s in range(SEQS):
                act.wait_ge(small_done, s + 1)
                act.activation(small[:, s * SEQ:(s + 1) * SEQ], bank[4 + s][0:SMALL, :], ACT.Copy).then_inc(small_copied, 1)
            act.wait_ge(small_copied, 2)
            act.activation(soft[:, :], small[0:HEADS, :], ACT.Abs, bias=mix.dt_bias[:, 0:1]).then_inc(soft_step, 1)
            act.wait_ge(soft_step, 1)
            act.activation(soft[:, :], soft[:, :], ACT.Exp, scale=-1.0).then_inc(soft_step, 1)
            act.wait_ge(soft_step, 2)
            act.activation(soft[:, :], soft[:, :], ACT.Ln, bias=1.0).then_inc(soft_step, 1)
            act.wait_ge(to_tokens, 4)
            act.activation(mix.dt[:, :, :], bank[0][:, :].rearrange("p (t h) -> p t h", h=HEADS), ACT.Copy).then_inc(tokens_copied, 1)
            act.activation(mix.cum[:, :, :], bank[1][:, :].rearrange("p (t h) -> p t h", h=HEADS), ACT.Copy).then_inc(tokens_copied, 1)
            act.activation(mix.exp_cum[:, :, :], bank[1][:, :].rearrange("p (t h) -> p t h", h=HEADS), ACT.Exp).then_inc(tokens_copied, 1)
            act.wait_ge(lg_step, 6)
            act.activation(sm[:, :, :, :], sm[:, :, :, :], ACT.Exp).then_inc(lg_exp, 1)
            act.wait_ge(last_loaded, 16)
            act.activation(mix.exp_last[:, :, :], last[:, :, :].rearrange("p h t -> p t h"), ACT.Exp)
            for t in range(NT + 1):
                if t < NT:
                    act.wait_ge(mix_turned, t + 1)
                    if t >= 2:
                        act.wait_ge(branch_done, t - 1)
                    act.activation(mixed_t[:, t % 2, :], bank[4 + t % 2][:, 0:CW], ACT.Copy).then_inc(mix_copied, 1)
                if t:
                    act.wait_ge(branch_done, t)
                    act.activation(branch[:, t - 1, :], bank[6 + (t - 1) % 2][:, 0:CW], ACT.Copy).then_inc(branch_copied, 1)
            act.wait_ge(tables, 1)
            act.activation(mix.decay[:, :, :], mix.decay[:, :, :], ACT.Exp).then_inc(tables, 1)

        @block.tensor
        def _(pe):
            for n in range(2 * NT):
                t, h = divmod(n, 2)
                pe.wait_ge(xn_done, t + 1)
                need(pe, lo_done, n - 3)
                for k in range(4):
                    mm = pe.transpose(bank[n % 4][:, k * P:(k + 1) * P],
                                      xt[:, t, (4 * h + k) * P:(4 * h + k + 1) * P], core.ident[:, :])
                mm.then_inc(turned, 1)
            pe.wait_ge(lo_done, 2 * NT)
            pe.wait_ge(small_step, 2)
            for s in range(SEQS):
                toks = slice(s * SEQ, (s + 1) * SEQ)
                for k in range(KT):
                    pe.matmul(bank[4 + s][0:SMALL, :], small_hi[:, k, :], mix.x_hi[:, k, toks],
                              start=(k == 0), stop=False)
                    pe.matmul(bank[4 + s][0:SMALL, :], small_hi[:, k, :], mix.x_lo[:, k, toks],
                              start=False, stop=False)
                    mm = pe.matmul(bank[4 + s][0:SMALL, :], small_lo[:, k, :], mix.x_hi[:, k, toks],
                                   start=False, stop=(k == KT - 1))
                mm.then_inc(small_done, 1)
            pe.wait_ge(small_copied, 2)
            for h in range(2):
                for t in range(4 * h, 4 * h + 4):
                    mm = pe.transpose(bank[2 + h][:, (t % 4) * SMALL:(t % 4 + 1) * SMALL],
                                      small[:, t * P:(t + 1) * P], core.ident[0:SMALL, 0:SMALL])
                mm.then_inc(to_tokens, 1)
            pe.wait_ge(dt_step, 3)
            for t in range(NT):
                mm = pe.transpose(bank[0][:, t * HEADS:(t + 1) * HEADS], dt_fm[:, t * P:(t + 1) * P],
                                  core.ident[0:HEADS, 0:HEADS])
            mm.then_inc(to_tokens, 1)
            pe.wait_ge(scanned, NT)
            for t in range(NT):
                mm = pe.transpose(bank[1][:, t * HEADS:(t + 1) * HEADS], cum_fm[:, t * P:(t + 1) * P],
                                  core.ident[0:HEADS, 0:HEADS])
            mm.then_inc(to_tokens, 1)
            def turn_mixed(t):
                pe.wait_ge(mix_step, STREAMS * (t + 1))
                need(pe, mix_copied, t - 1)
                for c in range(2):
                    mm = pe.transpose(bank[4 + t % 2][:, c * P:(c + 1) * P], mixed[:, t % 2, c * P:(c + 1) * P],
                                      core.ident[:, :])
                mm.then_inc(mix_turned, 1)

            turn_mixed(0)
            for t in range(NT):
                if t + 1 < NT:
                    turn_mixed(t + 1)
                pe.wait_ge(mix_copied, t + 1)
                need(pe, branch_copied, t - 1)
                for c in range(2):
                    mm = pe.matmul(bank[6 + t % 2][:, 0:CW], mixed_t[:, t % 2, c * P:(c + 1) * P],
                                   w_branch[:, c, :], start=(c == 0), stop=(c == 1))
                mm.then_inc(branch_done, 1)


START = CONV_SLOTS
MULT = CONV_SLOTS + 1
TURN = SLOTS


def mixer_block(nc, core, mix, half):
    d = core.dram
    bank_proj = core.bank[0:2]
    bank_x, bank_bg, bank_y, bank_inter, bank_state, bank_turn = core.bank[2:8]
    with ExitStack() as ctx:
        def sb(name, shape, dt=F32):
            return ctx.enter_context(nc.sbuf_tensor(f"{name}_{half}", shape, dt))

        def sem(name):
            return core.semaphore(f"{name}_{half}")

        w_raw = sb("w_raw", [P, 2, KT, P])
        w_hi = [sb(f"w_hi{i}", [P, KT, P], F32R) for i in range(2)]
        w_lo = [sb(f"w_lo{i}", [P, KT, P], F32R) for i in range(2)]
        acc = sb("acc", [P, 2, SEQ])
        th = sb("th", [P, 2, SEQ])
        tap_par = sb("tap_par", [P, CONV_TILES, 2])
        xbc = sb("xbc", [P, CONV_TILES, HALF])
        gate = sb("gate", [P, XT, HALF])
        cum_b = sb("cum_b", [P, 2, HPG, P])
        attn = sb("attn", [P, 2, HPG, P])
        bc = sb("bc", [P, P])
        b_tok = sb("b_tok", [P, 2, P])
        dtx = sb("dtx", [P, 2, GC])
        dtx_dec = sb("dtx_dec", [P, 2, GC])
        dx = sb("dx", [P, GC])
        state = sb("state", [P, SEQS, GC])
        inter = sb("inter", [P, GC])
        y = sb("y", [P, 2, GC])
        ssq = sb("ssq", [P, 2])
        var_eps = sb("nvar", [P, 2])
        eps = sb("eps", [P, 1])
        rstd = sb("nrstd", [P, 2])
        yn = sb("yn", [P, NT, GC])
        yg = sb("yg", [P, 2, XT, P])

        w_loaded = [sem("w_loaded0"), sem("w_loaded1")]
        w_hi_done, w_split = sem("w_hi_done"), sem("w_split")
        proj_done, conv_taken, gate_taken = sem("proj_done"), sem("conv_taken"), sem("gate_taken")
        tap_done, conv_step, tanh_done, silu_done = sem("tap_done"), sem("conv_step"), sem("tanh_done"), sem("silu_done")
        gate_done = sem("gate_done")
        cum_loaded = [sem("cum_loaded0"), sem("cum_loaded1")]
        diff_done, exp_done, bc_done, dtx_done = sem("diff_done"), sem("exp_done"), sem("bc_done"), sem("dtx_done")
        dx_done, b_copied, dec_done, attn_done = sem("dx_done"), sem("b_copied"), sem("dec_done"), sem("attn_done")
        started, multiplied, y_turned = sem("started"), sem("multiplied"), sem("y_turned")
        inter_step, y_done, state_step, state_done = sem("inter_step"), sem("y_done"), sem("state_step"), sem("state_done")
        squared, nvar_done, rstd_done, yn_done = sem("squared"), sem("nvar_done"), sem("nrstd_done"), sem("yn_done")
        gated = sem("gated")
        stored = [sem("stored0"), sem("stored1")]
        constants, tap_ready = sem("constants"), sem("tap_ready")
        block = ctx.enter_context(nc.Block())

        MOVES = NT - SEQS

        def heads(ap):
            return ap.rearrange("p (h c) -> p h c", c=HD)

        def per_head(table, k, g):
            return table[:, chunk_tile(k), bass.ds(g * HPG, HPG)].unsqueeze(2).to_broadcast([P, HPG, HD])

        def groups(eng, step):
            step(0, True, False)
            step(1, False, False)
            with eng.Fori(2, GROUPS - 1) as g:
                step(g, False, False)
            step(GROUPS - 1, False, True)

        def tail_of(g, s, first):
            if first:
                return None, None, None
            return g - 1, (NT - 1 if s == MULT + NT - 1 - SLOTS else None), (s if s < NT else None)

        @block.sync
        def _(sp):
            def load_w(g, m):
                n = TILES * g + m
                need(sp, w_split, n - 1)
                sp.dma_start(w_raw[:, m % 2, :, :], d["w_in"][g, m]).then_inc(w_loaded[m % 2], 16)

            def store(g, k):
                sp.wait_ge(gated, NT * g + k + 1)
                t = chunk_tile(k)
                sp.dma_start(d["y"][half, bass.ds(g * XT, XT), :, t * P:(t + 1) * P].rearrange("k p i -> p k i"),
                             yg[:, k % 2, :, :]).then_inc(stored[k % 2], 16)

            def step(g, first, last):
                for s in range(SLOTS):
                    if not first and s < NT:
                        store(g - 1, s)
                    if s % 2 == 0:
                        ahead = s // 2 + 3
                        if ahead < TILES:
                            load_w(g, ahead)
                        elif not last:
                            load_w(g + 1, ahead - TILES)

            for m in range(3):
                load_w(0, m)
            groups(sp, step)
            for k in range(NT):
                store(GROUPS - 1, k)
            for i in range(2):
                sp.wait_ge(stored[i], 16 * GROUPS * NT // 2)

        @block.gpsimd
        def _(pool):
            def decayed(g, k):
                pool.wait_ge(dtx_done, NT * g + k + 1)
                need(pool, multiplied, NT * g + k - 1)
                pool.tensor_tensor(heads(dtx_dec[:, k % 2, :]), heads(dtx[:, k % 2, :]),
                                   per_head(mix.decay, k, g), ALU.mult).then_inc(dec_done, 1)

            def norm(g, k):
                pool.wait_ge(squared, NT * g + k + 1)
                pool.tensor_tensor(var_eps[:, k % 2:k % 2 + 1], ssq[:, k % 2:k % 2 + 1], eps[:, :],
                                   ALU.add).then_inc(nvar_done, 1)
                pool.wait_ge(nvar_done, NT * g + k + 1)
                need(pool, yn_done, NT * g + k - 1)
                pool.tensor_tensor(rstd[:, k % 2:k % 2 + 1], var_eps[:, k % 2:k % 2 + 1], core.neg_half[:, 0:1],
                                   ALU.pow).then_inc(rstd_done, 1)

            def step(g, first, last):
                for s in range(SLOTS):
                    before, mult, _ = tail_of(g, s, first)
                    if mult is not None:
                        norm(before, mult)
                    if START <= s:
                        k = s - START
                        if k:
                            norm(g, k - 1)
                        if k < MOVES:
                            decayed(g, k)

            pool.memset(eps[:, :], NORM_EPS).then_inc(constants, 1)
            pool.wait_ge(constants, 1)
            groups(pool, step)
            norm(GROUPS - 1, NT - 1)

        @block.scalar
        def _(act):
            def split_hi(g, m):
                n = TILES * g + m
                act.wait_ge(w_loaded[m % 2], 16 * ((TILES // 2) * g + m // 2 + 1))
                need(act, proj_done, SLOTS * g + 2 * (m - 1))
                act.activation(w_hi[m % 2][:, :, :], w_raw[:, m % 2, :, :], ACT.Copy).then_inc(w_hi_done, 1)

            def tap(g, s):
                act.wait_ge(proj_done, SLOTS * g + s + 1)
                need(act, silu_done, CONV_SLOTS * g + s - 1)
                act.wait_ge(tap_ready, g + 1)
                m = s // 2
                act.activation(acc[:, s % 2, :], bank_proj[s % 2][:, :], ACT.Identity,
                               bias=tap_par[:, m, 1:2], scale=tap_par[:, m, 0:1]).then_inc(tap_done, 1)

            def tap_params(g):
                act.activation(tap_par[:, :, :], mix.conv_w[:, g, :, 3:5], ACT.Copy).then_inc(tap_ready, 1)

            def tanh(g, s):
                act.wait_ge(conv_taken, CONV_SLOTS * g + s + 1)
                act.activation(th[:, s % 2, :], acc[:, s % 2, :], ACT.Tanh).then_inc(tanh_done, 1)

            def gate_in(g, s):
                v = s - CONV_SLOTS
                t, q = divmod(v, SEQS)
                act.wait_ge(proj_done, SLOTS * g + s + 1)
                if v < 2:
                    act.wait_ge(silu_done, CONV_SLOTS * g + s - 1)
                else:
                    act.wait_ge(gate_done, GATE_SLOTS * g + v - 1)
                if v == 0:
                    need(act, gated, NT * g)
                act.activation(th[:, s % 2, :], bank_proj[s % 2][:, :], ACT.Tanh, scale=0.5).then_inc(tanh_done, 1)
                act.activation(gate[:, t, q * SEQ:(q + 1) * SEQ], bank_proj[s % 2][:, :], ACT.Identity,
                               scale=mix.norm_w[:, g, t:t + 1]).then_inc(gate_taken, 1)

            def load_cum(g, k):
                need(act, diff_done, NT * g + k - 1)
                act.dma_start(cum_b[:, k % 2, :, :],
                              d["cum"][half, chunk_tile(k), bass.ds(g * HPG, HPG), :].partition_broadcast(P)
                              ).then_inc(cum_loaded[k % 2], 16)

            def exps(g, k):
                act.wait_ge(diff_done, NT * g + k + 1)
                act.activation(attn[:, k % 2, :, :], attn[:, k % 2, :, :], ACT.Exp).then_inc(exp_done, 1)

            def b_tokens(g, k):
                act.wait_ge(bc_done, NT * g + k + 1)
                need(act, multiplied, NT * g + k - 1)
                act.activation(b_tok[:, k % 2, :], bank_bg[:, 0:P], ACT.Copy).then_inc(b_copied, 1)

            def square(g, k):
                act.wait_ge(y_done, NT * g + k + 1)
                need(act, y_turned, NT * (g - 1) + k + 1)
                act.activation(yn[:, k, :], y[:, k % 2, :], ACT.Square, scale=GC ** -0.5,
                               accum_out=ssq[:, k % 2:k % 2 + 1]).then_inc(squared, 1)

            def scale_y(g, k):
                act.wait_ge(rstd_done, NT * g + k + 1)
                act.activation(yn[:, k, :], y[:, k % 2, :], ACT.Copy, scale=rstd[:, k % 2:k % 2 + 1]).then_inc(yn_done, 1)

            def step(g, first, last):
                for s in range(SLOTS):
                    before, mult, _ = tail_of(g, s, first)
                    if s % 2 == 0:
                        m = s // 2 + 1
                        if m < TILES:
                            split_hi(g, m)
                        elif not last:
                            split_hi(g + 1, 0)
                    if s < CONV_SLOTS:
                        tap(g, s)
                        if s:
                            tanh(g, s - 1)
                    else:
                        if s == CONV_SLOTS:
                            tanh(g, s - 1)
                        gate_in(g, s)
                        if s == CONV_SLOTS and not last:
                            tap_params(g + 1)
                    if mult is not None:
                        square(before, mult)
                        scale_y(before, mult)
                    if s in (4, 5):
                        load_cum(g, s - 4)
                    if START <= s:
                        k = s - START
                        exps(g, k)
                        if k < NT - 2:
                            load_cum(g, k + 2)
                        if k < MOVES:
                            b_tokens(g, k)
                        if k:
                            square(g, k - 1)
                            scale_y(g, k - 1)

            tap_params(0)
            split_hi(0, 0)
            groups(act, step)
            square(GROUPS - 1, NT - 1)
            scale_y(GROUPS - 1, NT - 1)

        @block.vector
        def _(dve):
            def split_lo(g, m):
                dve.wait_ge(w_hi_done, TILES * g + m + 1)
                need(dve, proj_done, SLOTS * g + 2 * (m - 1))
                dve.tensor_tensor(w_lo[m % 2][:, :, :], w_raw[:, m % 2, :, :], w_hi[m % 2][:, :, :].bitcast(F32),
                                  ALU.subtract).then_inc(w_split, 1)

            def conv(g, s):
                m = s // 2
                dve.wait_ge(tap_done, CONV_SLOTS * g + s + 1)
                for back in (1, 2, 3):
                    if back > 1:
                        dve.wait_ge(conv_step, 2 * (CONV_SLOTS * g + s) + back - 1)
                    dve.scalar_tensor_tensor(acc[:, s % 2, back:], bank_proj[s % 2][:, 0:SEQ - back],
                                             mix.conv_w[:, g, m, 3 - back:4 - back], acc[:, s % 2, back:],
                                             ALU.mult, ALU.add).then_inc(conv_taken if back == 3 else conv_step, 1)

            def silu(g, s):
                m, q = divmod(s, SEQS)
                dve.wait_ge(tanh_done, SLOTS * g + s + 1)
                if s == 0:
                    need(dve, started, NT * g)
                if m == CONV_TILES - 1:
                    need(dve, multiplied, NT * g)
                dve.scalar_tensor_tensor(xbc[:, m, q * SEQ:(q + 1) * SEQ], th[:, s % 2, :], 1.0, acc[:, s % 2, :],
                                         ALU.add, ALU.mult).then_inc(silu_done, 1)

            def gate_silu(g, s):
                v = s - CONV_SLOTS
                t, q = divmod(v, SEQS)
                dve.wait_ge(gate_taken, GATE_SLOTS * g + v + 1)
                dve.scalar_tensor_tensor(gate[:, t, q * SEQ:(q + 1) * SEQ], th[:, s % 2, :], 1.0,
                                         gate[:, t, q * SEQ:(q + 1) * SEQ], ALU.add, ALU.mult).then_inc(gate_done, 1)

            def diffs(g, k):
                dve.wait_ge(cum_loaded[k % 2], 16 * ((NT // 2) * g + k // 2 + 1))
                need(dve, multiplied, NT * g + k - 1)
                for h in range(HPG):
                    op = dve.tensor_scalar(attn[:, k % 2, h, :], cum_b[:, k % 2, h, :],
                                           mix.cum[:, chunk_tile(k), bass.ds(g * HPG + h, 1)], 0.0,
                                           ALU.subtract, ALU.min)
                op.then_inc(diff_done, 1)

            def after_start(g, k):
                dve.wait_ge(started, NT * g + k + 1)
                dve.tensor_tensor(bc[:, :], bank_bg[:, P:2 * P], core.causal[:, :], ALU.mult).then_inc(bc_done, 1)
                need(dve, multiplied, NT * g + k - 1)
                dve.tensor_tensor(heads(dtx[:, k % 2, :]), heads(bank_x[:, :]), per_head(mix.dt, k, g),
                                  ALU.mult).then_inc(dtx_done, 1)
                dve.wait_ge(exp_done, NT * g + k + 1)
                dve.wait_ge(bc_done, NT * g + k + 1)
                dve.tensor_tensor(attn[:, k % 2, :, :], attn[:, k % 2, :, :],
                                  bc[:, :].unsqueeze(1).to_broadcast([P, HPG, P]), ALU.mult).then_inc(attn_done, 1)
                dve.tensor_tensor(heads(dx[:, :]), heads(bank_x[:, :]),
                                  mix.d_all[:, bass.ds(g * HPG, HPG)].unsqueeze(2).to_broadcast([P, HPG, HD]),
                                  ALU.mult).then_inc(dx_done, 1)

            def after_mult(g, k):
                dve.wait_ge(multiplied, NT * g + k + 1)
                need(dve, yn_done, NT * g + k - 1)
                yk = y[:, k % 2, :]
                if k < SEQS:
                    dve.wait_ge(dx_done, NT * g + k + 1)
                    dve.tensor_tensor(yk, bank_y[:, :], dx[:, :], ALU.add).then_inc(y_done, 1)
                    dve.tensor_copy(state[:, k % 2, :], bank_state[:, :]).then_inc(state_done, 1)
                    return
                at = 2 * (MOVES * g + k - SEQS)
                dve.tensor_tensor(heads(inter[:, :]), heads(bank_inter[:, :]), per_head(mix.exp_cum, k, g),
                                  ALU.mult).then_inc(inter_step, 1)
                if k < MOVES:
                    dve.wait_ge(state_done, MOVES * g + k - SEQS + 1)
                    dve.tensor_tensor(heads(state[:, k % 2, :]), heads(state[:, k % 2, :]), per_head(mix.exp_last, k, g),
                                      ALU.mult).then_inc(state_step, 1)
                dve.wait_ge(inter_step, at + 1)
                dve.tensor_tensor(inter[:, :], inter[:, :], bank_y[:, :], ALU.add).then_inc(inter_step, 1)
                if k < MOVES:
                    dve.wait_ge(state_step, (MOVES - SEQS) * g + k - SEQS + 1)
                    dve.tensor_tensor(state[:, k % 2, :], state[:, k % 2, :], bank_state[:, :],
                                      ALU.add).then_inc(state_done, 1)
                dve.wait_ge(inter_step, at + 2)
                dve.wait_ge(dx_done, NT * g + k + 1)
                dve.tensor_tensor(yk, inter[:, :], dx[:, :], ALU.add).then_inc(y_done, 1)

            def gate_y(g, k):
                t = chunk_tile(k)
                dve.wait_ge(y_turned, NT * g + k + 1)
                dve.wait_ge(gate_done, GATE_SLOTS * (g + 1))
                need(dve, stored[k % 2], 16 * ((NT // 2) * g + k // 2))
                dve.tensor_tensor(yg[:, k % 2, :, :], bank_turn[:, :].rearrange("p (k i) -> p k i", i=P),
                                  gate[:, :, t * P:(t + 1) * P], ALU.mult).then_inc(gated, 1)

            def step(g, first, last):
                for s in range(SLOTS):
                    before, mult, turn = tail_of(g, s, first)
                    if s % 2 == 0:
                        m = s // 2 + 1
                        if m < TILES:
                            split_lo(g, m)
                        elif not last:
                            split_lo(g + 1, 0)
                    if s < CONV_SLOTS:
                        conv(g, s)
                        if s:
                            silu(g, s - 1)
                    else:
                        if s == CONV_SLOTS:
                            silu(g, s - 1)
                        gate_silu(g, s)
                    if mult is not None:
                        after_mult(before, mult)
                    if turn is not None:
                        gate_y(before, turn)
                    if START <= s:
                        k = s - START
                        diffs(g, k)
                        if k:
                            after_mult(g, k - 1)
                        after_start(g, k)

            split_lo(0, 0)
            groups(dve, step)
            after_mult(GROUPS - 1, NT - 1)
            for k in range(NT):
                gate_y(GROUPS - 1, k)

        @block.tensor
        def _(pe):
            def project(g, s):
                m, q = divmod(s, SEQS)
                pe.wait_ge(w_split, TILES * g + m + 1)
                if s < 2:
                    need(pe, gate_taken, GATE_SLOTS * (g - 1) + GATE_SLOTS - 1 + s)
                elif s < CONV_SLOTS + 2:
                    pe.wait_ge(conv_taken, CONV_SLOTS * g + s - 1)
                else:
                    pe.wait_ge(gate_taken, GATE_SLOTS * g + s - CONV_SLOTS - 1)
                out = bank_proj[s % 2][:, :]
                for k in range(KT):
                    hi = mix.x_hi[:, k, q * SEQ:(q + 1) * SEQ]
                    lo = mix.x_lo[:, k, q * SEQ:(q + 1) * SEQ]
                    pe.matmul(out, w_hi[m % 2][:, k, :], hi, start=(k == 0), stop=False)
                    pe.matmul(out, w_hi[m % 2][:, k, :], lo, start=False, stop=False)
                    mm = pe.matmul(out, w_lo[m % 2][:, k, :], hi, start=False, stop=(k == KT - 1))
                mm.then_inc(proj_done, 1)

            def start(g, k):
                t = chunk_tile(k)
                toks = slice(t * P, (t + 1) * P)
                pe.wait_ge(silu_done, CONV_SLOTS * (g + 1))
                need(pe, dx_done, NT * g + k)
                need(pe, bc_done, NT * g + k)
                need(pe, b_copied, MOVES * g + min(k, MOVES))
                for c in range(XT):
                    pe.transpose(bank_x[:, c * P:(c + 1) * P], xbc[:, c, toks], core.ident[:, :])
                pe.transpose(bank_bg[:, 0:P], xbc[:, XT, toks], core.ident[:, :])
                pe.matmul(bank_bg[:, P:2 * P], xbc[:, XT, toks], xbc[:, XT + 1, toks],
                          start=True, stop=True).then_inc(started, 1)

            def mult(g, k):
                t = chunk_tile(k)
                pe.wait_ge(attn_done, NT * g + k + 1)
                pe.wait_ge(dtx_done, NT * g + k + 1)
                need(pe, y_done, NT * g + k)
                need(pe, state_done, MOVES * g + min(k, MOVES))
                if k < MOVES:
                    pe.wait_ge(dec_done, MOVES * g + k + 1)
                    pe.wait_ge(b_copied, MOVES * g + k + 1)
                    pe.matmul(bank_state[:, :], b_tok[:, k % 2, :], dtx_dec[:, k % 2, :], start=True, stop=True)
                if k >= SEQS:
                    pe.matmul(bank_inter[:, :], xbc[:, XT + 1, t * P:(t + 1) * P], state[:, k % 2, :],
                              start=True, stop=True)
                for h in range(HPG):
                    mm = pe.matmul(bank_y[:, h * HD:(h + 1) * HD], attn[:, k % 2, h, :],
                                   dtx[:, k % 2, h * HD:(h + 1) * HD], start=True, stop=True)
                mm.then_inc(multiplied, 1)

            def turn(g, k):
                pe.wait_ge(yn_done, NT * g + k + 1)
                need(pe, gated, NT * g + k)
                for c in range(XT):
                    mm = pe.transpose(bank_turn[:, c * P:(c + 1) * P], yn[:, k, c * P:(c + 1) * P], core.ident[:, :])
                mm.then_inc(y_turned, 1)

            def step(g, first, last):
                for s in range(SLOTS):
                    before, mult_k, turn_k = tail_of(g, s, first)
                    project(g, s)
                    if mult_k is not None:
                        mult(before, mult_k)
                    if turn_k is not None:
                        turn(before, turn_k)
                    if START <= s:
                        k = s - START
                        if k:
                            mult(g, k - 1)
                        start(g, k)

            groups(pe, step)
            mult(GROUPS - 1, NT - 1)
            for k in range(NT):
                turn(GROUPS - 1, k)


def output_block(nc, core):
    d = core.dram
    bank = core.bank
    NS = STREAMS
    PASSES = 2 * HALVES
    ROWS = 2 * NT
    with ExitStack() as ctx:
        def sb(name, shape, dt=F32):
            return ctx.enter_context(nc.sbuf_tensor(name, shape, dt))

        def sem(name):
            return core.semaphore(name)

        y_raw = sb("y_raw", [P, 2, HALF])
        w_raw = sb("wo_raw", [P, 2, 512])
        y_hi = [sb(f"y_hi{i}", [P, HALF], F32R) for i in range(2)]
        y_lo = [sb(f"y_lo{i}", [P, HALF], F32R) for i in range(2)]
        w_hi = [sb(f"wo_hi{i}", [P, 512], F32R) for i in range(2)]
        w_lo = [sb(f"wo_lo{i}", [P, 512], F32R) for i in range(2)]
        s_sb = sb("s_sb", [P, NT, DM])
        sigm = sb("sigm", [P, 2])
        mat = sb("mat", [P, ROWS, NS, NS])
        mat_e = sb("mat_e", [P, ROWS, NS, NS])
        top = sb("top", [P, ROWS, NS])
        tot = sb("tot", [P, ROWS, NS])
        xq = sb("xq", [P, DM])
        post = sb("post", [P, NS])
        br = sb("br", [P, CW])
        xn = sb("xnq", [P, DM])
        f = sb("f", [P, DM])
        tf = sb("tf", [P, DM])
        o_sb = sb("o_sb", [P, DM])
        f_keep = sb("f_keep", [P, NT, 512])
        x_keep = sb("x_keep", [P, NT, 512])

        k_loaded = [sem("k_loaded0"), sem("k_loaded1")]
        k_hi, k_split, k_done = sem("k_hi"), sem("k_split"), sem("k_done")
        evacuated = [sem("evacuated_even"), sem("evacuated_odd")]
        sig_exp, sig_step = sem("sig_exp"), sem("sig_step")
        guard_step, guard_act, sk_step, res_step = sem("guard_step"), sem("guard_act"), sem("sk_step"), sem("res_step")
        tile_loaded, post_copied = sem("tile_loaded"), sem("post_copied")
        tile_xn, post_done, f_step, f_tanh, f_silu = (sem("tile_xn"), sem("post_done"), sem("f_step"), sem("f_tanh"),
                                                      sem("f_silu"))
        s_mul, x_kept, o_done, o_stored = sem("s_mul"), sem("x_kept"), sem("o_done"), sem("o_stored")
        o_loaded = sem("o_loaded")
        last_mul, last_done, last_stored = sem("last_mul"), sem("last_done"), [sem("last_stored0"), sem("last_stored1")]
        block = ctx.enter_context(nc.Block())

        TURNS = OT // 2 - 2
        SK_TURNS = (TURNS, (SINKHORN - 1) // 2 - TURNS)
        SK_AHEAD = SINKHORN - 1 - 2 * sum(SK_TURNS)

        def k_steps(eng, p, one, extra=None):
            n = SK_TURNS[p]
            if p == 0:
                one(p, 0, 0)
            one(p, 0, 1)
            with eng.Fori(1, 1 + n) as i:
                for j in range(2):
                    one(p, i, j)
                    if extra is not None:
                        extra(p, i - 1, j)
            if n < TURNS:
                with eng.Fori(1 + n, OT // 2 - 1) as i:
                    one(p, i, 0)
                    one(p, i, 1)
            one(p, OT // 2 - 1, 0)
            one(p, OT // 2 - 1, 1)
            one(p + 1, 0, 0)

        def tile_steps(eng, p, one, part):
            def turn(i, last):
                for q in range(4):
                    if not (last and q == 3):
                        one(p, 2 * i + (q + 1) // 2, (q + 1) % 2)
                    elif p + 1 < PASSES:
                        one(p + 1, 0, 0)
                    part((p - 2) * NT + i, i, p, q, last)

            with eng.Fori(0, NT - 1) as i:
                turn(i, False)
            turn(NT - 1, True)

        @block.sync
        def _(sp):
            def load(p, i, j):
                need(sp, k_split, OT * p + 2 * i + j - 1)
                sp.dma_start(y_raw[:, j, :], d["y"][p // 2, 2 * i + j]).then_inc(k_loaded[j], 16)
                sp.dma_start(w_raw[:, j, :], d["w_out"][p % 2, 2 * i + j]).then_inc(k_loaded[j], 16)

            for p in range(2):
                k_steps(sp, p, load)
            def load_tile(n, i, p):
                sp.dma_start(xq[:, :], d["x"][n]).then_inc(tile_loaded, 16)
                sp.dma_start(br[:, :], d["branch"][p - 2, :, i, :]).then_inc(tile_loaded, 16)

            def tile(n, i, p, q, last):
                if q == 1 and not (last and p == PASSES - 1):
                    sp.wait_ge(tile_xn, n + 1)
                    sp.wait_ge(post_done, NS * n + NS)
                    load_tile(n + 1, 0 if last else i + 1, p + 1 if last else p)

            load_tile(0, 0, 2)
            for p in range(2, PASSES):
                tile_steps(sp, p, load, tile)

        @block.gpsimd
        def _(pool):
            def tile(n, i, p, q, last):
                if q:
                    return
                pool.dma_start(o_sb[:, :], d["x"][n]).then_inc(o_loaded, 16)
                width = DM if p == 2 else 512
                pool.wait_ge(o_loaded, 16 * n + 16)
                if p == 3:
                    pool.tensor_copy(x_keep[:, i, :], o_sb[:, 512:]).then_inc(x_kept, 1)
                pool.wait_ge(s_mul, n + 1)
                pool.tensor_tensor(o_sb[:, 0:width], tf[:, 0:width], o_sb[:, 0:width], ALU.add).then_inc(o_done, 1)
                pool.wait_ge(o_done, n + 1)
                if p == 3:
                    pool.wait_ge(x_kept, i + 1)
                pool.nop(nofuse=True)
                pool.dma_start(d["out"][n][:, 0:width], o_sb[:, 0:width]).then_inc(o_stored, 16)
                pool.wait_ge(o_stored, 16 * n + 16)
                pool.nop(nofuse=True)

            for p in range(2, PASSES):
                tile_steps(pool, p, lambda p, i, j: None, tile)
            for t in range(NT):
                pool.wait_ge(last_mul, t + 1)
                pool.tensor_tensor(f_keep[:, t, :], f_keep[:, t, :], x_keep[:, t, :], ALU.add).then_inc(last_done, 1)
            pool.wait_ge(o_stored, 16 * ROWS)

        @block.scalar
        def _(act):
            def split_hi(p, i, j):
                kk = OT * p + 2 * i + j
                act.wait_ge(k_loaded[j], 32 * ((OT // 2) * p + i + 1))
                need(act, k_done, kk - 1)
                act.activation(y_hi[j][:, :], y_raw[:, j, :], ACT.Copy)
                act.activation(w_hi[j][:, :], w_raw[:, j, :], ACT.Copy).then_inc(k_hi, 1)

            def evacuate(p):
                act.wait_ge(k_done, OT * (p + 1))
                if p == 2:
                    act.wait_ge(s_mul, NT)
                for t in range(0, NT, 2):
                    act.activation(s_sb[:, t, (p % 2) * 512:(p % 2 + 1) * 512], bank[t][:, :],
                                   ACT.Copy).then_inc(evacuated[0], 1)

            def tile(n, i, p, q, last):
                if q == 0:
                    act.activation(post[:, :], core.h_post[:, n, :], ACT.Copy).then_inc(post_copied, 1)
                    act.wait_ge(post_copied, n + 1)
                    act.wait_ge(tile_loaded, 32 * n + 32)
                    for s in range(NS):
                        act.activation(f[:, s * CW:(s + 1) * CW], br[:, :], ACT.Copy,
                                       scale=post[:, s:s + 1]).then_inc(post_done, 1)
                if q == 1:
                    act.wait_ge(o_loaded, 16 * n + 16)
                    act.wait_ge(f_step, NS * NS * (n + 1))
                    act.activation(tf[:, :], f[:, :], ACT.Tanh, scale=0.5).then_inc(f_tanh, 1)
                if q == 3:
                    act.wait_ge(f_silu, n + 1)

            act.activation(sigm[:, 0:1], core.gate_value[:, 0:1], ACT.Exp, scale=-1.0).then_inc(sig_exp, 1)
            act.wait_ge(guard_step, 3)
            act.activation(mat_e[:, :, :, :], mat[:, :, :, :], ACT.Exp).then_inc(guard_act, 1)
            act.wait_ge(guard_step, 4)
            act.activation(tot[:, :, :], tot[:, :, :], ACT.Ln).then_inc(guard_act, 1)
            act.wait_ge(guard_step, 7)
            act.activation(mat[:, :, :, :], mat[:, :, :, :], ACT.Exp).then_inc(guard_act, 1)
            for p in range(2):
                k_steps(act, p, split_hi)
                evacuate(p)
            tile_steps(act, 2, split_hi, tile)
            evacuate(2)
            tile_steps(act, 3, split_hi, tile)
            for t in range(NT):
                act.wait_ge(last_done, t + 1)
                act.dma_start(d["out"][NT + t][:, 512:], f_keep[:, t, :]).then_inc(last_stored[t % 2], 16)
            for i in range(2):
                act.wait_ge(last_stored[i], 16 * NT // 2)

        @block.vector
        def _(dve):
            def split_lo(p, i, j):
                kk = OT * p + 2 * i + j
                dve.wait_ge(k_hi, kk + 1)
                need(dve, k_done, kk - 1)
                dve.tensor_tensor(y_lo[j][:, :], y_raw[:, j, :], y_hi[j][:, :].bitcast(F32), ALU.subtract)
                dve.tensor_tensor(w_lo[j][:, :], w_raw[:, j, :], w_hi[j][:, :].bitcast(F32), ALU.subtract).then_inc(k_split, 1)

            def over_rows(a):
                return a.unsqueeze(3).to_broadcast([P, ROWS, NS, NS])

            def over_columns(a):
                return a.unsqueeze(2).to_broadcast([P, ROWS, NS, NS])

            by_row = mat[:, :, :, :]
            by_column = mat[:, :, :, :].rearrange("p t i j -> p t j i")

            def guarded():
                dve.tensor_reduce(top[:, :, :], by_row, AX.X, ALU.max).then_inc(guard_step, 1)
                dve.wait_ge(guard_step, 2)
                dve.tensor_tensor(by_row, by_row, over_rows(top[:, :, :]), ALU.subtract).then_inc(guard_step, 1)
                dve.wait_ge(guard_act, 1)
                dve.tensor_reduce(tot[:, :, :], mat_e[:, :, :, :], AX.X, ALU.add).then_inc(guard_step, 1)
                dve.wait_ge(guard_act, 2)
                dve.tensor_tensor(by_row, by_row, over_rows(tot[:, :, :]), ALU.subtract).then_inc(guard_step, 1)
                dve.wait_ge(guard_step, 5)
                dve.tensor_reduce(top[:, :, :], by_column, AX.X, ALU.max).then_inc(guard_step, 1)
                dve.wait_ge(guard_step, 6)
                dve.tensor_tensor(by_row, by_row, over_columns(top[:, :, :]), ALU.subtract).then_inc(guard_step, 1)
                dve.wait_ge(guard_act, 3)
                dve.tensor_reduce(tot[:, :, :], by_column, AX.X, ALU.add).then_inc(guard_step, 1)
                dve.wait_ge(guard_step, 8)
                dve.reciprocal(tot[:, :, :], tot[:, :, :]).then_inc(guard_step, 1)
                dve.wait_ge(guard_step, 9)
                dve.tensor_tensor(by_row, by_row, over_columns(tot[:, :, :]), ALU.mult).then_inc(guard_step, 1)
                dve.wait_ge(guard_step, 10)

            def iterate(n):
                for side, view, over in ((0, by_row, over_rows), (1, by_column, over_columns)):
                    at = 3 * (2 * n + side)
                    if not (isinstance(at, int) and at == 0):
                        dve.wait_ge(sk_step, at)
                    dve.tensor_reduce(tot[:, :, :], view, AX.X, ALU.add).then_inc(sk_step, 1)
                    dve.wait_ge(sk_step, at + 1)
                    dve.reciprocal(tot[:, :, :], tot[:, :, :]).then_inc(sk_step, 1)
                    dve.wait_ge(sk_step, at + 2)
                    dve.tensor_tensor(by_row, by_row, over(tot[:, :, :]), ALU.mult).then_inc(sk_step, 1)

            def extra(p, i, j):
                iterate(SK_AHEAD + 2 * (p * SK_TURNS[0]) + 2 * i + j)

            def evacuate(p):
                dve.wait_ge(k_done, OT * (p + 1))
                if p == 2:
                    dve.wait_ge(s_mul, NT)
                for t in range(1, NT, 2):
                    dve.tensor_copy(s_sb[:, t, (p % 2) * 512:(p % 2 + 1) * 512], bank[t][:, :]).then_inc(evacuated[1], 1)

            def tile(n, i, p, q, last):
                if q == 0:
                    dve.wait_ge(tile_loaded, 32 * n + 32)
                    dve.tensor_scalar(xn[:, :], xq[:, :], core.mean[:, bass.ds(n, 1)], core.rstd[:, bass.ds(n, 1)],
                                      ALU.subtract, ALU.mult).then_inc(tile_xn, 1)
                    dve.wait_ge(tile_xn, n + 1)
                    dve.wait_ge(post_done, NS * n + NS)
                if q < 2:
                    for c in (2 * q, 2 * q + 1):
                        for r in range(NS):
                            if c:
                                dve.wait_ge(f_step, NS * NS * n + NS * (c - 1) + r + 1)
                            out = f[:, r * CW:(r + 1) * CW]
                            dve.scalar_tensor_tensor(out, xn[:, c * CW:(c + 1) * CW], mat[:, n, r, c:c + 1], out,
                                                     ALU.mult, ALU.add).then_inc(f_step, 1)
                if q == 2:
                    dve.wait_ge(f_tanh, n + 1)
                    dve.scalar_tensor_tensor(tf[:, :], tf[:, :], 1.0, f[:, :], ALU.add, ALU.mult).then_inc(f_silu, 1)
                if q == 3:
                    dve.wait_ge(f_silu, n + 1)
                    if p == 2:
                        dve.scalar_tensor_tensor(tf[:, :], tf[:, :], 0.5, s_sb[:, i, :], ALU.mult,
                                                 ALU.mult).then_inc(s_mul, 1)
                    else:
                        dve.tensor_scalar(f_keep[:, i, :], tf[:, 512:], 0.5, None, ALU.mult)
                        dve.scalar_tensor_tensor(tf[:, 0:512], tf[:, 0:512], 0.5, s_sb[:, i, 0:512], ALU.mult,
                                                 ALU.mult).then_inc(s_mul, 1)

            dve.wait_ge(sig_exp, 1)
            dve.tensor_scalar(sigm[:, 0:1], sigm[:, 0:1], 1.0, None, ALU.add).then_inc(sig_step, 1)
            dve.tensor_scalar(mat[:, :, :, :], core.res_logits[:, :, :].rearrange("p t (i j) -> p t i j", j=NS),
                              1.0 / TAU, None, ALU.mult).then_inc(guard_step, 1)
            dve.wait_ge(sig_step, 1)
            dve.reciprocal(sigm[:, 0:1], sigm[:, 0:1]).then_inc(sig_step, 1)
            dve.wait_ge(sig_step, 2)
            dve.tensor_scalar(sigm[:, 1:2], sigm[:, 0:1], -1.0, 1.0, ALU.mult, ALU.add).then_inc(sig_step, 1)
            dve.wait_ge(guard_step, 1)
            guarded()
            for n in range(SK_AHEAD):
                iterate(n)
            for p in range(2):
                k_steps(dve, p, split_lo, extra)
                evacuate(p)
            dve.wait_ge(sk_step, 6 * (SINKHORN - 1))
            dve.wait_ge(sig_step, 3)
            dve.tensor_scalar(by_row, by_row, sigm[:, 0:1], None, ALU.mult).then_inc(res_step, 1)
            dve.wait_ge(res_step, 1)
            diag = mat[:, :, :, :].rearrange("p t i j -> p t (i j)")[:, :, 0::NS + 1]
            dve.tensor_scalar(diag, diag, sigm[:, 1:2], None, ALU.add).then_inc(res_step, 1)
            dve.wait_ge(res_step, 2)
            dve.wait_ge(evacuated[0], NT)
            dve.wait_ge(evacuated[1], NT)
            tile_steps(dve, 2, split_lo, tile)
            evacuate(2)
            dve.wait_ge(evacuated[0], 3 * NT // 2)
            dve.wait_ge(evacuated[1], 3 * NT // 2)
            tile_steps(dve, 3, split_lo, tile)
            dve.wait_ge(k_done, OT * PASSES)
            dve.wait_ge(s_mul, ROWS)
            for t in range(NT):
                dve.tensor_tensor(f_keep[:, t, :], f_keep[:, t, :], bank[t][:, :], ALU.mult).then_inc(last_mul, 1)

        @block.tensor
        def _(pe):
            def products(p, i, j, first=False, last=False):
                pe.wait_ge(k_split, OT * p + 2 * i + j + 1)
                for t in range(NT):
                    if first and p:
                        pe.wait_ge(evacuated[t % 2], NT // 2 * (p - 1) + t // 2 + 1)
                    toks = slice(t * P, (t + 1) * P)
                    pe.matmul(bank[t][:, :], y_hi[j][:, toks], w_hi[j][:, :], start=first, stop=False)
                    pe.matmul(bank[t][:, :], y_hi[j][:, toks], w_lo[j][:, :], start=False, stop=False)
                    mm = pe.matmul(bank[t][:, :], y_lo[j][:, toks], w_hi[j][:, :], start=False, stop=last)
                mm.then_inc(k_done, 1)

            for p in range(PASSES):
                products(p, 0, 0, first=True)
                products(p, 0, 1)
                with pe.Fori(1, OT // 2 - 1) as i:
                    products(p, i, 0)
                    products(p, i, 1)
                products(p, OT // 2 - 1, 0)
                products(p, OT // 2 - 1, 1, last=True)


def program(nc, x, w_in, w_small, conv_w, norm_w, D, dt_bias, A_log, base, w_branch, gate, w_out, out):
    def scratch(name, shape):
        return nc.dram_tensor(name, shape, F32, kind="Internal").ap()

    dram = dict(x=x, w_in=w_in, w_small=w_small, conv_w=conv_w, norm_w=norm_w, D=D, dt_bias=dt_bias,
                A_log=A_log, base=base, w_branch=w_branch, gate=gate, w_out=w_out, out=out,
                cum=scratch("cum_scratch", (HALVES, NT, HEADS, P)), last=scratch("last_scratch", (HALVES, HEADS, NT)),
                y=scratch("y_scratch", (HALVES, OT, P, HALF)), branch=scratch("branch_scratch", (HALVES, P, NT, CW)))
    with ExitStack() as ctx:
        core = Core(nc, ctx, dram)
        with ExitStack() as inner:
            mix = Mixer(nc, inner)
            setup_block(nc, core, mix)
            core.end_phase()
            for half in range(HALVES):
                prepare_block(nc, core, mix, half)
                core.end_phase()
                mixer_block(nc, core, mix, half)
                core.end_phase()
        output_block(nc, core)


def kernel(**inputs):
    import numpy as _np
    import concourse.bacc as _bacc
    from concourse.bass_utils import run_bass_kernel_spmd as _run

    a = {n.replace("L0_attn_", "").replace("L0_ffn_", "f_"): _np.asarray(v) for n, v in inputs.items()}
    gn = GROUPS * P
    wi = a["in_proj_w"]

    def tiles(w):
        n = w.shape[0] // (GROUPS * P)
        return w.reshape(GROUPS, n, P, KT, P).transpose(0, 1, 4, 3, 2)

    w_in = _np.concatenate([tiles(wi[INNER:2 * INNER]), tiles(wi[2 * INNER:2 * INNER + gn]),
                            tiles(wi[2 * INNER + gn:2 * INNER + 2 * gn]), tiles(wi[0:INNER])], axis=1)

    def channels(v):
        rest = v.shape[1:]
        parts = [v[0:INNER].reshape(GROUPS, XT, P, *rest), v[INNER:INNER + gn].reshape(GROUPS, 1, P, *rest),
                 v[INNER + gn:].reshape(GROUPS, 1, P, *rest)]
        return _np.moveaxis(_np.concatenate(parts, axis=1), 2, 0)

    small = _np.concatenate([wi[2 * INNER + 2 * gn:], a["f_W_res"], a["f_W_pre"], a["f_W_post"]], axis=0)
    arrays = {
        "x": a["hidden_states"].reshape(2 * NT, P, DM),
        "w_in": w_in,
        "w_small": small.reshape(SMALL, KT, P).transpose(2, 1, 0),
        "conv_w": channels(_np.concatenate([a["conv_weight"], a["conv_bias"][:, None]], axis=1)),
        "norm_w": a["norm_weight"].reshape(GROUPS, XT, P).transpose(2, 0, 1),
        "D": a["D"],
        "dt_bias": a["dt_bias"].reshape(HEADS, 1),
        "A_log": a["A_log"].reshape(HEADS, 1),
        "base": _np.concatenate([a["f_H_res_base"].reshape(-1), a["f_H_pre_base"], a["f_H_post_base"]]),
        "w_branch": a["f_W_branch"].reshape(2, P, CW).transpose(1, 0, 2),
        "gate": a["f_gate"],
        "w_out": a["out_proj_w"].reshape(2, 512, OT, P).transpose(0, 2, 3, 1),
    }
    arrays = {n: _np.ascontiguousarray(v) for n, v in arrays.items()}
    nc = _bacc.Bacc("TRN2", target_bir_lowering=False, num_devices=1)
    args = {n: nc.dram_tensor(f"in_{n}", v.shape, mybir.dt.from_np(v.dtype), kind="ExternalInput").ap()
            for n, v in arrays.items()}
    args["out"] = nc.dram_tensor("out", (2 * NT, P, DM), F32, kind="ExternalOutput").ap()
    program(nc, **args)
    r = _run(nc, [{f"in_{n}": v for n, v in arrays.items()}], core_ids=[0])
    return r.results[0]["out"].reshape(4, SEQ, DM)
```

```python
from contextlib import ExitStack

import concourse.bass as bass
from concourse import mybir

F32 = mybir.dt.float32
F32R = mybir.dt.float32r
ALU = mybir.AluOpType
ACT = mybir.ActivationFunctionType
AX = mybir.AxisListType

P = 128
TOKENS, DM = 2048, 1024
SEQ = 512
HALF = 1024
HALVES = TOKENS // HALF
SEQS = HALF // SEQ
NT = HALF // P
CHUNKS = SEQ // P
KT = DM // P
HEADS, HD, GROUPS = 64, 64, 8
HPG = HEADS // GROUPS
GC = HPG * HD
XT = GC // P
INNER = HEADS * HD
CONV_TILES = XT + 2
TILES = CONV_TILES + XT
SLOTS = TILES * SEQS
CONV_SLOTS = CONV_TILES * SEQS
GATE_SLOTS = XT * SEQS
OT = INNER // P
STREAMS, CW = 4, 256
SMALL = HEADS + STREAMS * STREAMS + 2 * STREAMS
LN_EPS, NORM_EPS, RMS_EPS = 1e-5, 1e-5, 1.1920929e-07
TAU = 0.1
SINKHORN = 50
LOG_ZERO = -110.0


def need(eng, sem, value):
    if isinstance(value, int) and value <= 0:
        return
    eng.wait_ge(sem, value)


def chunk_tile(k):
    return CHUNKS * (k % SEQS) + k // SEQS


class Core:

    def __init__(self, nc, ctx, dram):
        self.nc, self.dram = nc, dram
        self.phase_sems = []

        def sb(name, shape, dt=F32):
            return ctx.enter_context(nc.sbuf_tensor(name, shape, dt))

        self.bank = [ctx.enter_context(nc.psum_tensor(f"bank{i}", [P, 512], F32)) for i in range(8)]
        self.ident = sb("ident", [P, P])
        self.causal = sb("causal", [P, P])
        self.neg_half = sb("neg_half", [P, NT])
        self.mean = sb("mean", [P, 2 * NT])
        self.rstd = sb("rstd", [P, 2 * NT])
        self.res_logits = sb("res_logits", [P, 2 * NT, STREAMS * STREAMS])
        self.h_post = sb("h_post", [P, 2 * NT, STREAMS])
        self.gate_value = sb("gate_value", [P, 1])

    def semaphore(self, name):
        self.phase_sems.append(self.nc.alloc_semaphore(name=name))
        return self.phase_sems[-1]

    def end_phase(self):
        self.nc.all_engine_barrier()
        self.nc.clear_and_free_semaphores(self.phase_sems)
        self.phase_sems = []
        self.nc.all_engine_barrier()


def setup_block(nc, core, mix):
    d = core.dram
    with ExitStack() as ctx:
        loaded = core.semaphore("loaded")
        pool_step = core.semaphore("pool_step")
        halved = core.semaphore("halved")
        scaled = core.semaphore("scaled")
        block = ctx.enter_context(nc.Block())

        @block.sync
        def _(sp):
            sp.dma_start(mix.conv_w[:, :, :, :], d["conv_w"]).then_inc(loaded, 16)
            sp.dma_start(mix.norm_w[:, :, :], d["norm_w"]).then_inc(loaded, 16)
            sp.dma_start(mix.d_all[:, :], d["D"].partition_broadcast(P)).then_inc(loaded, 16)
            sp.dma_start(mix.a_neg[:, :], d["A_log"].partition_broadcast(P)).then_inc(loaded, 16)
            sp.dma_start(core.gate_value[:, :], d["gate"].partition_broadcast(P)).then_inc(loaded, 16)

        @block.gpsimd
        def _(pool):
            pool.memset(core.ident[:, :], 0.0).then_inc(pool_step, 1)
            pool.memset(core.causal[:, :], 1.0).then_inc(pool_step, 1)
            pool.memset(core.neg_half[:, :], -0.5).then_inc(pool_step, 1)
            pool.wait_ge(pool_step, 3)
            pool.affine_select(out=core.ident[:, :], in_=core.ident[:, :], compare_op=ALU.not_equal,
                               fill=1.0, base=0, pattern=[[-1, P]], channel_multiplier=1).then_inc(pool_step, 1)
            pool.affine_select(out=core.causal[:, :], in_=core.causal[:, :], compare_op=ALU.is_ge,
                               fill=0.0, base=0, pattern=[[1, P]], channel_multiplier=-1).then_inc(pool_step, 1)
            pool.wait_ge(pool_step, 5)

        @block.scalar
        def _(act):
            act.wait_ge(loaded, 80)
            act.activation(mix.a_neg[:, :], mix.a_neg[:, :], ACT.Exp).then_inc(halved, 1)

        @block.vector
        def _(dve):
            dve.wait_ge(loaded, 80)
            dve.tensor_scalar(mix.conv_w[:, :, :, :], mix.conv_w[:, :, :, :], 0.5, None, ALU.mult)
            dve.tensor_scalar(mix.norm_w[:, :, :], mix.norm_w[:, :, :], 0.5, None, ALU.mult).then_inc(scaled, 1)
            dve.wait_ge(halved, 1)
            dve.tensor_scalar(mix.a_neg[:, :], mix.a_neg[:, :], -1.0, None, ALU.mult).then_inc(scaled, 1)
            dve.wait_ge(scaled, 2)


class Mixer:

    def __init__(self, nc, ctx):
        def sb(name, shape, dt=F32):
            return ctx.enter_context(nc.sbuf_tensor(name, shape, dt))

        self.conv_w = sb("conv_w", [P, GROUPS, CONV_TILES, 5])
        self.norm_w = sb("norm_w", [P, GROUPS, XT])
        self.d_all = sb("d_all", [P, HEADS])
        self.a_neg = sb("a_neg", [P, HEADS])
        self.x_hi = sb("x_hi", [P, KT, HALF], F32R)
        self.x_lo = sb("x_lo", [P, KT, HALF], F32R)
        self.dt = sb("dt", [P, NT, HEADS])
        self.cum = sb("cum", [P, NT, HEADS])
        self.exp_cum = sb("exp_cum", [P, NT, HEADS])
        self.decay = sb("decay", [P, NT, HEADS])
        self.exp_last = sb("exp_last", [P, NT, HEADS])


START = CONV_SLOTS
MULT = CONV_SLOTS + 1
TURN = SLOTS
EARLY_TURN = 4


def mixer_block(nc, core, mix, half):
    d = core.dram
    bank_proj = core.bank[0:2]
    bank_x, bank_bg, bank_y, bank_inter, bank_state, bank_turn = core.bank[2:8]
    with ExitStack() as ctx:
        def sb(name, shape, dt=F32):
            return ctx.enter_context(nc.sbuf_tensor(f"{name}_{half}", shape, dt))

        def sem(name):
            return core.semaphore(f"{name}_{half}")

        w_raw = sb("w_raw", [P, 2, KT, P])
        w_hi = [sb(f"w_hi{i}", [P, KT, P], F32R) for i in range(2)]
        w_lo = [sb(f"w_lo{i}", [P, KT, P], F32R) for i in range(2)]
        acc = sb("acc", [P, 2, SEQ])
        th = sb("th", [P, 2, SEQ])
        tap_par = sb("tap_par", [P, CONV_TILES, 2])
        xbc = sb("xbc", [P, CONV_TILES, HALF])
        gate = sb("gate", [P, XT, HALF])
        cum_b = sb("cum_b", [P, 2, HPG, P])
        attn = sb("attn", [P, 2, HPG, P])
        bc = sb("bc", [P, P])
        b_tok = sb("b_tok", [P, 2, P])
        dtx = sb("dtx", [P, 2, GC])
        dtx_dec = sb("dtx_dec", [P, 2, GC])
        dx = sb("dx", [P, GC])
        state = sb("state", [P, SEQS, GC])
        inter = sb("inter", [P, GC])
        y = sb("y", [P, 2, GC])
        ssq = sb("ssq", [P, 2])
        var_eps = sb("nvar", [P, 2])
        eps = sb("eps", [P, 1])
        rstd = sb("nrstd", [P, 2])
        yn = sb("yn", [P, NT, GC])
        yg = sb("yg", [P, 2, XT, P])
        mv = sb("mv", [P, NT, 2])
        lv = sb("lv", [P, NT])
        rms = sb("rms", [P, NT])

        def flat(t):
            return t[:, :, :].rearrange("p a b -> p (a b)")

        xt = gate
        small_raw = xbc[:, 0, 0:KT * SMALL].rearrange("p (k c) -> p k c", c=SMALL)
        small_hi, small_lo = w_hi[1][:, :, 0:SMALL], w_lo[1][:, :, 0:SMALL]
        small = flat(yn)[0:SMALL, 0:HALF]
        bx = [flat(yn)[:, DM * (1 + i):DM * (2 + i)] for i in range(2)]
        mixed = [flat(yn)[:, 3 * DM + CW * i:3 * DM + CW * (i + 1)] for i in range(2)]
        mixed_t = [flat(yn)[:, 3 * DM + CW * (2 + i):3 * DM + CW * (3 + i)] for i in range(2)]
        branch = [dtx[:, 0, CW * i:CW * (i + 1)] for i in range(2)]
        w_branch = dtx[:, 1, :].rearrange("p (k c) -> p k c", c=CW)
        decays = attn[:, 0, 0:4, :].rearrange("p a b -> p (a b)").rearrange("p (t h) -> p t h", h=HEADS)
        z = attn[:, 0, 4:8, :].rearrange("p a b -> p (a b)").rearrange("p (t h) -> p t h", h=HEADS)
        soft = attn[:, 1, 0:4, :].rearrange("p a b -> p (a b)").rearrange("p (t h) -> p t h", h=HEADS)
        cum_hm = flat(dtx_dec)[0:HEADS, :]
        ones = inter[:, 0:P]
        LG = SMALL - HEADS
        dt_bias = yg[:, 0, 0, 0:HEADS]
        base = yg[:, 0, 1, 0:LG]
        stats = yg[:, 0, 2, 0:24].rearrange("p (a b c) -> p a b c", a=2, b=2)
        logits = y[:, 0, 0:NT * LG].rearrange("p (t c) -> p t c", c=LG)
        sm = y[:, 1, 0:NT * 2 * STREAMS].rearrange("p (t w s) -> p t w s", w=2, s=STREAMS)
        sm_max = y[:, 1, 128:128 + NT * 2].rearrange("p (t w) -> p t w", w=2)
        sm_sum = y[:, 1, 256:256 + NT * 2].rearrange("p (t w) -> p t w", w=2)

        x_loaded = [sem(f"x_loaded{t}") for t in range(XT)]
        small_loaded, rows_loaded, branch_w_loaded = sem("small_loaded"), sem("rows_loaded"), sem("branch_w_loaded")
        bx_loaded = [sem("bx_loaded0"), sem("bx_loaded1")]
        bn_step, aggr_done, lv_done, ln_rstd_done = sem("bn_step"), sem("aggr_done"), sem("lv_done"), sem("ln_rstd_done")
        xn_done, turned, hi_done, lo_done = sem("xn_done"), sem("turned"), sem("hi_done"), sem("lo_done")
        small_step, small_done, small_copied = sem("small_step"), sem("small_done"), sem("small_copied")
        rms_step, to_tokens, z_done, soft_step, dt_step = (sem("rms_step"), sem("to_tokens"), sem("z_done"),
                                                           sem("soft_step"), sem("dt_step"))
        summed, cum_copied, decay_step = sem("summed"), sem("cum_copied"), sem("decay_step")
        cum_turned, cum_hm_copied, cum_stored = sem("cum_turned"), sem("cum_hm_copied"), sem("cum_stored")
        lg_step, lg_exp = sem("lg_step"), sem("lg_exp")
        bx_done, mix_step, mix_turned, mix_copied = sem("bx_done"), sem("mix_step"), sem("mix_turned"), sem("mix_copied")
        branch_done, branch_copied = sem("branch_done"), sem("branch_copied")
        branch_stored = [sem("branch_stored0"), sem("branch_stored1")]
        w_loaded = [sem("w_loaded0"), sem("w_loaded1")]
        w_hi_done, w_split = sem("w_hi_done"), sem("w_split")
        proj_done, conv_taken, gate_taken = sem("proj_done"), sem("conv_taken"), sem("gate_taken")
        tap_done, conv_step, tanh_done, silu_done = sem("tap_done"), sem("conv_step"), sem("tanh_done"), sem("silu_done")
        gate_done = sem("gate_done")
        cum_loaded = [sem("cum_loaded0"), sem("cum_loaded1")]
        diff_done, exp_done, bc_done, dtx_done = sem("diff_done"), sem("exp_done"), sem("bc_done"), sem("dtx_done")
        dx_done, b_copied, dec_done, attn_done = sem("dx_done"), sem("b_copied"), sem("dec_done"), sem("attn_done")
        started, multiplied, y_turned = sem("started"), sem("multiplied"), sem("y_turned")
        inter_step, y_done, state_step, state_done = sem("inter_step"), sem("y_done"), sem("state_step"), sem("state_done")
        squared, nvar_done, rstd_done, yn_done = sem("squared"), sem("nvar_done"), sem("nrstd_done"), sem("yn_done")
        gated = sem("gated")
        stored = [sem("stored0"), sem("stored1")]
        constants, tap_ready = sem("constants"), sem("tap_ready")
        block = ctx.enter_context(nc.Block())

        MOVES = NT - SEQS

        def heads(ap):
            return ap.rearrange("p (h c) -> p h c", c=HD)

        def per_head(table, k, g):
            return table[:, chunk_tile(k), bass.ds(g * HPG, HPG)].unsqueeze(2).to_broadcast([P, HPG, HD])

        def groups(eng, step):
            step(0, True, False)
            step(1, False, False)
            with eng.Fori(2, GROUPS - 1) as g:
                step(g, False, False)
            step(GROUPS - 1, False, True)

        def tail_of(g, s, first):
            if first:
                return None, None, None
            return g - 1, (NT - 1 if s == MULT + NT - 1 - SLOTS else None), (s if s < NT else None)

        @block.sync
        def _(sp):
            def load_w(g, m):
                n = TILES * g + m
                need(sp, w_split, n - 1)
                sp.dma_start(w_raw[:, m % 2, :, :], d["w_in"][g, m]).then_inc(w_loaded[m % 2], 16)

            def store(g, k):
                sp.wait_ge(gated, NT * g + k + 1)
                t = chunk_tile(k)
                sp.dma_start(d["y"][half, bass.ds(g * XT, XT), :, t * P:(t + 1) * P].rearrange("k p i -> p k i"),
                             yg[:, k % 2, :, :]).then_inc(stored[k % 2], 16)

            def load_bx(t):
                if t >= 2:
                    sp.wait_ge(mix_step, 3 * (t - 1))
                else:
                    sp.wait_ge(small_copied, 2)
                sp.dma_start(bx[t % 2], d["x"][half * NT + t]).then_inc(bx_loaded[t % 2], 16)

            def step(g, first, last):
                for s in range(SLOTS):
                    if first and s < NT:
                        load_bx(s)
                    if not first and s < NT:
                        store(g - 1, s)
                    if s % 2 == 0:
                        ahead = s // 2 + 3
                        if ahead < TILES:
                            load_w(g, ahead)
                        elif not last:
                            load_w(g + 1, ahead - TILES)

            def load_x(t):
                need(sp, turned, 2 * (t - XT) + 2)
                sp.dma_start(xt[:, t % XT, :], d["x"][half * NT + t]).then_inc(x_loaded[t % XT], 16)

            for t in range(NT):
                load_x(t)
                if t == 1:
                    sp.dma_start(small_raw, d["w_small"]).then_inc(small_loaded, 16)
                    sp.dma_start(dt_bias, d["dt_bias"].partition_broadcast(P)).then_inc(rows_loaded, 16)
                    sp.dma_start(base, d["base"].partition_broadcast(P)).then_inc(rows_loaded, 16)
                if t == 3:
                    load_w(0, 0)
                    load_w(0, 1)
                    sp.dma_start(w_branch, d["w_branch"]).then_inc(branch_w_loaded, 16)
            load_w(0, 2)
            groups(sp, step)
            for k in range(NT):
                store(GROUPS - 1, k)
            for i in range(2):
                sp.wait_ge(stored[i], 16 * GROUPS * NT // 2)
                sp.wait_ge(branch_stored[i], 16 * NT // 2)
            sp.wait_ge(cum_stored, 16)

        @block.gpsimd
        def _(pool):
            def decayed(g, k):
                pool.wait_ge(dtx_done, NT * g + k + 1)
                need(pool, multiplied, NT * g + k - 1)
                pool.tensor_tensor(heads(dtx_dec[:, k % 2, :]), heads(dtx[:, k % 2, :]),
                                   per_head(mix.decay, k, g), ALU.mult).then_inc(dec_done, 1)

            def norm(g, k):
                pool.wait_ge(squared, NT * g + k + 1)
                pool.tensor_tensor(var_eps[:, k % 2:k % 2 + 1], ssq[:, k % 2:k % 2 + 1], eps[:, :],
                                   ALU.add).then_inc(nvar_done, 1)
                pool.wait_ge(nvar_done, NT * g + k + 1)
                need(pool, yn_done, NT * g + k - 1)
                pool.tensor_tensor(rstd[:, k % 2:k % 2 + 1], var_eps[:, k % 2:k % 2 + 1], core.neg_half[:, 0:1],
                                   ALU.pow).then_inc(rstd_done, 1)

            def front():
                pool.memset(ones, 1.0).then_inc(constants, 1)
                for t in range(NT):
                    col = core.rstd[:, half * NT + t:half * NT + t + 1]
                    pool.wait_ge(aggr_done, t + 1)
                    pool.tensor_scalar(lv[:, t:t + 1], mv[:, t, 1:2], LN_EPS, None, ALU.add).then_inc(lv_done, 1)
                    pool.wait_ge(lv_done, t + 1)
                    pool.tensor_tensor(col, lv[:, t:t + 1], core.neg_half[:, 0:1], ALU.pow).then_inc(ln_rstd_done, 1)
                pool.wait_ge(ln_rstd_done, NT)
                rstds = core.rstd[:, half * NT:(half + 1) * NT]
                pool.tensor_tensor(rms[:, :], mv[:, :, 1], rstds, ALU.mult).then_inc(rms_step, 1)
                pool.wait_ge(rms_step, 1)
                pool.tensor_tensor(rms[:, :], rms[:, :], rstds, ALU.mult).then_inc(rms_step, 1)
                pool.wait_ge(rms_step, 2)
                pool.tensor_scalar(rms[:, :], rms[:, :], RMS_EPS, None, ALU.add).then_inc(rms_step, 1)
                pool.wait_ge(rms_step, 3)
                pool.tensor_tensor(rms[:, :], rms[:, :], core.neg_half[:, :], ALU.pow).then_inc(rms_step, 1)

            def mix_streams(t):
                pool.wait_ge(bx_done, t + 1)
                pool.wait_ge(lg_step, 9)
                need(pool, mix_turned, t - 1)
                streams = bx[t % 2].rearrange("p (s c) -> p s c", c=CW)
                weights = sm[:, t, 0, :].unsqueeze(2).to_broadcast([P, STREAMS, CW])
                pool.tensor_tensor(streams, streams, weights, ALU.mult).then_inc(mix_step, 1)
                pool.wait_ge(mix_step, 3 * t + 1)
                pool.tensor_tensor(bx[t % 2][:, 0:2 * CW], bx[t % 2][:, 0:2 * CW], bx[t % 2][:, 2 * CW:],
                                   ALU.add).then_inc(mix_step, 1)
                pool.wait_ge(mix_step, 3 * t + 2)
                pool.tensor_tensor(mixed[t % 2], bx[t % 2][:, 0:CW], bx[t % 2][:, CW:2 * CW], ALU.add).then_inc(mix_step, 1)

            def step(g, first, last):
                if first:
                    for t in range(NT):
                        mix_streams(t)
                    pool.wait_ge(cum_stored, 16)
                for s in range(SLOTS):
                    before, mult, _ = tail_of(g, s, first)
                    if mult is not None:
                        norm(before, mult)
                    if START <= s:
                        k = s - START
                        if k:
                            norm(g, k - 1)
                        if k < MOVES:
                            decayed(g, k)

            pool.memset(eps[:, :], NORM_EPS).then_inc(constants, 1)
            front()
            pool.wait_ge(constants, 2)
            groups(pool, step)
            norm(GROUPS - 1, NT - 1)

        @block.scalar
        def _(act):
            def split_hi(g, m):
                n = TILES * g + m
                act.wait_ge(w_loaded[m % 2], 16 * ((TILES // 2) * g + m // 2 + 1))
                need(act, proj_done, SLOTS * g + 2 * (m - 1))
                act.activation(w_hi[m % 2][:, :, :], w_raw[:, m % 2, :, :], ACT.Copy).then_inc(w_hi_done, 1)

            def tap(g, s):
                act.wait_ge(proj_done, SLOTS * g + s + 1)
                need(act, silu_done, CONV_SLOTS * g + s - 1)
                act.wait_ge(tap_ready, g + 1)
                m = s // 2
                act.activation(acc[:, s % 2, :], bank_proj[s % 2][:, :], ACT.Identity,
                               bias=tap_par[:, m, 1:2], scale=tap_par[:, m, 0:1]).then_inc(tap_done, 1)

            def tap_params(g):
                act.activation(tap_par[:, :, :], mix.conv_w[:, g, :, 3:5], ACT.Copy).then_inc(tap_ready, 1)

            def tanh(g, s):
                act.wait_ge(conv_taken, CONV_SLOTS * g + s + 1)
                act.activation(th[:, s % 2, :], acc[:, s % 2, :], ACT.Tanh).then_inc(tanh_done, 1)

            def gate_in(g, s):
                v = s - CONV_SLOTS
                t, q = divmod(v, SEQS)
                act.wait_ge(proj_done, SLOTS * g + s + 1)
                if v < 2:
                    act.wait_ge(silu_done, CONV_SLOTS * g + s - 1)
                else:
                    act.wait_ge(gate_done, GATE_SLOTS * g + v - 1)
                if v == 0:
                    need(act, gated, NT * g)
                act.activation(th[:, s % 2, :], bank_proj[s % 2][:, :], ACT.Tanh, scale=0.5).then_inc(tanh_done, 1)
                act.activation(gate[:, t, q * SEQ:(q + 1) * SEQ], bank_proj[s % 2][:, :], ACT.Identity,
                               scale=mix.norm_w[:, g, t:t + 1]).then_inc(gate_taken, 1)

            def load_cum(g, k):
                need(act, diff_done, NT * g + k - 1)
                act.dma_start(cum_b[:, k % 2, :, :],
                              d["cum"][half, chunk_tile(k), bass.ds(g * HPG, HPG), :].partition_broadcast(P)
                              ).then_inc(cum_loaded[k % 2], 16)

            def exps(g, k):
                act.wait_ge(diff_done, NT * g + k + 1)
                act.activation(attn[:, k % 2, :, :], attn[:, k % 2, :, :], ACT.Exp).then_inc(exp_done, 1)

            def b_tokens(g, k):
                act.wait_ge(bc_done, NT * g + k + 1)
                need(act, multiplied, NT * g + k - 1)
                act.activation(b_tok[:, k % 2, :], bank_bg[:, 0:P], ACT.Copy).then_inc(b_copied, 1)

            def square(g, k):
                act.wait_ge(y_done, NT * g + k + 1)
                need(act, y_turned, NT * (g - 1) + k + 1)
                act.activation(yn[:, k, :], y[:, k % 2, :], ACT.Square, scale=GC ** -0.5,
                               accum_out=ssq[:, k % 2:k % 2 + 1]).then_inc(squared, 1)

            def scale_y(g, k):
                act.wait_ge(rstd_done, NT * g + k + 1)
                act.activation(yn[:, k, :], y[:, k % 2, :], ACT.Copy, scale=rstd[:, k % 2:k % 2 + 1]).then_inc(yn_done, 1)

            def high(n):
                t, h = divmod(n, 2)
                act.wait_ge(turned, n + 1)
                act.activation(mix.x_hi[:, 4 * h:4 * h + 4, t * P:(t + 1) * P],
                               core.bank[2 + n % 4][:, :].rearrange("p (k c) -> p k c", c=P), ACT.Copy).then_inc(hi_done, 1)

            def by_token(bank):
                return bank[:, :].rearrange("p (t h) -> p t h", h=HEADS)

            def early(s):
                if s == 2:
                    act.wait_ge(z_done, 2)
                    act.activation(soft, z, ACT.Abs).then_inc(soft_step, 1)
                    act.wait_ge(soft_step, 1)
                    act.activation(soft, soft, ACT.Exp, scale=-1.0).then_inc(soft_step, 1)
                    act.wait_ge(soft_step, 2)
                    act.activation(soft, soft, ACT.Ln, bias=1.0).then_inc(soft_step, 1)
                if s == 3:
                    act.wait_ge(lg_step, 6)
                    act.activation(sm, sm, ACT.Exp).then_inc(lg_exp, 1)
                if s == 4:
                    act.wait_ge(summed, 2)
                    act.activation(mix.cum[:, :, :], by_token(bank_y), ACT.Copy).then_inc(cum_copied, 1)
                    act.activation(mix.exp_cum[:, :, :], by_token(bank_y), ACT.Exp)
                    act.activation(mix.exp_last[:, :, :], by_token(bank_inter), ACT.Exp).then_inc(cum_copied, 1)
                if s == 6:
                    act.wait_ge(decay_step, 1)
                    act.activation(mix.decay[:, :, :], mix.decay[:, :, :], ACT.Exp).then_inc(decay_step, 1)
                    act.wait_ge(cum_turned, 2)
                    for i in range(2):
                        act.activation(cum_hm[:, i * 512:(i + 1) * 512], core.bank[6 + i][0:HEADS, :],
                                       ACT.Copy).then_inc(cum_hm_copied, 1)
                    act.wait_ge(cum_hm_copied, 2)
                    act.dma_start(d["cum"][half].rearrange("t h i -> h t i"),
                                  cum_hm.rearrange("h (t i) -> h t i", i=P)).then_inc(cum_stored, 16)
                t = s - EARLY_TURN - 1
                if 0 <= t < NT:
                    act.wait_ge(branch_done, t + 1)
                    if t >= 2:
                        act.wait_ge(branch_stored[t % 2], 16 * (t // 2))
                    act.activation(branch[t % 2], bank_bg[:, 0:CW], ACT.Copy).then_inc(branch_copied, 1)
                    act.wait_ge(branch_copied, t + 1)
                    act.dma_start(d["branch"][half, :, t, :], branch[t % 2]).then_inc(branch_stored[t % 2], 16)
                t = s - EARLY_TURN
                if 0 <= t < NT:
                    act.wait_ge(mix_turned, t + 1)
                    need(act, branch_done, t - 1)
                    act.activation(mixed_t[t % 2], bank_x[:, 0:CW], ACT.Copy).then_inc(mix_copied, 1)

            def step(g, first, last):
                for s in range(SLOTS):
                    before, mult, _ = tail_of(g, s, first)
                    if first:
                        early(s)
                    if s % 2 == 0:
                        m = s // 2 + 1
                        if m < TILES:
                            split_hi(g, m)
                        elif not last:
                            split_hi(g + 1, 0)
                    if s < CONV_SLOTS:
                        tap(g, s)
                        if s:
                            tanh(g, s - 1)
                    else:
                        if s == CONV_SLOTS:
                            tanh(g, s - 1)
                        gate_in(g, s)
                        if s == CONV_SLOTS and not last:
                            tap_params(g + 1)
                    if mult is not None:
                        square(before, mult)
                        scale_y(before, mult)
                    if s in ((10, 11) if first else (4, 5)):
                        if first:
                            act.wait_ge(cum_stored, 16)
                        load_cum(g, s % 2)
                    if START <= s:
                        k = s - START
                        exps(g, k)
                        if k < NT - 2:
                            load_cum(g, k + 2)
                        if k < MOVES:
                            b_tokens(g, k)
                        if k:
                            square(g, k - 1)
                            scale_y(g, k - 1)

            tap_params(0)
            for t in range(NT):
                high(2 * t)
                high(2 * t + 1)
                if t == 1:
                    act.wait_ge(small_loaded, 16)
                    act.activation(small_hi, small_raw, ACT.Copy).then_inc(small_step, 1)
                if t == NT - 2:
                    split_hi(0, 0)
            for q in range(SEQS):
                act.wait_ge(small_done, SEQS * (q + 1))
                act.activation(small[:, q * SEQ:(q + 1) * SEQ], core.bank[6 + q][0:SMALL, :], ACT.Copy).then_inc(small_copied, 1)
            groups(act, step)
            square(GROUPS - 1, NT - 1)
            scale_y(GROUPS - 1, NT - 1)

        @block.vector
        def _(dve):
            def split_lo(g, m):
                dve.wait_ge(w_hi_done, TILES * g + m + 1)
                need(dve, proj_done, SLOTS * g + 2 * (m - 1))
                dve.tensor_tensor(w_lo[m % 2][:, :, :], w_raw[:, m % 2, :, :], w_hi[m % 2][:, :, :].bitcast(F32),
                                  ALU.subtract).then_inc(w_split, 1)

            def conv(g, s):
                m = s // 2
                dve.wait_ge(tap_done, CONV_SLOTS * g + s + 1)
                for back in (1, 2, 3):
                    if back > 1:
                        dve.wait_ge(conv_step, 2 * (CONV_SLOTS * g + s) + back - 1)
                    dve.scalar_tensor_tensor(acc[:, s % 2, back:], bank_proj[s % 2][:, 0:SEQ - back],
                                             mix.conv_w[:, g, m, 3 - back:4 - back], acc[:, s % 2, back:],
                                             ALU.mult, ALU.add).then_inc(conv_taken if back == 3 else conv_step, 1)

            def silu(g, s):
                m, q = divmod(s, SEQS)
                dve.wait_ge(tanh_done, SLOTS * g + s + 1)
                if s == 0:
                    need(dve, started, NT * g)
                if m == CONV_TILES - 1:
                    need(dve, multiplied, NT * g)
                dve.scalar_tensor_tensor(xbc[:, m, q * SEQ:(q + 1) * SEQ], th[:, s % 2, :], 1.0, acc[:, s % 2, :],
                                         ALU.add, ALU.mult).then_inc(silu_done, 1)

            def gate_silu(g, s):
                v = s - CONV_SLOTS
                t, q = divmod(v, SEQS)
                dve.wait_ge(gate_taken, GATE_SLOTS * g + v + 1)
                dve.scalar_tensor_tensor(gate[:, t, q * SEQ:(q + 1) * SEQ], th[:, s % 2, :], 1.0,
                                         gate[:, t, q * SEQ:(q + 1) * SEQ], ALU.add, ALU.mult).then_inc(gate_done, 1)

            def diffs(g, k):
                dve.wait_ge(cum_loaded[k % 2], 16 * ((NT // 2) * g + k // 2 + 1))
                need(dve, multiplied, NT * g + k - 1)
                for h in range(HPG):
                    op = dve.tensor_scalar(attn[:, k % 2, h, :], cum_b[:, k % 2, h, :],
                                           mix.cum[:, chunk_tile(k), bass.ds(g * HPG + h, 1)], 0.0,
                                           ALU.subtract, ALU.min)
                op.then_inc(diff_done, 1)

            def after_start(g, k):
                dve.wait_ge(started, NT * g + k + 1)
                dve.tensor_tensor(bc[:, :], bank_bg[:, P:2 * P], core.causal[:, :], ALU.mult).then_inc(bc_done, 1)
                need(dve, multiplied, NT * g + k - 1)
                dve.tensor_tensor(heads(dtx[:, k % 2, :]), heads(bank_x[:, :]), per_head(mix.dt, k, g),
                                  ALU.mult).then_inc(dtx_done, 1)
                dve.wait_ge(exp_done, NT * g + k + 1)
                dve.wait_ge(bc_done, NT * g + k + 1)
                dve.tensor_tensor(attn[:, k % 2, :, :], attn[:, k % 2, :, :],
                                  bc[:, :].unsqueeze(1).to_broadcast([P, HPG, P]), ALU.mult).then_inc(attn_done, 1)
                dve.tensor_tensor(heads(dx[:, :]), heads(bank_x[:, :]),
                                  mix.d_all[:, bass.ds(g * HPG, HPG)].unsqueeze(2).to_broadcast([P, HPG, HD]),
                                  ALU.mult).then_inc(dx_done, 1)

            def after_mult(g, k):
                dve.wait_ge(multiplied, NT * g + k + 1)
                need(dve, yn_done, NT * g + k - 1)
                yk = y[:, k % 2, :]
                if k < SEQS:
                    dve.wait_ge(dx_done, NT * g + k + 1)
                    dve.tensor_tensor(yk, bank_y[:, :], dx[:, :], ALU.add).then_inc(y_done, 1)
                    dve.tensor_copy(state[:, k % 2, :], bank_state[:, :]).then_inc(state_done, 1)
                    return
                at = 2 * (MOVES * g + k - SEQS)
                dve.tensor_tensor(heads(inter[:, :]), heads(bank_inter[:, :]), per_head(mix.exp_cum, k, g),
                                  ALU.mult).then_inc(inter_step, 1)
                if k < MOVES:
                    dve.wait_ge(state_done, MOVES * g + k - SEQS + 1)
                    dve.tensor_tensor(heads(state[:, k % 2, :]), heads(state[:, k % 2, :]), per_head(mix.exp_last, k, g),
                                      ALU.mult).then_inc(state_step, 1)
                dve.wait_ge(inter_step, at + 1)
                dve.tensor_tensor(inter[:, :], inter[:, :], bank_y[:, :], ALU.add).then_inc(inter_step, 1)
                if k < MOVES:
                    dve.wait_ge(state_step, (MOVES - SEQS) * g + k - SEQS + 1)
                    dve.tensor_tensor(state[:, k % 2, :], state[:, k % 2, :], bank_state[:, :],
                                      ALU.add).then_inc(state_done, 1)
                dve.wait_ge(inter_step, at + 2)
                dve.wait_ge(dx_done, NT * g + k + 1)
                dve.tensor_tensor(yk, inter[:, :], dx[:, :], ALU.add).then_inc(y_done, 1)

            def gate_y(g, k):
                t = chunk_tile(k)
                dve.wait_ge(y_turned, NT * g + k + 1)
                dve.wait_ge(gate_done, GATE_SLOTS * (g + 1))
                need(dve, stored[k % 2], 16 * ((NT // 2) * g + k // 2))
                dve.tensor_tensor(yg[:, k % 2, :, :], bank_turn[:, :].rearrange("p (k i) -> p k i", i=P),
                                  gate[:, :, t * P:(t + 1) * P], ALU.mult).then_inc(gated, 1)

            def low(n):
                t, h = divmod(n, 2)
                dve.wait_ge(hi_done, n + 1)
                dve.tensor_tensor(mix.x_lo[:, 4 * h:4 * h + 4, t * P:(t + 1) * P],
                                  core.bank[2 + n % 4][:, :].rearrange("p (k c) -> p k c", c=P),
                                  mix.x_hi[:, 4 * h:4 * h + 4, t * P:(t + 1) * P].bitcast(F32),
                                  ALU.subtract).then_inc(lo_done, 1)

            def front():
                for t in range(NT):
                    dve.wait_ge(x_loaded[t % XT], 16 * (t // XT + 1))
                    for h in range(2):
                        dve.bn_stats(stats[:, t % 2, h, :], xt[:, t % XT, h * 512:(h + 1) * 512]).then_inc(bn_step, 1)
                    dve.wait_ge(bn_step, 2 * t + 2)
                    dve.bn_aggr(mv[:, t, :], stats[:, t % 2, :, :]).then_inc(aggr_done, 1)
                    if t:
                        low(2 * t - 2)
                        low(2 * t - 1)
                    if t == 2:
                        dve.wait_ge(small_step, 1)
                        dve.tensor_tensor(small_lo, small_raw, small_hi.bitcast(F32), ALU.subtract).then_inc(small_step, 1)
                    dve.wait_ge(ln_rstd_done, t + 1)
                    dve.wait_ge(aggr_done, t + 1)
                    dve.tensor_scalar(xt[:, t % XT, :], xt[:, t % XT, :], mv[:, t, 0:1],
                                      core.rstd[:, half * NT + t:half * NT + t + 1],
                                      ALU.subtract, ALU.mult).then_inc(xn_done, 1)
                low(2 * NT - 2)
                low(2 * NT - 1)
                dve.tensor_copy(core.mean[:, half * NT:(half + 1) * NT], mv[:, :, 0])

            def over_tiles(row, n):
                return row.unsqueeze(1).to_broadcast([P, NT // 2, n])

            def early(s):
                if s == 1:
                    dve.wait_ge(rows_loaded, 32)
                    for i, b in enumerate((bank_x, bank_bg)):
                        part = b[:, 0:4 * SMALL].rearrange("p (t c) -> p t c", c=SMALL)
                        tiles = slice(4 * i, 4 * i + 4)
                        dve.wait_ge(to_tokens, i + 1)
                        dve.tensor_tensor(z[:, tiles, :], part[:, :, 0:HEADS], over_tiles(dt_bias, HEADS),
                                          ALU.add).then_inc(z_done, 1)
                        if i == 0:
                            dve.wait_ge(rms_step, 4)
                        dve.tensor_tensor(logits[:, tiles, :], part[:, :, HEADS:],
                                          rms[:, tiles].unsqueeze(2).to_broadcast([P, NT // 2, LG]),
                                          ALU.mult).then_inc(lg_step, 1)
                if s == 2:
                    dve.wait_ge(z_done, 2)
                    dve.tensor_scalar(mix.dt[:, :, :], z, 0.0, None, ALU.max).then_inc(dt_step, 1)
                    dve.wait_ge(lg_step, 2)
                    dve.tensor_tensor(logits, logits, base.unsqueeze(1).to_broadcast([P, NT, LG]),
                                      ALU.add).then_inc(lg_step, 1)
                    dve.wait_ge(lg_step, 3)
                    two = logits[:, :, STREAMS * STREAMS:].rearrange("p t (w s) -> p t w s", s=STREAMS)
                    dve.tensor_copy(core.res_logits[:, half * NT:(half + 1) * NT, :], logits[:, :, 0:STREAMS * STREAMS])
                    dve.tensor_reduce(sm_max, two, AX.X, ALU.max).then_inc(lg_step, 1)
                    dve.wait_ge(lg_step, 4)
                    dve.tensor_tensor(sm, two, sm_max.unsqueeze(3).to_broadcast([P, NT, 2, STREAMS]),
                                      ALU.subtract).then_inc(lg_step, 2)
                if s == 3:
                    dve.wait_ge(dt_step, 1)
                    dve.wait_ge(soft_step, 3)
                    dve.tensor_tensor(mix.dt[:, :, :], mix.dt[:, :, :], soft, ALU.add).then_inc(dt_step, 1)
                    dve.wait_ge(dt_step, 2)
                    dve.tensor_tensor(decays, mix.dt[:, :, :], mix.a_neg[:, :].unsqueeze(1).to_broadcast([P, NT, HEADS]),
                                      ALU.mult).then_inc(dt_step, 1)
                    dve.wait_ge(dt_step, 3)
                    dve.tensor_scalar(decays, decays, LOG_ZERO, None, ALU.max).then_inc(dt_step, 1)
                    dve.wait_ge(lg_exp, 1)
                    dve.tensor_reduce(sm_sum, sm, AX.X, ALU.add).then_inc(lg_step, 1)
                    dve.wait_ge(lg_step, 7)
                    dve.reciprocal(sm_sum, sm_sum).then_inc(lg_step, 1)
                    dve.wait_ge(lg_step, 8)
                    dve.tensor_tensor(sm, sm, sm_sum.unsqueeze(3).to_broadcast([P, NT, 2, STREAMS]),
                                      ALU.mult).then_inc(lg_step, 1)
                    dve.wait_ge(lg_step, 9)
                    dve.tensor_copy(core.h_post[:, half * NT:(half + 1) * NT, :], sm[:, :, 1, :])
                if s == 5:
                    dve.wait_ge(cum_copied, 2)
                    dve.tensor_tensor(mix.decay[:, :, :], bank_inter[:, :].rearrange("p (t h) -> p t h", h=HEADS),
                                      mix.cum[:, :, :], ALU.subtract).then_inc(decay_step, 1)
                t = s - 2
                if 0 <= t < NT:
                    dve.wait_ge(bx_loaded[t % 2], 16 * (t // 2 + 1))
                    dve.tensor_scalar(bx[t % 2], bx[t % 2], mv[:, t, 0:1],
                                      core.rstd[:, half * NT + t:half * NT + t + 1],
                                      ALU.subtract, ALU.mult).then_inc(bx_done, 1)
                if s == START:
                    for i in range(2):
                        dve.wait_ge(branch_stored[i], 16 * NT // 2)

            def step(g, first, last):
                for s in range(SLOTS):
                    before, mult, turn = tail_of(g, s, first)
                    if s % 2 == 0:
                        m = s // 2 + 1
                        if m < TILES:
                            split_lo(g, m)
                        elif not last:
                            split_lo(g + 1, 0)
                    if first:
                        early(s)
                    if s < CONV_SLOTS:
                        conv(g, s)
                        if s:
                            silu(g, s - 1)
                    else:
                        if s == CONV_SLOTS:
                            silu(g, s - 1)
                        gate_silu(g, s)
                    if mult is not None:
                        after_mult(before, mult)
                    if turn is not None:
                        gate_y(before, turn)
                    if START <= s:
                        k = s - START
                        diffs(g, k)
                        if k:
                            after_mult(g, k - 1)
                        after_start(g, k)

            front()
            split_lo(0, 0)
            groups(dve, step)
            after_mult(GROUPS - 1, NT - 1)
            for k in range(NT):
                gate_y(GROUPS - 1, k)

        @block.tensor
        def _(pe):
            def project(g, s):
                m, q = divmod(s, SEQS)
                pe.wait_ge(w_split, TILES * g + m + 1)
                if s < 2:
                    need(pe, gate_taken, GATE_SLOTS * (g - 1) + GATE_SLOTS - 1 + s)
                elif s < CONV_SLOTS + 2:
                    pe.wait_ge(conv_taken, CONV_SLOTS * g + s - 1)
                else:
                    pe.wait_ge(gate_taken, GATE_SLOTS * g + s - CONV_SLOTS - 1)
                out = bank_proj[s % 2][:, :]
                for k in range(KT):
                    hi = mix.x_hi[:, k, q * SEQ:(q + 1) * SEQ]
                    lo = mix.x_lo[:, k, q * SEQ:(q + 1) * SEQ]
                    pe.matmul(out, w_hi[m % 2][:, k, :], hi, start=(k == 0), stop=False)
                    pe.matmul(out, w_hi[m % 2][:, k, :], lo, start=False, stop=False)
                    mm = pe.matmul(out, w_lo[m % 2][:, k, :], hi, start=False, stop=(k == KT - 1))
                mm.then_inc(proj_done, 1)

            def start(g, k):
                t = chunk_tile(k)
                toks = slice(t * P, (t + 1) * P)
                pe.wait_ge(silu_done, CONV_SLOTS * (g + 1))
                need(pe, dx_done, NT * g + k)
                need(pe, bc_done, NT * g + k)
                need(pe, b_copied, MOVES * g + min(k, MOVES))
                for c in range(XT):
                    pe.transpose(bank_x[:, c * P:(c + 1) * P], xbc[:, c, toks], core.ident[:, :])
                pe.transpose(bank_bg[:, 0:P], xbc[:, XT, toks], core.ident[:, :])
                pe.matmul(bank_bg[:, P:2 * P], xbc[:, XT, toks], xbc[:, XT + 1, toks],
                          start=True, stop=True).then_inc(started, 1)

            def mult(g, k):
                t = chunk_tile(k)
                pe.wait_ge(attn_done, NT * g + k + 1)
                pe.wait_ge(dtx_done, NT * g + k + 1)
                need(pe, y_done, NT * g + k)
                need(pe, state_done, MOVES * g + min(k, MOVES))
                if k < MOVES:
                    pe.wait_ge(dec_done, MOVES * g + k + 1)
                    pe.wait_ge(b_copied, MOVES * g + k + 1)
                    pe.matmul(bank_state[:, :], b_tok[:, k % 2, :], dtx_dec[:, k % 2, :], start=True, stop=True)
                if k >= SEQS:
                    pe.matmul(bank_inter[:, :], xbc[:, XT + 1, t * P:(t + 1) * P], state[:, k % 2, :],
                              start=True, stop=True)
                for h in range(HPG):
                    mm = pe.matmul(bank_y[:, h * HD:(h + 1) * HD], attn[:, k % 2, h, :],
                                   dtx[:, k % 2, h * HD:(h + 1) * HD], start=True, stop=True)
                mm.then_inc(multiplied, 1)

            def turn(g, k):
                pe.wait_ge(yn_done, NT * g + k + 1)
                need(pe, gated, NT * g + k)
                for c in range(XT):
                    mm = pe.transpose(bank_turn[:, c * P:(c + 1) * P], yn[:, k, c * P:(c + 1) * P], core.ident[:, :])
                mm.then_inc(y_turned, 1)

            def front():
                pair = 2 * P

                def small_products(n):
                    pe.wait_ge(lo_done, 4 * n + 4)
                    pe.wait_ge(small_step, 2)
                    toks = slice(n * pair, (n + 1) * pair)
                    out = core.bank[6 + n // 2][0:SMALL, (n % 2) * pair:(n % 2 + 1) * pair]
                    for k in range(KT):
                        pe.matmul(out, small_hi[:, k, :], mix.x_hi[:, k, toks], start=(k == 0), stop=False)
                        pe.matmul(out, small_hi[:, k, :], mix.x_lo[:, k, toks], start=False, stop=False)
                        mm = pe.matmul(out, small_lo[:, k, :], mix.x_hi[:, k, toks], start=False, stop=(k == KT - 1))
                    mm.then_inc(small_done, 1)

                for n in range(2 * NT):
                    t, h = divmod(n, 2)
                    pe.wait_ge(xn_done, t + 1)
                    need(pe, lo_done, n - 3)
                    for k in range(4):
                        mm = pe.transpose(core.bank[2 + n % 4][:, k * P:(k + 1) * P],
                                          xt[:, t % XT, (4 * h + k) * P:(4 * h + k + 1) * P], core.ident[:, :])
                    mm.then_inc(turned, 1)
                    if n % 4 == 1 and n > 4:
                        small_products(n // 4 - 1)
                small_products(NT // 2 - 1)

            def early(s):
                if s == 0:
                    pe.wait_ge(small_copied, 2)
                    for i, b in enumerate((bank_x, bank_bg)):
                        for t in range(4 * i, 4 * i + 4):
                            mm = pe.transpose(b[:, (t % 4) * SMALL:(t % 4 + 1) * SMALL],
                                              small[:, t * P:(t + 1) * P], core.ident[0:SMALL, 0:SMALL])
                        mm.then_inc(to_tokens, 1)
                if s == 3:
                    pe.wait_ge(dt_step, 4)
                    pe.wait_ge(constants, 2)
                    pe.matmul(bank_y[:, :], core.causal[:, :], decays.rearrange("p t h -> p (t h)"),
                              start=True, stop=True).then_inc(summed, 1)
                    pe.matmul(bank_inter[:, :], ones, decays.rearrange("p t h -> p (t h)"),
                              start=True, stop=True).then_inc(summed, 1)
                if s == 5:
                    pe.wait_ge(cum_copied, 2)
                    for i in range(2):
                        for t in range(4 * i, 4 * i + 4):
                            mm = pe.transpose(core.bank[6 + i][0:HEADS, (t % 4) * P:(t % 4 + 1) * P], mix.cum[:, t, :],
                                              core.ident[:, :])
                        mm.then_inc(cum_turned, 1)
                t = s - EARLY_TURN
                if 0 <= t < NT:
                    if t == 0:
                        pe.wait_ge(branch_w_loaded, 16)
                    pe.wait_ge(mix_copied, t + 1)
                    need(pe, branch_copied, t)
                    for c in range(2):
                        mm = pe.matmul(bank_bg[:, 0:CW], mixed_t[t % 2][:, c * P:(c + 1) * P],
                                       w_branch[:, c, :], start=(c == 0), stop=(c == 1))
                    mm.then_inc(branch_done, 1)

            def turn_mixed(t):
                pe.wait_ge(mix_step, 3 * (t + 1))
                pe.wait_ge(lg_step, 2)
                need(pe, mix_copied, t)
                for c in range(2):
                    mm = pe.transpose(bank_x[:, c * P:(c + 1) * P], mixed[t % 2][:, c * P:(c + 1) * P], core.ident[:, :])
                mm.then_inc(mix_turned, 1)

            def step(g, first, last):
                for s in range(SLOTS):
                    before, mult_k, turn_k = tail_of(g, s, first)
                    if first and 0 <= s - EARLY_TURN < NT:
                        turn_mixed(s - EARLY_TURN)
                    project(g, s)
                    if first:
                        early(s)
                        if s == START:
                            pe.wait_ge(branch_copied, NT)
                    if mult_k is not None:
                        mult(before, mult_k)
                    if turn_k is not None:
                        turn(before, turn_k)
                    if START <= s:
                        k = s - START
                        if k:
                            mult(g, k - 1)
                        start(g, k)

            front()
            groups(pe, step)
            mult(GROUPS - 1, NT - 1)
            for k in range(NT):
                turn(GROUPS - 1, k)


def output_block(nc, core):
    d = core.dram
    bank = core.bank
    NS = STREAMS
    PASSES = 2 * HALVES
    ROWS = 2 * NT
    with ExitStack() as ctx:
        def sb(name, shape, dt=F32):
            return ctx.enter_context(nc.sbuf_tensor(name, shape, dt))

        def sem(name):
            return core.semaphore(name)

        y_raw = sb("y_raw", [P, 2, HALF])
        w_raw = sb("wo_raw", [P, 2, 512])
        y_hi = [sb(f"y_hi{i}", [P, HALF], F32R) for i in range(2)]
        y_lo = [sb(f"y_lo{i}", [P, HALF], F32R) for i in range(2)]
        w_hi = [sb(f"wo_hi{i}", [P, 512], F32R) for i in range(2)]
        w_lo = [sb(f"wo_lo{i}", [P, 512], F32R) for i in range(2)]
        s_sb = sb("s_sb", [P, NT, DM])
        sigm = sb("sigm", [P, 2])
        mat = sb("mat", [P, ROWS, NS, NS])
        mat_e = sb("mat_e", [P, ROWS, NS, NS])
        top = sb("top", [P, ROWS, NS])
        tot = sb("tot", [P, ROWS, NS])
        xq = sb("xq", [P, DM])
        post = sb("post", [P, NS])
        br = sb("br", [P, CW])
        xn = sb("xnq", [P, DM])
        f = sb("f", [P, DM])
        tf = sb("tf", [P, DM])
        o_sb = sb("o_sb", [P, DM])
        f_keep = sb("f_keep", [P, NT, 512])
        x_keep = sb("x_keep", [P, NT, 512])

        k_loaded = [sem("k_loaded0"), sem("k_loaded1")]
        k_hi, k_split, k_done = sem("k_hi"), sem("k_split"), sem("k_done")
        evacuated = [sem("evacuated_even"), sem("evacuated_odd")]
        sig_exp, sig_step = sem("sig_exp"), sem("sig_step")
        guard_step, guard_act, sk_step, res_step = sem("guard_step"), sem("guard_act"), sem("sk_step"), sem("res_step")
        tile_loaded, post_copied = sem("tile_loaded"), sem("post_copied")
        tile_xn, post_done, f_step, f_tanh, f_silu = (sem("tile_xn"), sem("post_done"), sem("f_step"), sem("f_tanh"),
                                                      sem("f_silu"))
        s_mul, x_kept, o_done, o_stored = sem("s_mul"), sem("x_kept"), sem("o_done"), sem("o_stored")
        o_loaded = sem("o_loaded")
        last_mul, last_done, last_stored = sem("last_mul"), sem("last_done"), [sem("last_stored0"), sem("last_stored1")]
        block = ctx.enter_context(nc.Block())

        TURNS = OT // 2 - 2
        SK_TURNS = (TURNS, (SINKHORN - 1) // 2 - TURNS)
        SK_AHEAD = SINKHORN - 1 - 2 * sum(SK_TURNS)

        def k_steps(eng, p, one, extra=None):
            n = SK_TURNS[p]
            if p == 0:
                one(p, 0, 0)
            one(p, 0, 1)
            with eng.Fori(1, 1 + n) as i:
                for j in range(2):
                    one(p, i, j)
                    if extra is not None:
                        extra(p, i - 1, j)
            if n < TURNS:
                with eng.Fori(1 + n, OT // 2 - 1) as i:
                    one(p, i, 0)
                    one(p, i, 1)
            one(p, OT // 2 - 1, 0)
            one(p, OT // 2 - 1, 1)
            one(p + 1, 0, 0)

        def tile_steps(eng, p, one, part):
            def turn(i, last):
                for q in range(4):
                    if not (last and q == 3):
                        one(p, 2 * i + (q + 1) // 2, (q + 1) % 2)
                    elif p + 1 < PASSES:
                        one(p + 1, 0, 0)
                    part((p - 2) * NT + i, i, p, q, last)

            with eng.Fori(0, NT - 1) as i:
                turn(i, False)
            turn(NT - 1, True)

        @block.sync
        def _(sp):
            def load(p, i, j):
                need(sp, k_split, OT * p + 2 * i + j - 1)
                sp.dma_start(y_raw[:, j, :], d["y"][p // 2, 2 * i + j]).then_inc(k_loaded[j], 16)
                sp.dma_start(w_raw[:, j, :], d["w_out"][p % 2, 2 * i + j]).then_inc(k_loaded[j], 16)

            for p in range(2):
                k_steps(sp, p, load)
            def load_tile(n, i, p):
                sp.dma_start(xq[:, :], d["x"][n]).then_inc(tile_loaded, 16)
                sp.dma_start(br[:, :], d["branch"][p - 2, :, i, :]).then_inc(tile_loaded, 16)

            def tile(n, i, p, q, last):
                if q == 1 and not (last and p == PASSES - 1):
                    sp.wait_ge(tile_xn, n + 1)
                    sp.wait_ge(post_done, NS * n + NS)
                    load_tile(n + 1, 0 if last else i + 1, p + 1 if last else p)

            load_tile(0, 0, 2)
            for p in range(2, PASSES):
                tile_steps(sp, p, load, tile)

        @block.gpsimd
        def _(pool):
            def tile(n, i, p, q, last):
                if q:
                    return
                pool.dma_start(o_sb[:, :], d["x"][n]).then_inc(o_loaded, 16)
                width = DM if p == 2 else 512
                pool.wait_ge(o_loaded, 16 * n + 16)
                if p == 3:
                    pool.tensor_copy(x_keep[:, i, :], o_sb[:, 512:]).then_inc(x_kept, 1)
                pool.wait_ge(s_mul, n + 1)
                pool.tensor_tensor(o_sb[:, 0:width], tf[:, 0:width], o_sb[:, 0:width], ALU.add).then_inc(o_done, 1)
                pool.wait_ge(o_done, n + 1)
                if p == 3:
                    pool.wait_ge(x_kept, i + 1)
                pool.nop(nofuse=True)
                pool.dma_start(d["out"][n][:, 0:width], o_sb[:, 0:width]).then_inc(o_stored, 16)
                pool.wait_ge(o_stored, 16 * n + 16)
                pool.nop(nofuse=True)

            for p in range(2, PASSES):
                tile_steps(pool, p, lambda p, i, j: None, tile)
            for t in range(NT):
                pool.wait_ge(last_mul, t + 1)
                pool.tensor_tensor(f_keep[:, t, :], f_keep[:, t, :], x_keep[:, t, :], ALU.add).then_inc(last_done, 1)
            pool.wait_ge(o_stored, 16 * ROWS)

        @block.scalar
        def _(act):
            def split_hi(p, i, j):
                kk = OT * p + 2 * i + j
                act.wait_ge(k_loaded[j], 32 * ((OT // 2) * p + i + 1))
                need(act, k_done, kk - 1)
                act.activation(y_hi[j][:, :], y_raw[:, j, :], ACT.Copy)
                act.activation(w_hi[j][:, :], w_raw[:, j, :], ACT.Copy).then_inc(k_hi, 1)

            def evacuate(p):
                act.wait_ge(k_done, OT * (p + 1))
                if p == 2:
                    act.wait_ge(s_mul, NT)
                for t in range(0, NT, 2):
                    act.activation(s_sb[:, t, (p % 2) * 512:(p % 2 + 1) * 512], bank[t][:, :],
                                   ACT.Copy).then_inc(evacuated[0], 1)

            def tile(n, i, p, q, last):
                if q == 0:
                    act.activation(post[:, :], core.h_post[:, n, :], ACT.Copy).then_inc(post_copied, 1)
                    act.wait_ge(post_copied, n + 1)
                    act.wait_ge(tile_loaded, 32 * n + 32)
                    for s in range(NS):
                        act.activation(f[:, s * CW:(s + 1) * CW], br[:, :], ACT.Copy,
                                       scale=post[:, s:s + 1]).then_inc(post_done, 1)
                if q == 1:
                    act.wait_ge(o_loaded, 16 * n + 16)
                    act.wait_ge(f_step, NS * NS * (n + 1))
                    act.activation(tf[:, :], f[:, :], ACT.Tanh, scale=0.5).then_inc(f_tanh, 1)
                if q == 3:
                    act.wait_ge(f_silu, n + 1)

            act.activation(sigm[:, 0:1], core.gate_value[:, 0:1], ACT.Exp, scale=-1.0).then_inc(sig_exp, 1)
            act.wait_ge(guard_step, 3)
            act.activation(mat_e[:, :, :, :], mat[:, :, :, :], ACT.Exp).then_inc(guard_act, 1)
            act.wait_ge(guard_step, 4)
            act.activation(tot[:, :, :], tot[:, :, :], ACT.Ln).then_inc(guard_act, 1)
            act.wait_ge(guard_step, 7)
            act.activation(mat[:, :, :, :], mat[:, :, :, :], ACT.Exp).then_inc(guard_act, 1)
            for p in range(2):
                k_steps(act, p, split_hi)
                evacuate(p)
            tile_steps(act, 2, split_hi, tile)
            evacuate(2)
            tile_steps(act, 3, split_hi, tile)
            for t in range(NT):
                act.wait_ge(last_done, t + 1)
                act.dma_start(d["out"][NT + t][:, 512:], f_keep[:, t, :]).then_inc(last_stored[t % 2], 16)
            for i in range(2):
                act.wait_ge(last_stored[i], 16 * NT // 2)

        @block.vector
        def _(dve):
            def split_lo(p, i, j):
                kk = OT * p + 2 * i + j
                dve.wait_ge(k_hi, kk + 1)
                need(dve, k_done, kk - 1)
                dve.tensor_tensor(y_lo[j][:, :], y_raw[:, j, :], y_hi[j][:, :].bitcast(F32), ALU.subtract)
                dve.tensor_tensor(w_lo[j][:, :], w_raw[:, j, :], w_hi[j][:, :].bitcast(F32), ALU.subtract).then_inc(k_split, 1)

            def over_rows(a):
                return a.unsqueeze(3).to_broadcast([P, ROWS, NS, NS])

            def over_columns(a):
                return a.unsqueeze(2).to_broadcast([P, ROWS, NS, NS])

            by_row = mat[:, :, :, :]
            by_column = mat[:, :, :, :].rearrange("p t i j -> p t j i")

            def guarded():
                dve.tensor_reduce(top[:, :, :], by_row, AX.X, ALU.max).then_inc(guard_step, 1)
                dve.wait_ge(guard_step, 2)
                dve.tensor_tensor(by_row, by_row, over_rows(top[:, :, :]), ALU.subtract).then_inc(guard_step, 1)
                dve.wait_ge(guard_act, 1)
                dve.tensor_reduce(tot[:, :, :], mat_e[:, :, :, :], AX.X, ALU.add).then_inc(guard_step, 1)
                dve.wait_ge(guard_act, 2)
                dve.tensor_tensor(by_row, by_row, over_rows(tot[:, :, :]), ALU.subtract).then_inc(guard_step, 1)
                dve.wait_ge(guard_step, 5)
                dve.tensor_reduce(top[:, :, :], by_column, AX.X, ALU.max).then_inc(guard_step, 1)
                dve.wait_ge(guard_step, 6)
                dve.tensor_tensor(by_row, by_row, over_columns(top[:, :, :]), ALU.subtract).then_inc(guard_step, 1)
                dve.wait_ge(guard_act, 3)
                dve.tensor_reduce(tot[:, :, :], by_column, AX.X, ALU.add).then_inc(guard_step, 1)
                dve.wait_ge(guard_step, 8)
                dve.reciprocal(tot[:, :, :], tot[:, :, :]).then_inc(guard_step, 1)
                dve.wait_ge(guard_step, 9)
                dve.tensor_tensor(by_row, by_row, over_columns(tot[:, :, :]), ALU.mult).then_inc(guard_step, 1)
                dve.wait_ge(guard_step, 10)

            def iterate(n):
                for side, view, over in ((0, by_row, over_rows), (1, by_column, over_columns)):
                    at = 3 * (2 * n + side)
                    if not (isinstance(at, int) and at == 0):
                        dve.wait_ge(sk_step, at)
                    dve.tensor_reduce(tot[:, :, :], view, AX.X, ALU.add).then_inc(sk_step, 1)
                    dve.wait_ge(sk_step, at + 1)
                    dve.reciprocal(tot[:, :, :], tot[:, :, :]).then_inc(sk_step, 1)
                    dve.wait_ge(sk_step, at + 2)
                    dve.tensor_tensor(by_row, by_row, over(tot[:, :, :]), ALU.mult).then_inc(sk_step, 1)

            def extra(p, i, j):
                iterate(SK_AHEAD + 2 * (p * SK_TURNS[0]) + 2 * i + j)

            def evacuate(p):
                dve.wait_ge(k_done, OT * (p + 1))
                if p == 2:
                    dve.wait_ge(s_mul, NT)
                for t in range(1, NT, 2):
                    dve.tensor_copy(s_sb[:, t, (p % 2) * 512:(p % 2 + 1) * 512], bank[t][:, :]).then_inc(evacuated[1], 1)

            def tile(n, i, p, q, last):
                if q == 0:
                    dve.wait_ge(tile_loaded, 32 * n + 32)
                    dve.tensor_scalar(xn[:, :], xq[:, :], core.mean[:, bass.ds(n, 1)], core.rstd[:, bass.ds(n, 1)],
                                      ALU.subtract, ALU.mult).then_inc(tile_xn, 1)
                    dve.wait_ge(tile_xn, n + 1)
                    dve.wait_ge(post_done, NS * n + NS)
                if q < 2:
                    for c in (2 * q, 2 * q + 1):
                        for r in range(NS):
                            if c:
                                dve.wait_ge(f_step, NS * NS * n + NS * (c - 1) + r + 1)
                            out = f[:, r * CW:(r + 1) * CW]
                            dve.scalar_tensor_tensor(out, xn[:, c * CW:(c + 1) * CW], mat[:, n, r, c:c + 1], out,
                                                     ALU.mult, ALU.add).then_inc(f_step, 1)
                if q == 2:
                    dve.wait_ge(f_tanh, n + 1)
                    dve.scalar_tensor_tensor(tf[:, :], tf[:, :], 1.0, f[:, :], ALU.add, ALU.mult).then_inc(f_silu, 1)
                if q == 3:
                    dve.wait_ge(f_silu, n + 1)
                    if p == 2:
                        dve.scalar_tensor_tensor(tf[:, :], tf[:, :], 0.5, s_sb[:, i, :], ALU.mult,
                                                 ALU.mult).then_inc(s_mul, 1)
                    else:
                        dve.tensor_scalar(f_keep[:, i, :], tf[:, 512:], 0.5, None, ALU.mult)
                        dve.scalar_tensor_tensor(tf[:, 0:512], tf[:, 0:512], 0.5, s_sb[:, i, 0:512], ALU.mult,
                                                 ALU.mult).then_inc(s_mul, 1)

            dve.wait_ge(sig_exp, 1)
            dve.tensor_scalar(sigm[:, 0:1], sigm[:, 0:1], 1.0, None, ALU.add).then_inc(sig_step, 1)
            dve.tensor_scalar(mat[:, :, :, :], core.res_logits[:, :, :].rearrange("p t (i j) -> p t i j", j=NS),
                              1.0 / TAU, None, ALU.mult).then_inc(guard_step, 1)
            dve.wait_ge(sig_step, 1)
            dve.reciprocal(sigm[:, 0:1], sigm[:, 0:1]).then_inc(sig_step, 1)
            dve.wait_ge(sig_step, 2)
            dve.tensor_scalar(sigm[:, 1:2], sigm[:, 0:1], -1.0, 1.0, ALU.mult, ALU.add).then_inc(sig_step, 1)
            dve.wait_ge(guard_step, 1)
            guarded()
            for n in range(SK_AHEAD):
                iterate(n)
            for p in range(2):
                k_steps(dve, p, split_lo, extra)
                evacuate(p)
            dve.wait_ge(sk_step, 6 * (SINKHORN - 1))
            dve.wait_ge(sig_step, 3)
            dve.tensor_scalar(by_row, by_row, sigm[:, 0:1], None, ALU.mult).then_inc(res_step, 1)
            dve.wait_ge(res_step, 1)
            diag = mat[:, :, :, :].rearrange("p t i j -> p t (i j)")[:, :, 0::NS + 1]
            dve.tensor_scalar(diag, diag, sigm[:, 1:2], None, ALU.add).then_inc(res_step, 1)
            dve.wait_ge(res_step, 2)
            dve.wait_ge(evacuated[0], NT)
            dve.wait_ge(evacuated[1], NT)
            tile_steps(dve, 2, split_lo, tile)
            evacuate(2)
            dve.wait_ge(evacuated[0], 3 * NT // 2)
            dve.wait_ge(evacuated[1], 3 * NT // 2)
            tile_steps(dve, 3, split_lo, tile)
            dve.wait_ge(k_done, OT * PASSES)
            dve.wait_ge(s_mul, ROWS)
            for t in range(NT):
                dve.tensor_tensor(f_keep[:, t, :], f_keep[:, t, :], bank[t][:, :], ALU.mult).then_inc(last_mul, 1)

        @block.tensor
        def _(pe):
            def products(p, i, j, first=False, last=False):
                pe.wait_ge(k_split, OT * p + 2 * i + j + 1)
                for t in range(NT):
                    if first and p:
                        pe.wait_ge(evacuated[t % 2], NT // 2 * (p - 1) + t // 2 + 1)
                    toks = slice(t * P, (t + 1) * P)
                    pe.matmul(bank[t][:, :], y_hi[j][:, toks], w_hi[j][:, :], start=first, stop=False)
                    pe.matmul(bank[t][:, :], y_hi[j][:, toks], w_lo[j][:, :], start=False, stop=False)
                    mm = pe.matmul(bank[t][:, :], y_lo[j][:, toks], w_hi[j][:, :], start=False, stop=last)
                mm.then_inc(k_done, 1)

            for p in range(PASSES):
                products(p, 0, 0, first=True)
                products(p, 0, 1)
                with pe.Fori(1, OT // 2 - 1) as i:
                    products(p, i, 0)
                    products(p, i, 1)
                products(p, OT // 2 - 1, 0)
                products(p, OT // 2 - 1, 1, last=True)


def program(nc, x, w_in, w_small, conv_w, norm_w, D, dt_bias, A_log, base, w_branch, gate, w_out, out):
    def scratch(name, shape):
        return nc.dram_tensor(name, shape, F32, kind="Internal").ap()

    dram = dict(x=x, w_in=w_in, w_small=w_small, conv_w=conv_w, norm_w=norm_w, D=D, dt_bias=dt_bias,
                A_log=A_log, base=base, w_branch=w_branch, gate=gate, w_out=w_out, out=out,
                cum=scratch("cum_scratch", (HALVES, NT, HEADS, P)),
                y=scratch("y_scratch", (HALVES, OT, P, HALF)), branch=scratch("branch_scratch", (HALVES, P, NT, CW)))
    with ExitStack() as ctx:
        core = Core(nc, ctx, dram)
        with ExitStack() as inner:
            mix = Mixer(nc, inner)
            setup_block(nc, core, mix)
            core.end_phase()
            for half in range(HALVES):
                mixer_block(nc, core, mix, half)
                core.end_phase()
        output_block(nc, core)


def kernel(**inputs):
    import numpy as _np
    import concourse.bacc as _bacc
    from concourse.bass_utils import run_bass_kernel_spmd as _run

    a = {n.replace("L0_attn_", "").replace("L0_ffn_", "f_"): _np.asarray(v) for n, v in inputs.items()}
    gn = GROUPS * P
    wi = a["in_proj_w"]

    def tiles(w):
        n = w.shape[0] // (GROUPS * P)
        return w.reshape(GROUPS, n, P, KT, P).transpose(0, 1, 4, 3, 2)

    w_in = _np.concatenate([tiles(wi[INNER:2 * INNER]), tiles(wi[2 * INNER:2 * INNER + gn]),
                            tiles(wi[2 * INNER + gn:2 * INNER + 2 * gn]), tiles(wi[0:INNER])], axis=1)

    def channels(v):
        rest = v.shape[1:]
        parts = [v[0:INNER].reshape(GROUPS, XT, P, *rest), v[INNER:INNER + gn].reshape(GROUPS, 1, P, *rest),
                 v[INNER + gn:].reshape(GROUPS, 1, P, *rest)]
        return _np.moveaxis(_np.concatenate(parts, axis=1), 2, 0)

    small = _np.concatenate([wi[2 * INNER + 2 * gn:], a["f_W_res"], a["f_W_pre"], a["f_W_post"]], axis=0)
    arrays = {
        "x": a["hidden_states"].reshape(2 * NT, P, DM),
        "w_in": w_in,
        "w_small": small.reshape(SMALL, KT, P).transpose(2, 1, 0),
        "conv_w": channels(_np.concatenate([a["conv_weight"], a["conv_bias"][:, None]], axis=1)),
        "norm_w": a["norm_weight"].reshape(GROUPS, XT, P).transpose(2, 0, 1),
        "D": a["D"],
        "dt_bias": a["dt_bias"],
        "A_log": a["A_log"],
        "base": _np.concatenate([a["f_H_res_base"].reshape(-1), a["f_H_pre_base"], a["f_H_post_base"]]),
        "w_branch": a["f_W_branch"].reshape(2, P, CW).transpose(1, 0, 2),
        "gate": a["f_gate"],
        "w_out": a["out_proj_w"].reshape(2, 512, OT, P).transpose(0, 2, 3, 1),
    }
    arrays = {n: _np.ascontiguousarray(v) for n, v in arrays.items()}
    nc = _bacc.Bacc("TRN2", target_bir_lowering=False, num_devices=1)
    args = {n: nc.dram_tensor(f"in_{n}", v.shape, mybir.dt.from_np(v.dtype), kind="ExternalInput").ap()
            for n, v in arrays.items()}
    args["out"] = nc.dram_tensor("out", (2 * NT, P, DM), F32, kind="ExternalOutput").ap()
    program(nc, **args)
    r = _run(nc, [{f"in_{n}": v for n, v in arrays.items()}], core_ids=[0])
    return r.results[0]["out"].reshape(4, SEQ, DM)
```

```python
from contextlib import ExitStack

import concourse.bass as bass
from concourse import mybir

F32 = mybir.dt.float32
F32R = mybir.dt.float32r
ALU = mybir.AluOpType
ACT = mybir.ActivationFunctionType
AX = mybir.AxisListType

P = 128
TOKENS, DM = 2048, 1024
SEQ = 512
HALF = 1024
HALVES = TOKENS // HALF
SEQS = HALF // SEQ
NT = HALF // P
CHUNKS = SEQ // P
KT = DM // P
HEADS, HD, GROUPS = 64, 64, 8
HPG = HEADS // GROUPS
GC = HPG * HD
XT = GC // P
INNER = HEADS * HD
CONV_TILES = XT + 2
TILES = CONV_TILES + XT
SLOTS = TILES * SEQS
CONV_SLOTS = CONV_TILES * SEQS
GATE_SLOTS = XT * SEQS
OT = INNER // P
STREAMS, CW = 4, 256
SMALL = HEADS + STREAMS * STREAMS + 2 * STREAMS
LN_EPS, NORM_EPS, RMS_EPS = 1e-5, 1e-5, 1.1920929e-07
TAU = 0.1
SINKHORN = 50
LOG_ZERO = -110.0


def need(eng, sem, value):
    if isinstance(value, int) and value <= 0:
        return
    eng.wait_ge(sem, value)


def chunk_tile(k):
    return CHUNKS * (k % SEQS) + k // SEQS


class Core:

    def __init__(self, nc, ctx, dram):
        self.nc, self.dram = nc, dram
        self.phase_sems = []

        def sb(name, shape, dt=F32):
            return ctx.enter_context(nc.sbuf_tensor(name, shape, dt))

        self.bank = [ctx.enter_context(nc.psum_tensor(f"bank{i}", [P, 512], F32)) for i in range(8)]
        self.ident = sb("ident", [P, P])
        self.causal = sb("causal", [P, P])
        self.neg_half = sb("neg_half", [P, NT])
        self.mean = sb("mean", [P, 2 * NT])
        self.rstd = sb("rstd", [P, 2 * NT])
        self.res_logits = sb("res_logits", [P, 2 * NT, STREAMS * STREAMS])
        self.h_post = sb("h_post", [P, 2 * NT, STREAMS])
        self.gate_value = sb("gate_value", [P, 1])

    def semaphore(self, name):
        self.phase_sems.append(self.nc.alloc_semaphore(name=name))
        return self.phase_sems[-1]

    def end_phase(self):
        self.nc.all_engine_barrier()
        self.nc.clear_and_free_semaphores(self.phase_sems)
        self.phase_sems = []
        self.nc.all_engine_barrier()


def prefetch_x(sp, d, mix, half, loaded):
    for t in range(XT):
        sp.dma_start(mix.xbc[:, t, :], d["x"][half * NT + t]).then_inc(loaded, 16)


class Mixer:

    def __init__(self, nc, ctx):
        def sb(name, shape, dt=F32):
            return ctx.enter_context(nc.sbuf_tensor(name, shape, dt))

        self.conv_w = sb("conv_w", [P, GROUPS, CONV_TILES, 5])
        self.norm_w = sb("norm_w", [P, GROUPS, XT])
        self.d_all = sb("d_all", [P, HEADS])
        self.a_neg = sb("a_neg", [P, HEADS])
        self.x_hi = sb("x_hi", [P, KT, HALF], F32R)
        self.x_lo = sb("x_lo", [P, KT, HALF], F32R)
        self.xbc = sb("xbc", [P, CONV_TILES, HALF])
        self.dt = sb("dt", [P, NT, HEADS])
        self.cum = sb("cum", [P, NT, HEADS])
        self.exp_cum = sb("exp_cum", [P, NT, HEADS])
        self.decay = sb("decay", [P, NT, HEADS])
        self.exp_last = sb("exp_last", [P, NT, HEADS])


START = CONV_SLOTS
MULT = CONV_SLOTS + 1
TURN = SLOTS
DRAIN = 2
FILL = {2 * NT - 5: (0, 4), 2 * NT: (4, KT)}
EARLY_TURN = 4


def mixer_block(nc, core, mix, half):
    d = core.dram
    bank_proj = core.bank[0:2]
    bank_x, bank_bg, bank_y, bank_inter, bank_state, bank_turn = core.bank[2:8]
    with ExitStack() as ctx:
        def sb(name, shape, dt=F32):
            return ctx.enter_context(nc.sbuf_tensor(f"{name}_{half}", shape, dt))

        def sem(name):
            return core.semaphore(f"{name}_{half}")

        w_raw = sb("w_raw", [P, 2, KT, P])
        w_hi = [sb(f"w_hi{i}", [P, KT, P], F32R) for i in range(2)]
        w_lo = [sb(f"w_lo{i}", [P, KT, P], F32R) for i in range(2)]
        acc = sb("acc", [P, 2, SEQ])
        th = sb("th", [P, 2, SEQ])
        tap_par = sb("tap_par", [P, CONV_TILES, 2])
        xbc = mix.xbc
        gate = sb("gate", [P, XT, HALF])
        cum_b = sb("cum_b", [P, 2, HPG, P])
        attn = sb("attn", [P, 2, HPG, P])
        bc = sb("bc", [P, P])
        b_tok = sb("b_tok", [P, P])
        b_hi, b_lo = sb("b_hi", [P, P], F32R), sb("b_lo", [P, P], F32R)
        dec_hi, dec_lo = sb("dec_hi", [P, GC], F32R), sb("dec_lo", [P, GC], F32R)
        dtx = sb("dtx", [P, 2, GC])
        dtx_dec = sb("dtx_dec", [P, GC])
        dx = sb("dx", [P, GC])
        state = sb("state", [P, SEQS, GC])
        c_hi, c_lo = sb("c_hi", [P, P], F32R), sb("c_lo", [P, P], F32R)
        st_hi, st_lo = sb("st_hi", [P, GC], F32R), sb("st_lo", [P, GC], F32R)
        y = sb("y", [P, GC])
        ssq = sb("ssq", [P, 2])
        var_eps = sb("nvar", [P, 2])
        eps = sb("eps", [P, 1])
        rstd = sb("nrstd", [P, 2])
        yn = sb("yn", [P, NT, GC])
        rows = sb("rows", [P, SMALL + 24])
        mv = sb("mv", [P, NT, 2])
        lv = sb("lv", [P, NT])
        rms = sb("rms", [P, NT])

        def flat(t):
            return t[:, :, :].rearrange("p a b -> p (a b)")

        xt = xbc[:, 0:XT, :]
        small_raw = xbc[:, XT, 0:KT * SMALL].rearrange("p (k c) -> p k c", c=SMALL)
        small_hi, small_lo = w_hi[1][:, :, 0:SMALL], w_lo[1][:, :, 0:SMALL]
        small = flat(yn)[0:SMALL, 0:HALF]
        bx = [flat(yn)[:, DM * (1 + i):DM * (2 + i)] for i in range(2)]
        mixed = [flat(yn)[:, 3 * DM + CW * i:3 * DM + CW * (i + 1)] for i in range(2)]
        mixed_t = [flat(yn)[:, 3 * DM + CW * (2 + i):3 * DM + CW * (3 + i)] for i in range(2)]
        branch = [dtx[:, 0, CW * i:CW * (i + 1)] for i in range(2)]
        w_branch = dtx[:, 1, :].rearrange("p (k c) -> p k c", c=CW)
        decays = attn[:, 0, 0:4, :].rearrange("p a b -> p (a b)").rearrange("p (t h) -> p t h", h=HEADS)
        z = attn[:, 0, 4:8, :].rearrange("p a b -> p (a b)").rearrange("p (t h) -> p t h", h=HEADS)
        soft = attn[:, 1, 0:4, :].rearrange("p a b -> p (a b)").rearrange("p (t h) -> p t h", h=HEADS)
        cum_hm = cum_b[0:HEADS, 0, :, :].rearrange("p h i -> p (h i)")
        ones = dx[:, 0:P]
        LG = SMALL - HEADS
        dt_bias, base = rows[:, 0:HEADS], rows[:, HEADS:SMALL]
        stats = rows[:, SMALL:].rearrange("p (a b c) -> p a b c", a=2, b=2)
        logits = y[:, 0:NT * LG].rearrange("p (t c) -> p t c", c=LG)
        sm = y[:, 192:192 + NT * 2 * STREAMS].rearrange("p (t w s) -> p t w s", w=2, s=STREAMS)
        sm_max = y[:, 256:256 + NT * 2].rearrange("p (t w) -> p t w", w=2)
        sm_sum = y[:, 272:272 + NT * 2].rearrange("p (t w) -> p t w", w=2)

        x_loaded = [sem(f"x_loaded{t}") for t in range(XT)]
        small_loaded, rows_loaded, branch_w_loaded = sem("small_loaded"), sem("rows_loaded"), sem("branch_w_loaded")
        bx_loaded = [sem("bx_loaded0"), sem("bx_loaded1")]
        bn_step, aggr_done, lv_done, ln_rstd_done = sem("bn_step"), sem("aggr_done"), sem("lv_done"), sem("ln_rstd_done")
        xn_done, turned, hi_done, lo_done = sem("xn_done"), sem("turned"), sem("hi_done"), sem("lo_done")
        small_step, small_done, small_copied = sem("small_step"), sem("small_done"), sem("small_copied")
        rms_step, to_tokens, z_done, soft_step, dt_step = (sem("rms_step"), sem("to_tokens"), sem("z_done"),
                                                           sem("soft_step"), sem("dt_step"))
        summed, cum_copied, decay_step = sem("summed"), sem("cum_copied"), sem("decay_step")
        cum_turned, cum_hm_copied, cum_stored = sem("cum_turned"), sem("cum_hm_copied"), sem("cum_stored")
        lg_step, lg_exp = sem("lg_step"), sem("lg_exp")
        bx_done, mix_step, mix_turned, mix_copied = sem("bx_done"), sem("mix_step"), sem("mix_turned"), sem("mix_copied")
        branch_done, branch_copied = sem("branch_done"), sem("branch_copied")
        branch_stored = [sem("branch_stored0"), sem("branch_stored1")]
        w_loaded = [sem("w_loaded0"), sem("w_loaded1")]
        w_hi_done, w_split = sem("w_hi_done"), sem("w_split")
        proj_done, conv_taken, gate_taken = sem("proj_done"), sem("conv_taken"), sem("gate_taken")
        tap_done, conv_step, tanh_done, silu_done = sem("tap_done"), sem("conv_step"), sem("tanh_done"), sem("silu_done")
        gate_done = sem("gate_done")
        cum_loaded = [sem("cum_loaded0"), sem("cum_loaded1")]
        diff_done, exp_done, bc_done, dtx_done = sem("diff_done"), sem("exp_done"), sem("bc_done"), sem("dtx_done")
        dx_done, b_copied, dec_done, attn_done = sem("dx_done"), sem("b_copied"), sem("dec_done"), sem("attn_done")
        started, multiplied, y_turned = sem("started"), sem("multiplied"), sem("y_turned")
        inter_step, y_done, state_step, state_done = sem("inter_step"), sem("y_done"), sem("state_step"), sem("state_done")
        squared, nvar_done, rstd_done, yn_done = sem("squared"), sem("nvar_done"), sem("nrstd_done"), sem("yn_done")
        gated = sem("gated")
        inter_hi, inter_lo = sem("inter_hi"), sem("inter_lo")
        dec_high, dec_low = sem("dec_high"), sem("dec_low")
        stored = [sem("stored0"), sem("stored1")]
        x_ahead = sem("x_ahead")
        params_loaded, masks, params_done, a_exp = sem("params_loaded"), sem("masks"), sem("params_done"), sem("a_exp")
        first_half = half == 0
        x_here = 16 if first_half else 0
        constants, tap_ready = sem("constants"), sem("tap_ready")
        block = ctx.enter_context(nc.Block())

        MOVES = NT - SEQS

        def heads(ap):
            return ap.rearrange("p (h c) -> p h c", c=HD)

        def turn_bank(k, drain):
            return bank_proj[0] if drain and k % 2 else bank_turn

        def per_head(table, k, g):
            return table[:, chunk_tile(k), bass.ds(g * HPG, HPG)].unsqueeze(2).to_broadcast([P, HPG, HD])

        def groups(eng, step):
            step(0, True, False)
            step(1, False, False)
            with eng.Fori(2, GROUPS - 1) as g:
                step(g, False, False)
            step(GROUPS - 1, False, True)

        def tail_of(g, s, first):
            if first:
                return None, None, None
            return g - 1, (NT - 1 if s == MULT + NT - 1 - SLOTS else None), (s if s < NT else None)

        @block.sync
        def _(sp):
            def load_w(g, m):
                n = TILES * g + m
                need(sp, w_split, n - 1)
                sp.dma_start(w_raw[:, m % 2, :, :], d["w_in"][g, m]).then_inc(w_loaded[m % 2], 16)

            def store(g, k):
                sp.wait_ge(gated, NT * g + k + 1)
                t = chunk_tile(k)
                sp.dma_start(d["y"][half, bass.ds(g * XT, XT), :, t * P:(t + 1) * P].rearrange("k p i -> p k i"),
                             gate[:, :, t * P:(t + 1) * P]).then_inc(stored[k % 2], 16)

            def load_bx(t):
                if t >= 2:
                    sp.wait_ge(mix_step, 3 * (t - 1))
                else:
                    sp.wait_ge(small_copied, 2)
                sp.dma_start(bx[t % 2], d["x"][half * NT + t]).then_inc(bx_loaded[t % 2], 16)

            def step(g, first, last):
                for s in range(SLOTS):
                    if first and s < NT:
                        load_bx(s)
                    if not first and s < NT:
                        store(g - 1, s)
                    if s % 2 == 0:
                        ahead = s // 2 + 3
                        if ahead < TILES:
                            load_w(g, ahead)
                        elif not last:
                            load_w(g + 1, ahead - TILES)

            def load_x(t):
                sp.wait_ge(turned, 2 * (t - XT) + 2)
                sp.dma_start(xt[:, t % XT, :], d["x"][half * NT + t]).then_inc(x_loaded[t % XT], 16)

            if first_half:
                for t in range(XT):
                    sp.dma_start(xt[:, t, :], d["x"][t]).then_inc(x_loaded[t], 16)
            sp.dma_start(small_raw, d["w_small"]).then_inc(small_loaded, 16)
            if first_half:
                sp.dma_start(mix.conv_w[:, :, :, :], d["conv_w"]).then_inc(params_loaded, 16)
                sp.dma_start(mix.norm_w[:, :, :], d["norm_w"]).then_inc(params_loaded, 16)
                sp.dma_start(mix.d_all[:, :], d["D"].partition_broadcast(P)).then_inc(params_loaded, 16)
                sp.dma_start(mix.a_neg[:, :], d["A_log"].partition_broadcast(P)).then_inc(params_loaded, 16)
                sp.dma_start(core.gate_value[:, :], d["gate"].partition_broadcast(P)).then_inc(params_loaded, 16)
            load_w(0, 0)
            load_w(0, 1)
            for t in range(XT, NT):
                load_x(t)
            sp.dma_start(dt_bias, d["dt_bias"].partition_broadcast(P)).then_inc(rows_loaded, 16)
            sp.dma_start(base, d["base"].partition_broadcast(P)).then_inc(rows_loaded, 16)
            sp.dma_start(w_branch, d["w_branch"]).then_inc(branch_w_loaded, 16)
            load_w(0, 2)
            groups(sp, step)
            if half + 1 < HALVES:
                sp.wait_ge(started, NT * GROUPS)
                prefetch_x(sp, d, mix, half + 1, x_ahead)
            for k in range(NT):
                store(GROUPS - 1, k)
            if half + 1 < HALVES:
                sp.wait_ge(x_ahead, 16 * XT)
            for i in range(2):
                sp.wait_ge(stored[i], 16 * GROUPS * NT // 2)
                sp.wait_ge(branch_stored[i], 16 * NT // 2)
            sp.wait_ge(cum_stored, 16)

        @block.gpsimd
        def _(pool):
            def decayed(g, k):
                pool.wait_ge(dtx_done, NT * g + k + 1)
                need(pool, dec_low, MOVES * g + k)
                pool.tensor_tensor(heads(dtx_dec[:, :]), heads(dtx[:, k % 2, :]),
                                   per_head(mix.decay, k, g), ALU.mult).then_inc(dec_done, 1)

            def decayed_low(g, k):
                pool.wait_ge(b_copied, MOVES * g + k + 1)
                pool.tensor_tensor(b_lo[:, :], b_tok[:, :], b_hi[:, :].bitcast(F32), ALU.subtract)
                pool.wait_ge(dec_high, MOVES * g + k + 1)
                pool.tensor_tensor(dec_lo[:, :], dtx_dec[:, :], dec_hi[:, :].bitcast(F32),
                                   ALU.subtract).then_inc(dec_low, 1)

            def inter_low(g, k):
                pool.wait_ge(inter_hi, (NT - SEQS) * g + k - SEQS + 1)
                toks = slice(chunk_tile(k) * P, (chunk_tile(k) + 1) * P)
                pool.tensor_tensor(c_lo[:, :], xbc[:, XT + 1, toks], c_hi[:, :].bitcast(F32), ALU.subtract)
                pool.tensor_tensor(st_lo[:, :], state[:, k % 2, :], st_hi[:, :].bitcast(F32),
                                   ALU.subtract).then_inc(inter_lo, 1)

            def norm(g, k):
                pool.wait_ge(squared, NT * g + k + 1)
                pool.tensor_tensor(var_eps[:, k % 2:k % 2 + 1], ssq[:, k % 2:k % 2 + 1], eps[:, :],
                                   ALU.add).then_inc(nvar_done, 1)
                pool.wait_ge(nvar_done, NT * g + k + 1)
                need(pool, yn_done, NT * g + k - 1)
                pool.tensor_tensor(rstd[:, k % 2:k % 2 + 1], var_eps[:, k % 2:k % 2 + 1], core.neg_half[:, 0:1],
                                   ALU.pow).then_inc(rstd_done, 1)

            def make_masks():
                pool.memset(core.ident[:, :], 0.0).then_inc(masks, 1)
                pool.memset(core.causal[:, :], 1.0).then_inc(masks, 1)
                pool.memset(core.neg_half[:, :], -0.5).then_inc(masks, 1)
                pool.wait_ge(masks, 3)
                pool.affine_select(out=core.ident[:, :], in_=core.ident[:, :], compare_op=ALU.not_equal,
                                   fill=1.0, base=0, pattern=[[-1, P]], channel_multiplier=1).then_inc(masks, 1)
                pool.affine_select(out=core.causal[:, :], in_=core.causal[:, :], compare_op=ALU.is_ge,
                                   fill=0.0, base=0, pattern=[[1, P]], channel_multiplier=-1).then_inc(masks, 1)

            def front():
                pool.memset(ones, 1.0).then_inc(constants, 1)
                for t in range(NT):
                    col = core.rstd[:, half * NT + t:half * NT + t + 1]
                    pool.wait_ge(aggr_done, t + 1)
                    pool.tensor_scalar(lv[:, t:t + 1], mv[:, t, 1:2], LN_EPS, None, ALU.add).then_inc(lv_done, 1)
                    pool.wait_ge(lv_done, t + 1)
                    pool.tensor_tensor(col, lv[:, t:t + 1], core.neg_half[:, 0:1], ALU.pow).then_inc(ln_rstd_done, 1)
                    if t == 1:
                        pool.wait_ge(small_step, 1)
                        pool.tensor_tensor(small_lo, small_raw, small_hi.bitcast(F32), ALU.subtract).then_inc(small_step, 1)
                pool.wait_ge(ln_rstd_done, NT)
                rstds = core.rstd[:, half * NT:(half + 1) * NT]
                pool.tensor_tensor(rms[:, :], mv[:, :, 1], rstds, ALU.mult).then_inc(rms_step, 1)
                pool.wait_ge(rms_step, 1)
                pool.tensor_tensor(rms[:, :], rms[:, :], rstds, ALU.mult).then_inc(rms_step, 1)
                pool.wait_ge(rms_step, 2)
                pool.tensor_scalar(rms[:, :], rms[:, :], RMS_EPS, None, ALU.add).then_inc(rms_step, 1)
                pool.wait_ge(rms_step, 3)
                pool.tensor_tensor(rms[:, :], rms[:, :], core.neg_half[:, :], ALU.pow).then_inc(rms_step, 1)

            def mix_streams(t):
                pool.wait_ge(bx_done, t + 1)
                pool.wait_ge(lg_step, 9)
                need(pool, mix_turned, t - 1)
                streams = bx[t % 2].rearrange("p (s c) -> p s c", c=CW)
                weights = sm[:, t, 0, :].unsqueeze(2).to_broadcast([P, STREAMS, CW])
                pool.tensor_tensor(streams, streams, weights, ALU.mult).then_inc(mix_step, 1)
                pool.wait_ge(mix_step, 3 * t + 1)
                pool.tensor_tensor(bx[t % 2][:, 0:2 * CW], bx[t % 2][:, 0:2 * CW], bx[t % 2][:, 2 * CW:],
                                   ALU.add).then_inc(mix_step, 1)
                pool.wait_ge(mix_step, 3 * t + 2)
                pool.tensor_tensor(mixed[t % 2], bx[t % 2][:, 0:CW], bx[t % 2][:, CW:2 * CW], ALU.add).then_inc(mix_step, 1)

            def step(g, first, last):
                if first:
                    for t in range(NT):
                        mix_streams(t)
                    pool.wait_ge(cum_stored, 16)
                for s in range(SLOTS):
                    before, mult, _ = tail_of(g, s, first)
                    if mult is not None:
                        norm(before, mult)
                    if START <= s:
                        k = s - START
                        if k >= SEQS:
                            inter_low(g, k)
                        if k:
                            norm(g, k - 1)
                        if k < MOVES:
                            decayed(g, k)
                            decayed_low(g, k)

            pool.memset(eps[:, :], NORM_EPS).then_inc(constants, 1)
            if first_half:
                make_masks()
            front()
            pool.wait_ge(constants, 2)
            groups(pool, step)
            norm(GROUPS - 1, NT - 1)

        @block.scalar
        def _(act):
            def split_hi(g, m):
                n = TILES * g + m
                act.wait_ge(w_loaded[m % 2], 16 * ((TILES // 2) * g + m // 2 + 1))
                need(act, proj_done, SLOTS * g + 2 * (m - 1))
                act.activation(w_hi[m % 2][:, :, :], w_raw[:, m % 2, :, :], ACT.Copy).then_inc(w_hi_done, 1)

            def split_next_hi(g, s, last):
                if s % 2 == 0:
                    m = s // 2 + 1
                    if m < TILES:
                        split_hi(g, m)
                    elif not last:
                        split_hi(g + 1, 0)

            def tap(g, s):
                act.wait_ge(proj_done, SLOTS * g + s + 1)
                need(act, silu_done, CONV_SLOTS * g + s - 1)
                act.wait_ge(tap_ready, g + 1)
                m = s // 2
                act.activation(acc[:, s % 2, :], bank_proj[s % 2][:, :], ACT.Identity,
                               bias=tap_par[:, m, 1:2], scale=tap_par[:, m, 0:1]).then_inc(tap_done, 1)

            def tap_params(g):
                act.activation(tap_par[:, :, :], mix.conv_w[:, g, :, 3:5], ACT.Copy).then_inc(tap_ready, 1)

            def tanh(g, s):
                act.wait_ge(conv_taken, CONV_SLOTS * g + s + 1)
                act.activation(th[:, s % 2, :], acc[:, s % 2, :], ACT.Tanh).then_inc(tanh_done, 1)

            def gate_in(g, s):
                v = s - CONV_SLOTS
                t, q = divmod(v, SEQS)
                act.wait_ge(proj_done, SLOTS * g + s + 1)
                if v < 2:
                    act.wait_ge(silu_done, CONV_SLOTS * g + s - 1)
                else:
                    act.wait_ge(gate_done, GATE_SLOTS * g + v - 1)
                if v == 0:
                    for i in range(2):
                        need(act, stored[i], 16 * (NT // 2) * g)
                act.activation(th[:, s % 2, :], bank_proj[s % 2][:, :], ACT.Tanh, scale=0.5).then_inc(tanh_done, 1)
                act.activation(gate[:, t, q * SEQ:(q + 1) * SEQ], bank_proj[s % 2][:, :], ACT.Identity,
                               scale=mix.norm_w[:, g, t:t + 1]).then_inc(gate_taken, 1)

            def load_cum(g, k):
                need(act, diff_done, NT * g + k - 1)
                act.dma_start(cum_b[:, k % 2, :, :],
                              d["cum"][half, chunk_tile(k), bass.ds(g * HPG, HPG), :].partition_broadcast(P)
                              ).then_inc(cum_loaded[k % 2], 16)

            def exps(g, k):
                act.wait_ge(diff_done, NT * g + k + 1)
                act.activation(attn[:, k % 2, :, :], attn[:, k % 2, :, :], ACT.Exp).then_inc(exp_done, 1)

            def b_tokens(g, k):
                act.wait_ge(bc_done, NT * g + k + 1)
                need(act, multiplied, NT * g + k)
                need(act, dec_low, MOVES * g + k)
                act.activation(b_tok[:, :], bank_bg[:, 0:P], ACT.Copy)
                act.activation(b_hi[:, :], bank_bg[:, 0:P], ACT.Copy).then_inc(b_copied, 1)

            def decayed_high(g, k):
                act.wait_ge(dec_done, MOVES * g + k + 1)
                need(act, multiplied, NT * g + k)
                act.activation(dec_hi[:, :], dtx_dec[:, :], ACT.Copy).then_inc(dec_high, 1)

            def square(g, k):
                act.wait_ge(y_done, NT * g + k + 1)
                need(act, y_turned, NT * (g - 1) + k + 1)
                act.activation(yn[:, k, :], y[:, :], ACT.Square, scale=GC ** -0.5,
                               accum_out=ssq[:, k % 2:k % 2 + 1]).then_inc(squared, 1)

            def inter_high(g, k):
                act.wait_ge(multiplied, NT * g + k)
                act.wait_ge(state_done, MOVES * g + k - SEQS + 1)
                toks = slice(chunk_tile(k) * P, (chunk_tile(k) + 1) * P)
                act.activation(c_hi[:, :], xbc[:, XT + 1, toks], ACT.Copy)
                act.activation(st_hi[:, :], state[:, k % 2, :], ACT.Copy).then_inc(inter_hi, 1)

            def scale_y(g, k):
                act.wait_ge(rstd_done, NT * g + k + 1)
                act.activation(yn[:, k, :], y[:, :], ACT.Copy, scale=rstd[:, k % 2:k % 2 + 1]).then_inc(yn_done, 1)

            def high(n):
                t, h = divmod(n, 2)
                act.wait_ge(turned, n + 1)
                act.activation(mix.x_hi[:, 4 * h:4 * h + 4, t * P:(t + 1) * P],
                               core.bank[2 + n % 4][:, :].rearrange("p (k c) -> p k c", c=P), ACT.Copy).then_inc(hi_done, 1)

            def by_token(bank):
                return bank[:, :].rearrange("p (t h) -> p t h", h=HEADS)

            def early(s):
                if s == 2:
                    act.wait_ge(lg_step, 6)
                    act.activation(sm, sm, ACT.Exp).then_inc(lg_exp, 1)
                    act.wait_ge(z_done, 2)
                    act.activation(soft, z, ACT.Abs).then_inc(soft_step, 1)
                    act.wait_ge(soft_step, 1)
                    act.activation(soft, soft, ACT.Exp, scale=-1.0).then_inc(soft_step, 1)
                    act.wait_ge(soft_step, 2)
                    act.activation(soft, soft, ACT.Ln, bias=1.0).then_inc(soft_step, 1)
                if s == 5:
                    act.wait_ge(summed, 2)
                    act.activation(mix.cum[:, :, :], by_token(bank_y), ACT.Copy).then_inc(cum_copied, 1)
                    act.activation(mix.exp_cum[:, :, :], by_token(bank_y), ACT.Exp)
                    act.activation(mix.exp_last[:, :, :], by_token(bank_inter), ACT.Exp).then_inc(cum_copied, 1)
                if s == 7:
                    act.wait_ge(decay_step, 1)
                    act.activation(mix.decay[:, :, :], mix.decay[:, :, :], ACT.Exp).then_inc(decay_step, 1)
                    act.wait_ge(cum_turned, 2)
                    for i in range(2):
                        act.activation(cum_hm[:, i * 512:(i + 1) * 512], core.bank[6 + i][0:HEADS, :],
                                       ACT.Copy).then_inc(cum_hm_copied, 1)
                    act.wait_ge(cum_hm_copied, 2)
                    act.dma_start(d["cum"][half].rearrange("t h i -> h t i"),
                                  cum_hm.rearrange("h (t i) -> h t i", i=P)).then_inc(cum_stored, 16)
                t = s - EARLY_TURN - 1
                if 0 <= t < NT:
                    act.wait_ge(branch_done, t + 1)
                    if t >= 2:
                        act.wait_ge(branch_stored[t % 2], 16 * (t // 2))
                    act.activation(branch[t % 2], bank_bg[:, 0:CW], ACT.Copy).then_inc(branch_copied, 1)
                    act.wait_ge(branch_copied, t + 1)
                    act.dma_start(d["branch"][half, :, t, :], branch[t % 2]).then_inc(branch_stored[t % 2], 16)
                t = s - EARLY_TURN
                if 0 <= t < NT:
                    act.wait_ge(mix_turned, t + 1)
                    need(act, branch_done, t - 1)
                    act.activation(mixed_t[t % 2], bank_x[:, 0:CW], ACT.Copy).then_inc(mix_copied, 1)

            def step(g, first, last):
                for s in range(SLOTS):
                    before, mult, _ = tail_of(g, s, first)
                    if first:
                        early(s)
                    if s < START:
                        split_next_hi(g, s, last)
                    if s < CONV_SLOTS:
                        tap(g, s)
                        if s:
                            tanh(g, s - 1)
                    else:
                        if s == CONV_SLOTS:
                            tanh(g, s - 1)
                        gate_in(g, s)
                        if s == CONV_SLOTS and not last:
                            tap_params(g + 1)
                    if mult is not None:
                        square(before, mult)
                        scale_y(before, mult)
                    if s in ((10, 11) if first else (4, 5)):
                        if first:
                            act.wait_ge(cum_stored, 16)
                        load_cum(g, s % 2)
                    if START <= s:
                        k = s - START
                        exps(g, k)
                        split_next_hi(g, s, last)
                        if k < NT - 2:
                            load_cum(g, k + 2)
                        if k >= SEQS:
                            inter_high(g, k)
                        if k:
                            square(g, k - 1)
                        if k < MOVES:
                            b_tokens(g, k)
                        if k:
                            scale_y(g, k - 1)
                        if k < MOVES:
                            decayed_high(g, k)

            for t in range(NT):
                high(2 * t)
                high(2 * t + 1)
                if t == 3 and first_half:
                    act.wait_ge(params_loaded, 80)
                    act.activation(mix.a_neg[:, :], mix.a_neg[:, :], ACT.Exp).then_inc(a_exp, 1)
                if t == 0:
                    act.wait_ge(small_loaded, 16)
                    act.activation(small_hi, small_raw, ACT.Copy).then_inc(small_step, 1)
                if t == 3:
                    split_hi(0, 0)
            if first_half:
                act.wait_ge(params_done, 2)
            tap_params(0)
            for q in range(SEQS):
                act.wait_ge(small_done, SEQS * (q + 1))
                act.activation(small[:, q * SEQ:(q + 1) * SEQ], core.bank[6 + q][0:SMALL, :], ACT.Copy).then_inc(small_copied, 1)
            groups(act, step)
            square(GROUPS - 1, NT - 1)
            scale_y(GROUPS - 1, NT - 1)

        @block.vector
        def _(dve):
            def split_lo(g, m):
                dve.wait_ge(w_hi_done, TILES * g + m + 1)
                need(dve, proj_done, SLOTS * g + 2 * (m - 1))
                dve.tensor_tensor(w_lo[m % 2][:, :, :], w_raw[:, m % 2, :, :], w_hi[m % 2][:, :, :].bitcast(F32),
                                  ALU.subtract).then_inc(w_split, 1)

            def split_next_lo(g, s, last):
                if s % 2 == 0:
                    m = s // 2 + 1
                    if m < TILES:
                        split_lo(g, m)
                    elif not last:
                        split_lo(g + 1, 0)

            def conv(g, s):
                m = s // 2
                dve.wait_ge(tap_done, CONV_SLOTS * g + s + 1)
                for back in (1, 2, 3):
                    if back > 1:
                        dve.wait_ge(conv_step, 2 * (CONV_SLOTS * g + s) + back - 1)
                    dve.scalar_tensor_tensor(acc[:, s % 2, back:], bank_proj[s % 2][:, 0:SEQ - back],
                                             mix.conv_w[:, g, m, 3 - back:4 - back], acc[:, s % 2, back:],
                                             ALU.mult, ALU.add).then_inc(conv_taken if back == 3 else conv_step, 1)

            def silu(g, s):
                m, q = divmod(s, SEQS)
                dve.wait_ge(tanh_done, SLOTS * g + s + 1)
                if s == 0:
                    need(dve, started, NT * g)
                if m == CONV_TILES - 1:
                    need(dve, multiplied, NT * g)
                dve.scalar_tensor_tensor(xbc[:, m, q * SEQ:(q + 1) * SEQ], th[:, s % 2, :], 1.0, acc[:, s % 2, :],
                                         ALU.add, ALU.mult).then_inc(silu_done, 1)

            def gate_silu(g, s):
                v = s - CONV_SLOTS
                t, q = divmod(v, SEQS)
                dve.wait_ge(gate_taken, GATE_SLOTS * g + v + 1)
                dve.scalar_tensor_tensor(gate[:, t, q * SEQ:(q + 1) * SEQ], th[:, s % 2, :], 1.0,
                                         gate[:, t, q * SEQ:(q + 1) * SEQ], ALU.add, ALU.mult).then_inc(gate_done, 1)

            def diffs(g, k):
                dve.wait_ge(cum_loaded[k % 2], 16 * ((NT // 2) * g + k // 2 + 1))
                need(dve, multiplied, NT * g + k - 1)
                for h in range(HPG):
                    op = dve.tensor_scalar(attn[:, k % 2, h, :], cum_b[:, k % 2, h, :],
                                           mix.cum[:, chunk_tile(k), bass.ds(g * HPG + h, 1)], 0.0,
                                           ALU.subtract, ALU.min)
                op.then_inc(diff_done, 1)

            def after_start(g, k):
                dve.wait_ge(started, NT * g + k + 1)
                dve.tensor_tensor(bc[:, :], bank_bg[:, P:2 * P], core.causal[:, :], ALU.mult).then_inc(bc_done, 1)
                need(dve, multiplied, NT * g + k - 1)
                dve.tensor_tensor(heads(dtx[:, k % 2, :]), heads(bank_x[:, :]), per_head(mix.dt, k, g),
                                  ALU.mult).then_inc(dtx_done, 1)
                dve.wait_ge(exp_done, NT * g + k + 1)
                dve.wait_ge(bc_done, NT * g + k + 1)
                dve.tensor_tensor(attn[:, k % 2, :, :], attn[:, k % 2, :, :],
                                  bc[:, :].unsqueeze(1).to_broadcast([P, HPG, P]), ALU.mult).then_inc(attn_done, 1)
                dve.tensor_tensor(heads(dx[:, :]), heads(bank_x[:, :]),
                                  mix.d_all[:, bass.ds(g * HPG, HPG)].unsqueeze(2).to_broadcast([P, HPG, HD]),
                                  ALU.mult).then_inc(dx_done, 1)

            def after_mult(g, k):
                dve.wait_ge(multiplied, NT * g + k + 1)
                need(dve, yn_done, NT * g + k)
                yk = y[:, :]
                if k < SEQS:
                    dve.wait_ge(dx_done, NT * g + k + 1)
                    dve.tensor_tensor(yk, bank_y[:, :], dx[:, :], ALU.add).then_inc(y_done, 1)
                    dve.tensor_copy(state[:, k % 2, :], bank_state[:, :]).then_inc(state_done, 1)
                    return
                at = 2 * (MOVES * g + k - SEQS)
                dve.tensor_tensor(heads(yk), heads(bank_inter[:, :]), per_head(mix.exp_cum, k, g),
                                  ALU.mult).then_inc(inter_step, 1)
                if k < MOVES:
                    dve.wait_ge(state_done, MOVES * g + k - SEQS + 1)
                    dve.tensor_tensor(heads(state[:, k % 2, :]), heads(state[:, k % 2, :]), per_head(mix.exp_last, k, g),
                                      ALU.mult).then_inc(state_step, 1)
                dve.wait_ge(inter_step, at + 1)
                dve.tensor_tensor(yk, yk, bank_y[:, :], ALU.add).then_inc(inter_step, 1)
                if k < MOVES:
                    dve.wait_ge(state_step, (MOVES - SEQS) * g + k - SEQS + 1)
                    dve.tensor_tensor(state[:, k % 2, :], state[:, k % 2, :], bank_state[:, :],
                                      ALU.add).then_inc(state_done, 1)
                dve.wait_ge(inter_step, at + 2)
                dve.wait_ge(dx_done, NT * g + k + 1)
                dve.tensor_tensor(yk, yk, dx[:, :], ALU.add).then_inc(y_done, 1)

            def gate_y(g, k, drain=False):
                t = chunk_tile(k)
                dve.wait_ge(y_turned, NT * g + k + 1)
                dve.wait_ge(gate_done, GATE_SLOTS * (g + 1))
                gate_k = gate[:, :, t * P:(t + 1) * P]
                dve.tensor_tensor(gate_k, turn_bank(k, drain)[:, :].rearrange("p (k i) -> p k i", i=P), gate_k,
                                  ALU.mult).then_inc(gated, 1)

            def low(n):
                t, h = divmod(n, 2)
                dve.wait_ge(hi_done, n + 1)
                dve.tensor_tensor(mix.x_lo[:, 4 * h:4 * h + 4, t * P:(t + 1) * P],
                                  core.bank[2 + n % 4][:, :].rearrange("p (k c) -> p k c", c=P),
                                  mix.x_hi[:, 4 * h:4 * h + 4, t * P:(t + 1) * P].bitcast(F32),
                                  ALU.subtract).then_inc(lo_done, 1)

            def front():
                for t in range(NT):
                    if t >= XT:
                        dve.wait_ge(x_loaded[t % XT], 16 + x_here)
                    else:
                        need(dve, x_loaded[t], x_here)
                    for h in range(2):
                        dve.bn_stats(stats[:, t % 2, h, :], xt[:, t % XT, h * 512:(h + 1) * 512]).then_inc(bn_step, 1)
                    dve.wait_ge(bn_step, 2 * t + 2)
                    dve.bn_aggr(mv[:, t, :], stats[:, t % 2, :, :]).then_inc(aggr_done, 1)
                    if t:
                        low(2 * t - 2)
                        low(2 * t - 1)
                    dve.wait_ge(ln_rstd_done, t + 1)
                    dve.wait_ge(aggr_done, t + 1)
                    dve.tensor_scalar(xt[:, t % XT, :], xt[:, t % XT, :], mv[:, t, 0:1],
                                      core.rstd[:, half * NT + t:half * NT + t + 1],
                                      ALU.subtract, ALU.mult).then_inc(xn_done, 1)
                    if t == 4:
                        split_lo(0, 0)
                    if t == 4 and first_half:
                        dve.wait_ge(params_loaded, 80)
                        dve.tensor_scalar(mix.conv_w[:, :, :, :], mix.conv_w[:, :, :, :], 0.5, None, ALU.mult).then_inc(params_done, 1)
                        dve.tensor_scalar(mix.norm_w[:, :, :], mix.norm_w[:, :, :], 0.5, None, ALU.mult).then_inc(params_done, 1)
                        dve.wait_ge(a_exp, 1)
                        dve.tensor_scalar(mix.a_neg[:, :], mix.a_neg[:, :], -1.0, None, ALU.mult).then_inc(params_done, 1)
                        dve.wait_ge(params_done, 3)
                        dve.wait_ge(masks, 5)
                low(2 * NT - 2)
                low(2 * NT - 1)
                dve.tensor_copy(core.mean[:, half * NT:(half + 1) * NT], mv[:, :, 0])

            def over_tiles(row, n):
                return row.unsqueeze(1).to_broadcast([P, NT // 2, n])

            def early(s):
                if s == 1:
                    dve.wait_ge(rows_loaded, 32)
                    for i, b in enumerate((bank_x, bank_bg)):
                        part = b[:, 0:4 * SMALL].rearrange("p (t c) -> p t c", c=SMALL)
                        tiles = slice(4 * i, 4 * i + 4)
                        dve.wait_ge(to_tokens, i + 1)
                        dve.tensor_tensor(z[:, tiles, :], part[:, :, 0:HEADS], over_tiles(dt_bias, HEADS),
                                          ALU.add).then_inc(z_done, 1)
                        if i == 0:
                            dve.wait_ge(rms_step, 4)
                        dve.tensor_tensor(logits[:, tiles, :], part[:, :, HEADS:],
                                          rms[:, tiles].unsqueeze(2).to_broadcast([P, NT // 2, LG]),
                                          ALU.mult).then_inc(lg_step, 1)
                    dve.wait_ge(lg_step, 2)
                    dve.tensor_tensor(logits, logits, base.unsqueeze(1).to_broadcast([P, NT, LG]),
                                      ALU.add).then_inc(lg_step, 1)
                    dve.wait_ge(lg_step, 3)
                    two = logits[:, :, STREAMS * STREAMS:].rearrange("p t (w s) -> p t w s", s=STREAMS)
                    dve.tensor_copy(core.res_logits[:, half * NT:(half + 1) * NT, :], logits[:, :, 0:STREAMS * STREAMS])
                    dve.tensor_reduce(sm_max, two, AX.X, ALU.max).then_inc(lg_step, 1)
                    dve.wait_ge(lg_step, 4)
                    dve.tensor_tensor(sm, two, sm_max.unsqueeze(3).to_broadcast([P, NT, 2, STREAMS]),
                                      ALU.subtract).then_inc(lg_step, 2)
                if s == 2:
                    dve.wait_ge(z_done, 2)
                    dve.tensor_scalar(mix.dt[:, :, :], z, 0.0, None, ALU.max).then_inc(dt_step, 1)
                    dve.wait_ge(lg_exp, 1)
                    dve.tensor_reduce(sm_sum, sm, AX.X, ALU.add).then_inc(lg_step, 1)
                    dve.wait_ge(lg_step, 7)
                    dve.reciprocal(sm_sum, sm_sum).then_inc(lg_step, 1)
                    dve.wait_ge(lg_step, 8)
                    dve.tensor_tensor(sm, sm, sm_sum.unsqueeze(3).to_broadcast([P, NT, 2, STREAMS]),
                                      ALU.mult).then_inc(lg_step, 1)
                    dve.wait_ge(lg_step, 9)
                    dve.tensor_copy(core.h_post[:, half * NT:(half + 1) * NT, :], sm[:, :, 1, :])
                if s == 3:
                    dve.wait_ge(dt_step, 1)
                    dve.wait_ge(soft_step, 3)
                    dve.tensor_tensor(mix.dt[:, :, :], mix.dt[:, :, :], soft, ALU.add).then_inc(dt_step, 1)
                    dve.wait_ge(dt_step, 2)
                    dve.tensor_tensor(decays, mix.dt[:, :, :], mix.a_neg[:, :].unsqueeze(1).to_broadcast([P, NT, HEADS]),
                                      ALU.mult).then_inc(dt_step, 1)
                    dve.wait_ge(dt_step, 3)
                    dve.tensor_scalar(decays, decays, LOG_ZERO, None, ALU.max).then_inc(dt_step, 1)
                if s == 6:
                    dve.wait_ge(cum_copied, 2)
                    dve.tensor_tensor(mix.decay[:, :, :], bank_inter[:, :].rearrange("p (t h) -> p t h", h=HEADS),
                                      mix.cum[:, :, :], ALU.subtract).then_inc(decay_step, 1)
                t = s - 2
                if 0 <= t < NT:
                    dve.wait_ge(bx_loaded[t % 2], 16 * (t // 2 + 1))
                    dve.tensor_scalar(bx[t % 2], bx[t % 2], mv[:, t, 0:1],
                                      core.rstd[:, half * NT + t:half * NT + t + 1],
                                      ALU.subtract, ALU.mult).then_inc(bx_done, 1)
                if s == START:
                    for i in range(2):
                        dve.wait_ge(branch_stored[i], 16 * NT // 2)

            def step(g, first, last):
                for s in range(SLOTS):
                    before, mult, turn = tail_of(g, s, first)
                    if s < START:
                        split_next_lo(g, s, last)
                    elif s > START:
                        diffs(g, s - START)
                    if first:
                        early(s)
                    if s < CONV_SLOTS:
                        conv(g, s)
                        if s:
                            silu(g, s - 1)
                    else:
                        if s == CONV_SLOTS:
                            silu(g, s - 1)
                            diffs(g, 0)
                        gate_silu(g, s)
                    if mult is not None:
                        after_mult(before, mult)
                    if turn is not None:
                        gate_y(before, turn)
                    if START <= s:
                        k = s - START
                        if k:
                            after_mult(g, k - 1)
                        after_start(g, k)
                        split_next_lo(g, s, last)

            front()
            groups(dve, step)
            for k in range(NT):
                if k == DRAIN:
                    after_mult(GROUPS - 1, NT - 1)
                gate_y(GROUPS - 1, k, True)

        @block.tensor
        def _(pe):
            def project(g, s, part=(0, KT)):
                m, q = divmod(s, SEQS)
                pe.wait_ge(w_split, TILES * g + m + 1)
                if s < 2:
                    need(pe, gate_taken, GATE_SLOTS * (g - 1) + GATE_SLOTS - 1 + s)
                elif s < CONV_SLOTS + 2:
                    pe.wait_ge(conv_taken, CONV_SLOTS * g + s - 1)
                else:
                    pe.wait_ge(gate_taken, GATE_SLOTS * g + s - CONV_SLOTS - 1)
                out = bank_proj[s % 2][:, :]
                for k in range(*part):
                    hi = mix.x_hi[:, k, q * SEQ:(q + 1) * SEQ]
                    lo = mix.x_lo[:, k, q * SEQ:(q + 1) * SEQ]
                    pe.matmul(out, w_hi[m % 2][:, k, :], hi, start=(k == 0), stop=False)
                    pe.matmul(out, w_hi[m % 2][:, k, :], lo, start=False, stop=False)
                    mm = pe.matmul(out, w_lo[m % 2][:, k, :], hi, start=False, stop=(k == KT - 1))
                if part[1] == KT:
                    mm.then_inc(proj_done, 1)

            def start(g, k):
                t = chunk_tile(k)
                toks = slice(t * P, (t + 1) * P)
                pe.wait_ge(silu_done, CONV_SLOTS * (g + 1))
                need(pe, dx_done, NT * g + k)
                need(pe, bc_done, NT * g + k)
                need(pe, b_copied, MOVES * g + min(k, MOVES))
                for c in range(XT):
                    pe.transpose(bank_x[:, c * P:(c + 1) * P], xbc[:, c, toks], core.ident[:, :])
                pe.transpose(bank_bg[:, 0:P], xbc[:, XT, toks], core.ident[:, :])
                pe.matmul(bank_bg[:, P:2 * P], xbc[:, XT, toks], xbc[:, XT + 1, toks],
                          start=True, stop=True).then_inc(started, 1)

            def mult(g, k):
                t = chunk_tile(k)
                pe.wait_ge(attn_done, NT * g + k + 1)
                pe.wait_ge(dtx_done, NT * g + k + 1)
                need(pe, y_done, NT * g + k)
                need(pe, state_done, MOVES * g + min(k, MOVES))
                for h in range(HPG):
                    mm = pe.matmul(bank_y[:, h * HD:(h + 1) * HD], attn[:, k % 2, h, :],
                                   dtx[:, k % 2, h * HD:(h + 1) * HD], start=True, stop=True)
                if k >= SEQS:
                    pe.wait_ge(inter_lo, (NT - SEQS) * g + k - SEQS + 1)
                    pe.matmul(bank_inter[:, :], c_hi[:, :], st_hi[:, :], start=True, stop=False)
                    pe.matmul(bank_inter[:, :], c_hi[:, :], st_lo[:, :], start=False, stop=False)
                    mm = pe.matmul(bank_inter[:, :], c_lo[:, :], st_hi[:, :], start=False, stop=True)
                if k < MOVES:
                    pe.wait_ge(dec_low, MOVES * g + k + 1)
                    pe.matmul(bank_state[:, :], b_hi[:, :], dec_hi[:, :], start=True, stop=False)
                    pe.matmul(bank_state[:, :], b_hi[:, :], dec_lo[:, :], start=False, stop=False)
                    mm = pe.matmul(bank_state[:, :], b_lo[:, :], dec_hi[:, :], start=False, stop=True)
                mm.then_inc(multiplied, 1)

            def turn(g, k, drain=False):
                pe.wait_ge(yn_done, NT * g + k + 1)
                if drain:
                    pe.wait_ge(gate_taken, GATE_SLOTS * GROUPS)
                    need(pe, gated, NT * g + k - 1)
                else:
                    need(pe, gated, NT * g + k)
                for c in range(XT):
                    mm = pe.transpose(turn_bank(k, drain)[:, c * P:(c + 1) * P], yn[:, k, c * P:(c + 1) * P], core.ident[:, :])
                mm.then_inc(y_turned, 1)

            def front():
                pair = 2 * P

                def small_products(n):
                    pe.wait_ge(lo_done, 4 * n + 4)
                    pe.wait_ge(small_step, 2)
                    toks = slice(n * pair, (n + 1) * pair)
                    out = core.bank[6 + n // 2][0:SMALL, (n % 2) * pair:(n % 2 + 1) * pair]
                    for k in range(KT):
                        pe.matmul(out, small_hi[:, k, :], mix.x_hi[:, k, toks], start=(k == 0), stop=False)
                        pe.matmul(out, small_hi[:, k, :], mix.x_lo[:, k, toks], start=False, stop=False)
                        mm = pe.matmul(out, small_lo[:, k, :], mix.x_hi[:, k, toks], start=False, stop=(k == KT - 1))
                    mm.then_inc(small_done, 1)

                if first_half:
                    pe.wait_ge(masks, 5)
                for n in range(2 * NT):
                    t, h = divmod(n, 2)
                    pe.wait_ge(xn_done, t + 1)
                    need(pe, lo_done, n - 3)
                    for k in range(4):
                        mm = pe.transpose(core.bank[2 + n % 4][:, k * P:(k + 1) * P],
                                          xt[:, t % XT, (4 * h + k) * P:(4 * h + k + 1) * P], core.ident[:, :])
                    mm.then_inc(turned, 1)
                    if n % 4 == 1 and n > 4:
                        small_products(n // 4 - 1)
                    if n in FILL:
                        project(0, 0, FILL[n])
                project(0, 0, FILL[2 * NT])
                small_products(NT // 2 - 1)

            def small_to_tokens():
                pe.wait_ge(small_copied, 2)
                for i, b in enumerate((bank_x, bank_bg)):
                    for t in range(4 * i, 4 * i + 4):
                        mm = pe.transpose(b[:, (t % 4) * SMALL:(t % 4 + 1) * SMALL],
                                          small[:, t * P:(t + 1) * P], core.ident[0:SMALL, 0:SMALL])
                    mm.then_inc(to_tokens, 1)

            def early(s):
                if s == 4:
                    pe.wait_ge(dt_step, 4)
                    pe.wait_ge(constants, 2)
                    pe.matmul(bank_y[:, :], core.causal[:, :], decays.rearrange("p t h -> p (t h)"),
                              start=True, stop=True).then_inc(summed, 1)
                    pe.matmul(bank_inter[:, :], ones, decays.rearrange("p t h -> p (t h)"),
                              start=True, stop=True).then_inc(summed, 1)
                if s == 6:
                    pe.wait_ge(cum_copied, 2)
                    for i in range(2):
                        for t in range(4 * i, 4 * i + 4):
                            mm = pe.transpose(core.bank[6 + i][0:HEADS, (t % 4) * P:(t % 4 + 1) * P], mix.cum[:, t, :],
                                              core.ident[:, :])
                        mm.then_inc(cum_turned, 1)
                t = s - EARLY_TURN
                if 0 <= t < NT:
                    if t == 0:
                        pe.wait_ge(branch_w_loaded, 16)
                    pe.wait_ge(mix_copied, t + 1)
                    need(pe, branch_copied, t)
                    for c in range(2):
                        mm = pe.matmul(bank_bg[:, 0:CW], mixed_t[t % 2][:, c * P:(c + 1) * P],
                                       w_branch[:, c, :], start=(c == 0), stop=(c == 1))
                    mm.then_inc(branch_done, 1)

            def turn_mixed(t):
                pe.wait_ge(mix_step, 3 * (t + 1))
                pe.wait_ge(lg_step, 2)
                need(pe, mix_copied, t)
                for c in range(2):
                    mm = pe.transpose(bank_x[:, c * P:(c + 1) * P], mixed[t % 2][:, c * P:(c + 1) * P], core.ident[:, :])
                mm.then_inc(mix_turned, 1)

            def step(g, first, last):
                for s in range(SLOTS):
                    before, mult_k, turn_k = tail_of(g, s, first)
                    if not first:
                        project(g, s)
                    elif s:
                        project(g, s, (0, KT // 2))
                        if s == 1:
                            small_to_tokens()
                        if 0 <= s - EARLY_TURN < NT:
                            turn_mixed(s - EARLY_TURN)
                        project(g, s, (KT // 2, KT))
                    if first:
                        early(s)
                        if s == START:
                            pe.wait_ge(branch_copied, NT)
                    if mult_k is not None:
                        mult(before, mult_k)
                    if turn_k is not None:
                        turn(before, turn_k)
                    if START <= s:
                        k = s - START
                        if k:
                            mult(g, k - 1)
                        start(g, k)

            front()
            groups(pe, step)
            for k in range(NT):
                if k == DRAIN:
                    mult(GROUPS - 1, NT - 1)
                turn(GROUPS - 1, k, True)


def output_block(nc, core):
    d = core.dram
    bank = core.bank
    NS = STREAMS
    PASSES = 2 * HALVES
    ROWS = 2 * NT
    with ExitStack() as ctx:
        def sb(name, shape, dt=F32):
            return ctx.enter_context(nc.sbuf_tensor(name, shape, dt))

        def sem(name):
            return core.semaphore(name)

        y_raw = sb("y_raw", [P, 2, HALF])
        w_raw = sb("wo_raw", [P, 2, 512])
        y_hi = [sb(f"y_hi{i}", [P, HALF], F32R) for i in range(2)]
        y_lo = [sb(f"y_lo{i}", [P, HALF], F32R) for i in range(2)]
        w_hi = [sb(f"wo_hi{i}", [P, 512], F32R) for i in range(2)]
        w_lo = [sb(f"wo_lo{i}", [P, 512], F32R) for i in range(2)]
        s_sb = sb("s_sb", [P, NT, DM])
        sigm = sb("sigm", [P, 2])
        mat = sb("mat", [P, ROWS, NS, NS])
        mat_e = sb("mat_e", [P, ROWS, NS, NS])
        top = sb("top", [P, ROWS, NS])
        tot = sb("tot", [P, ROWS, NS])
        xq = sb("xq", [P, DM])
        post = sb("post", [P, NS])
        br = sb("br", [P, CW])
        xn = sb("xnq", [P, DM])
        f = sb("f", [P, DM])
        tf = sb("tf", [P, DM])
        o_sb = sb("o_sb", [P, DM])
        f_keep = sb("f_keep", [P, NT, 512])
        x_keep = sb("x_keep", [P, NT, 512])

        k_loaded = [sem("k_loaded0"), sem("k_loaded1")]
        k_hi, k_split, k_done = sem("k_hi"), sem("k_split"), sem("k_done")
        evacuated = [sem("evacuated_even"), sem("evacuated_odd")]
        sig_exp, sig_step = sem("sig_exp"), sem("sig_step")
        guard_step, guard_act, sk_step, res_step = sem("guard_step"), sem("guard_act"), sem("sk_step"), sem("res_step")
        tile_loaded, post_copied = sem("tile_loaded"), sem("post_copied")
        tile_xn, post_done, f_step, f_tanh, f_silu = (sem("tile_xn"), sem("post_done"), sem("f_step"), sem("f_tanh"),
                                                      sem("f_silu"))
        s_mul, x_kept, o_done, o_stored = sem("s_mul"), sem("x_kept"), sem("o_done"), sem("o_stored")
        o_loaded = sem("o_loaded")
        last_mul, last_done = sem("last_mul"), [sem("last_done_even"), sem("last_done_odd")]
        last_stored = [sem("last_stored0"), sem("last_stored1")]
        block = ctx.enter_context(nc.Block())

        TURNS = OT // 2 - 2
        SK_TURNS = (TURNS, (SINKHORN - 1) // 2 - TURNS)
        SK_AHEAD = SINKHORN - 1 - 2 * sum(SK_TURNS)

        def k_steps(eng, p, one, extra=None, begin=None):
            n = SK_TURNS[p]
            if p == 0:
                one(p, 0, 0)
            one(p, 0, 1)
            if p == 0 and begin is not None:
                begin()
            with eng.Fori(1, 1 + n) as i:
                for j in range(2):
                    one(p, i, j)
                    if extra is not None:
                        extra(p, i - 1, j)
            if n < TURNS:
                with eng.Fori(1 + n, OT // 2 - 1) as i:
                    one(p, i, 0)
                    one(p, i, 1)
            one(p, OT // 2 - 1, 0)
            one(p, OT // 2 - 1, 1)
            one(p + 1, 0, 0)

        F_PARTS = ((0, 6), (6, 14), (14, NS * NS), (0, 0))

        def tile_steps(eng, p, one, part):
            def turn(i, last):
                for q in range(4):
                    if not (last and q == 3):
                        one(p, 2 * i + (q + 1) // 2, (q + 1) % 2)
                    elif p + 1 < PASSES:
                        one(p + 1, 0, 0)
                    part((p - 2) * NT + i, i, p, q, last)

            with eng.Fori(0, NT - 1) as i:
                turn(i, False)
            turn(NT - 1, True)

        @block.sync
        def _(sp):
            def load(p, i, j):
                need(sp, k_split, OT * p + 2 * i + j - 1)
                sp.dma_start(y_raw[:, j, :], d["y"][p // 2, 2 * i + j]).then_inc(k_loaded[j], 16)
                sp.dma_start(w_raw[:, j, :], d["w_out"][p % 2, 2 * i + j]).then_inc(k_loaded[j], 16)

            for p in range(2):
                k_steps(sp, p, load)
            def load_tile(n, i, p, part):
                if part < 2:
                    half = slice(part * 512, (part + 1) * 512)
                    sp.dma_start(xq[:, half], d["x"][n][:, half]).then_inc(tile_loaded, 16)
                else:
                    sp.dma_start(br[:, :], d["branch"][p - 2, :, i, :]).then_inc(tile_loaded, 16)

            def tile(n, i, p, q, last):
                if q and not (last and p == PASSES - 1):
                    sp.wait_ge(tile_xn, n + 1)
                    sp.wait_ge(post_done, NS * n + NS)
                    load_tile(n + 1, 0 if last else i + 1, p + 1 if last else p, q - 1)

            for part in range(3):
                load_tile(0, 0, 2, part)
            for p in range(2, PASSES):
                tile_steps(sp, p, load, tile)

        @block.gpsimd
        def _(pool):
            def tile(n, i, p, q, last):
                if q:
                    return
                pool.dma_start(o_sb[:, :], d["x"][n]).then_inc(o_loaded, 16)
                width = DM if p == 2 else 512
                pool.wait_ge(o_loaded, 16 * n + 16)
                if p == 3:
                    pool.tensor_copy(x_keep[:, i, :], o_sb[:, 512:]).then_inc(x_kept, 1)
                pool.wait_ge(s_mul, n + 1)
                pool.tensor_tensor(o_sb[:, 0:width], tf[:, 0:width], o_sb[:, 0:width], ALU.add).then_inc(o_done, 1)
                pool.wait_ge(o_done, n + 1)
                if p == 3:
                    pool.wait_ge(x_kept, i + 1)
                pool.nop(nofuse=True)
                pool.dma_start(d["out"][n][:, 0:width], o_sb[:, 0:width]).then_inc(o_stored, 16)
                pool.wait_ge(o_stored, 16 * n + 16)
                pool.nop(nofuse=True)

            for p in range(2, PASSES):
                tile_steps(pool, p, lambda p, i, j: None, tile)
            for t in range(0, NT, 2):
                pool.wait_ge(last_mul, t + 1)
                pool.tensor_tensor(f_keep[:, t, :], f_keep[:, t, :], x_keep[:, t, :], ALU.add).then_inc(last_done[0], 1)
            pool.wait_ge(o_stored, 16 * ROWS)

        @block.scalar
        def _(act):
            def split_hi(p, i, j):
                kk = OT * p + 2 * i + j
                act.wait_ge(k_loaded[j], 32 * ((OT // 2) * p + i + 1))
                need(act, k_done, kk - 1)
                act.activation(y_hi[j][:, :], y_raw[:, j, :], ACT.Copy)
                act.activation(w_hi[j][:, :], w_raw[:, j, :], ACT.Copy).then_inc(k_hi, 1)

            def evacuate(p):
                act.wait_ge(k_done, OT * (p + 1))
                if p == 2:
                    act.wait_ge(s_mul, NT)
                for t in range(0, NT, 2):
                    act.activation(s_sb[:, t, (p % 2) * 512:(p % 2 + 1) * 512], bank[t][:, :],
                                   ACT.Copy).then_inc(evacuated[0], 1)

            def tile(n, i, p, q, last):
                if q == 0:
                    act.activation(post[:, :], core.h_post[:, n, :], ACT.Copy).then_inc(post_copied, 1)
                    act.wait_ge(post_copied, n + 1)
                    act.wait_ge(tile_loaded, 48 * n + 48)
                    for s in range(NS):
                        act.activation(f[:, s * CW:(s + 1) * CW], br[:, :], ACT.Copy,
                                       scale=post[:, s:s + 1]).then_inc(post_done, 1)
                if q == 2:
                    act.wait_ge(o_loaded, 16 * n + 16)
                    act.wait_ge(f_step, NS * NS * (n + 1))
                    act.activation(tf[:, :], f[:, :], ACT.Tanh, scale=0.5).then_inc(f_tanh, 1)
                if q == 3:
                    act.wait_ge(f_silu, n + 1)

            act.activation(sigm[:, 0:1], core.gate_value[:, 0:1], ACT.Exp, scale=-1.0).then_inc(sig_exp, 1)
            def guarded():
                act.wait_ge(guard_step, 3)
                act.activation(mat_e[:, :, :, :], mat[:, :, :, :], ACT.Exp).then_inc(guard_act, 1)
                act.wait_ge(guard_step, 4)
                act.activation(tot[:, :, :], tot[:, :, :], ACT.Ln).then_inc(guard_act, 1)
                act.wait_ge(guard_step, 7)
                act.activation(mat[:, :, :, :], mat[:, :, :, :], ACT.Exp).then_inc(guard_act, 1)

            for p in range(2):
                k_steps(act, p, split_hi, begin=guarded)
                evacuate(p)
            tile_steps(act, 2, split_hi, tile)
            evacuate(2)
            tile_steps(act, 3, split_hi, tile)
            for t in range(NT):
                act.wait_ge(last_done[t % 2], t // 2 + 1)
                act.dma_start(d["out"][NT + t][:, 512:], f_keep[:, t, :]).then_inc(last_stored[t % 2], 16)
            for i in range(2):
                act.wait_ge(last_stored[i], 16 * NT // 2)

        @block.vector
        def _(dve):
            def split_lo(p, i, j):
                kk = OT * p + 2 * i + j
                dve.wait_ge(k_hi, kk + 1)
                need(dve, k_done, kk - 1)
                dve.tensor_tensor(y_lo[j][:, :], y_raw[:, j, :], y_hi[j][:, :].bitcast(F32), ALU.subtract)
                dve.tensor_tensor(w_lo[j][:, :], w_raw[:, j, :], w_hi[j][:, :].bitcast(F32), ALU.subtract).then_inc(k_split, 1)

            def over_rows(a):
                return a.unsqueeze(3).to_broadcast([P, ROWS, NS, NS])

            def over_columns(a):
                return a.unsqueeze(2).to_broadcast([P, ROWS, NS, NS])

            by_row = mat[:, :, :, :]
            by_column = mat[:, :, :, :].rearrange("p t i j -> p t j i")

            def guarded():
                dve.tensor_reduce(top[:, :, :], by_row, AX.X, ALU.max).then_inc(guard_step, 1)
                dve.wait_ge(guard_step, 2)
                dve.tensor_tensor(by_row, by_row, over_rows(top[:, :, :]), ALU.subtract).then_inc(guard_step, 1)
                dve.wait_ge(guard_act, 1)
                dve.tensor_reduce(tot[:, :, :], mat_e[:, :, :, :], AX.X, ALU.add).then_inc(guard_step, 1)
                dve.wait_ge(guard_act, 2)
                dve.tensor_tensor(by_row, by_row, over_rows(tot[:, :, :]), ALU.subtract).then_inc(guard_step, 1)
                dve.wait_ge(guard_step, 5)
                dve.tensor_reduce(top[:, :, :], by_column, AX.X, ALU.max).then_inc(guard_step, 1)
                dve.wait_ge(guard_step, 6)
                dve.tensor_tensor(by_row, by_row, over_columns(top[:, :, :]), ALU.subtract).then_inc(guard_step, 1)
                dve.wait_ge(guard_act, 3)
                dve.tensor_reduce(tot[:, :, :], by_column, AX.X, ALU.add).then_inc(guard_step, 1)
                dve.wait_ge(guard_step, 8)
                dve.reciprocal(tot[:, :, :], tot[:, :, :]).then_inc(guard_step, 1)
                dve.wait_ge(guard_step, 9)
                dve.tensor_tensor(by_row, by_row, over_columns(tot[:, :, :]), ALU.mult).then_inc(guard_step, 1)
                dve.wait_ge(guard_step, 10)

            def iterate(n):
                for side, view, over in ((0, by_row, over_rows), (1, by_column, over_columns)):
                    at = 3 * (2 * n + side)
                    if not (isinstance(at, int) and at == 0):
                        dve.wait_ge(sk_step, at)
                    dve.tensor_reduce(tot[:, :, :], view, AX.X, ALU.add).then_inc(sk_step, 1)
                    dve.wait_ge(sk_step, at + 1)
                    dve.reciprocal(tot[:, :, :], tot[:, :, :]).then_inc(sk_step, 1)
                    dve.wait_ge(sk_step, at + 2)
                    dve.tensor_tensor(by_row, by_row, over(tot[:, :, :]), ALU.mult).then_inc(sk_step, 1)

            def extra(p, i, j):
                iterate(SK_AHEAD + 2 * (p * SK_TURNS[0]) + 2 * i + j)

            def evacuate(p):
                dve.wait_ge(k_done, OT * (p + 1))
                if p == 2:
                    dve.wait_ge(s_mul, NT)
                for t in range(1, NT, 2):
                    dve.tensor_copy(s_sb[:, t, (p % 2) * 512:(p % 2 + 1) * 512], bank[t][:, :]).then_inc(evacuated[1], 1)

            def tile(n, i, p, q, last):
                if q == 0:
                    dve.wait_ge(tile_loaded, 48 * n + 48)
                    dve.tensor_scalar(xn[:, :], xq[:, :], core.mean[:, bass.ds(n, 1)], core.rstd[:, bass.ds(n, 1)],
                                      ALU.subtract, ALU.mult).then_inc(tile_xn, 1)
                    dve.wait_ge(tile_xn, n + 1)
                    dve.wait_ge(post_done, NS * n + NS)
                for at in range(*F_PARTS[q]):
                    c, r = divmod(at, NS)
                    if c:
                        dve.wait_ge(f_step, NS * NS * n + at - NS + 1)
                    out = f[:, r * CW:(r + 1) * CW]
                    dve.scalar_tensor_tensor(out, xn[:, c * CW:(c + 1) * CW], mat[:, n, r, c:c + 1], out,
                                             ALU.mult, ALU.add).then_inc(f_step, 1)
                if q == 3:
                    dve.wait_ge(f_tanh, n + 1)
                    dve.scalar_tensor_tensor(tf[:, :], tf[:, :], 1.0, f[:, :], ALU.add, ALU.mult).then_inc(f_silu, 1)
                    dve.wait_ge(f_silu, n + 1)
                    if p == 2:
                        dve.scalar_tensor_tensor(tf[:, :], tf[:, :], 0.5, s_sb[:, i, :], ALU.mult,
                                                 ALU.mult).then_inc(s_mul, 1)
                    else:
                        dve.tensor_scalar(f_keep[:, i, :], tf[:, 512:], 0.5, None, ALU.mult)
                        dve.scalar_tensor_tensor(tf[:, 0:512], tf[:, 0:512], 0.5, s_sb[:, i, 0:512], ALU.mult,
                                                 ALU.mult).then_inc(s_mul, 1)

            def begin():
                dve.wait_ge(sig_exp, 1)
                dve.tensor_scalar(sigm[:, 0:1], sigm[:, 0:1], 1.0, None, ALU.add).then_inc(sig_step, 1)
                dve.tensor_scalar(mat[:, :, :, :], core.res_logits[:, :, :].rearrange("p t (i j) -> p t i j", j=NS),
                                  1.0 / TAU, None, ALU.mult).then_inc(guard_step, 1)
                dve.wait_ge(sig_step, 1)
                dve.reciprocal(sigm[:, 0:1], sigm[:, 0:1]).then_inc(sig_step, 1)
                dve.wait_ge(sig_step, 2)
                dve.tensor_scalar(sigm[:, 1:2], sigm[:, 0:1], -1.0, 1.0, ALU.mult, ALU.add).then_inc(sig_step, 1)
                dve.wait_ge(guard_step, 1)
                guarded()
                for n in range(SK_AHEAD):
                    iterate(n)

            for p in range(2):
                k_steps(dve, p, split_lo, extra, begin)
                evacuate(p)
            dve.wait_ge(sk_step, 6 * (SINKHORN - 1))
            dve.wait_ge(sig_step, 3)
            dve.tensor_scalar(by_row, by_row, sigm[:, 0:1], None, ALU.mult).then_inc(res_step, 1)
            dve.wait_ge(res_step, 1)
            diag = mat[:, :, :, :].rearrange("p t i j -> p t (i j)")[:, :, 0::NS + 1]
            dve.tensor_scalar(diag, diag, sigm[:, 1:2], None, ALU.add).then_inc(res_step, 1)
            dve.wait_ge(res_step, 2)
            dve.wait_ge(evacuated[0], NT)
            dve.wait_ge(evacuated[1], NT)
            tile_steps(dve, 2, split_lo, tile)
            evacuate(2)
            dve.wait_ge(evacuated[0], 3 * NT // 2)
            dve.wait_ge(evacuated[1], 3 * NT // 2)
            tile_steps(dve, 3, split_lo, tile)
            dve.wait_ge(k_done, OT * PASSES)
            dve.wait_ge(s_mul, ROWS)
            for t in range(NT):
                dve.tensor_tensor(f_keep[:, t, :], f_keep[:, t, :], bank[t][:, :], ALU.mult).then_inc(last_mul, 1)
                if t % 2:
                    dve.wait_ge(last_mul, t + 1)
                    dve.wait_ge(x_kept, t + 1)
                    dve.tensor_tensor(f_keep[:, t, :], f_keep[:, t, :], x_keep[:, t, :], ALU.add).then_inc(last_done[1], 1)

        @block.tensor
        def _(pe):
            def products(p, i, j, first=False, last=False):
                pe.wait_ge(k_split, OT * p + 2 * i + j + 1)
                for t in range(NT):
                    if first and p:
                        pe.wait_ge(evacuated[t % 2], NT // 2 * (p - 1) + t // 2 + 1)
                    toks = slice(t * P, (t + 1) * P)
                    pe.matmul(bank[t][:, :], y_hi[j][:, toks], w_hi[j][:, :], start=first, stop=False)
                    pe.matmul(bank[t][:, :], y_hi[j][:, toks], w_lo[j][:, :], start=False, stop=False)
                    mm = pe.matmul(bank[t][:, :], y_lo[j][:, toks], w_hi[j][:, :], start=False, stop=last)
                mm.then_inc(k_done, 1)

            for p in range(PASSES):
                products(p, 0, 0, first=True)
                products(p, 0, 1)
                with pe.Fori(1, OT // 2 - 1) as i:
                    products(p, i, 0)
                    products(p, i, 1)
                products(p, OT // 2 - 1, 0)
                products(p, OT // 2 - 1, 1, last=True)


def program(nc, x, w_in, w_small, conv_w, norm_w, D, dt_bias, A_log, base, w_branch, gate, w_out, out):
    def scratch(name, shape):
        return nc.dram_tensor(name, shape, F32, kind="Internal").ap()

    dram = dict(x=x, w_in=w_in, w_small=w_small, conv_w=conv_w, norm_w=norm_w, D=D, dt_bias=dt_bias,
                A_log=A_log, base=base, w_branch=w_branch, gate=gate, w_out=w_out, out=out,
                cum=scratch("cum_scratch", (HALVES, NT, HEADS, P)),
                y=scratch("y_scratch", (HALVES, OT, P, HALF)), branch=scratch("branch_scratch", (HALVES, P, NT, CW)))
    with ExitStack() as ctx:
        core = Core(nc, ctx, dram)
        with ExitStack() as inner:
            mix = Mixer(nc, inner)
            for half in range(HALVES):
                mixer_block(nc, core, mix, half)
                core.end_phase()
        output_block(nc, core)


def kernel(**inputs):
    import numpy as _np
    import concourse.bacc as _bacc
    from concourse.bass_utils import run_bass_kernel_spmd as _run

    a = {n.replace("L0_attn_", "").replace("L0_ffn_", "f_"): _np.asarray(v) for n, v in inputs.items()}
    gn = GROUPS * P
    wi = a["in_proj_w"]

    def tiles(w):
        n = w.shape[0] // (GROUPS * P)
        return w.reshape(GROUPS, n, P, KT, P).transpose(0, 1, 4, 3, 2)

    w_in = _np.concatenate([tiles(wi[INNER:2 * INNER]), tiles(wi[2 * INNER:2 * INNER + gn]),
                            tiles(wi[2 * INNER + gn:2 * INNER + 2 * gn]), tiles(wi[0:INNER])], axis=1)

    def channels(v):
        rest = v.shape[1:]
        parts = [v[0:INNER].reshape(GROUPS, XT, P, *rest), v[INNER:INNER + gn].reshape(GROUPS, 1, P, *rest),
                 v[INNER + gn:].reshape(GROUPS, 1, P, *rest)]
        return _np.moveaxis(_np.concatenate(parts, axis=1), 2, 0)

    small = _np.concatenate([wi[2 * INNER + 2 * gn:], a["f_W_res"], a["f_W_pre"], a["f_W_post"]], axis=0)
    arrays = {
        "x": a["hidden_states"].reshape(2 * NT, P, DM),
        "w_in": w_in,
        "w_small": small.reshape(SMALL, KT, P).transpose(2, 1, 0),
        "conv_w": channels(_np.concatenate([a["conv_weight"], a["conv_bias"][:, None]], axis=1)),
        "norm_w": a["norm_weight"].reshape(GROUPS, XT, P).transpose(2, 0, 1),
        "D": a["D"],
        "dt_bias": a["dt_bias"],
        "A_log": a["A_log"],
        "base": _np.concatenate([a["f_H_res_base"].reshape(-1), a["f_H_pre_base"], a["f_H_post_base"]]),
        "w_branch": a["f_W_branch"].reshape(2, P, CW).transpose(1, 0, 2),
        "gate": a["f_gate"],
        "w_out": a["out_proj_w"].reshape(2, 512, OT, P).transpose(0, 2, 3, 1),
    }
    arrays = {n: _np.ascontiguousarray(v) for n, v in arrays.items()}
    nc = _bacc.Bacc("TRN2", target_bir_lowering=False, num_devices=1)
    args = {n: nc.dram_tensor(f"in_{n}", v.shape, mybir.dt.from_np(v.dtype), kind="ExternalInput").ap()
            for n, v in arrays.items()}
    args["out"] = nc.dram_tensor("out", (2 * NT, P, DM), F32, kind="ExternalOutput").ap()
    program(nc, **args)
    r = _run(nc, [{f"in_{n}": v for n, v in arrays.items()}], core_ids=[0])
    return r.results[0]["out"].reshape(4, SEQ, DM)
```
